# Optimizing a Trainium2 kernel written in Bass

```python
import numpy as np
import jax
import jax.numpy as jnp

def _softmax(x, axis=-1):
    return jax.nn.softmax(x, axis=axis)

def _gelu(x):
    return jax.nn.gelu(x, approximate=True)

def _silu(x):
    return jax.nn.silu(x)

def _sigmoid(x):
    return jax.nn.sigmoid(x)

def _layernorm(x, axis=-1, eps=1e-05):
    m = jnp.mean(x, axis=axis, keepdims=True)
    v = jnp.var(x, axis=axis, keepdims=True)
    return (x - m) / jnp.sqrt(v + eps)

def _scatter_add(tgt, idx, src, axis=0):
    return tgt.at[idx].add(src)

def _segment_sum(src, seg, n):
    return jax.ops.segment_sum(src, seg, n)
kernel_name = 'mk_prb_d2_jaxref_r8_735c23'

def setup_inputs(seed: int=0):
    np.random.seed(seed)
    _w = jnp.asarray

    def _L0_attn_setup():
        import jax, jax.numpy as jnp
        import numpy as np
        CHUNK = 32
        B, L, D, H = (4, 256, 128, 4)
        DK, DV = (D // H, D // H)
        GH = D * 2

        def l2norm(x):
            return x / jnp.linalg.norm(x, axis=-1, keepdims=True)

        def short_conv(x, w):
            kk = w.shape[-1]
            xt = jnp.transpose(x, (0, 2, 1))
            xt = jnp.pad(xt, ((0, 0), (0, 0), (kk - 1, 0)))
            y = jax.lax.conv_general_dilated(xt, w[:, None, :], (1,), 'VALID', dimension_numbers=('NCH', 'OIH', 'NCH'), feature_group_count=w.shape[0])
            return jax.nn.silu(jnp.transpose(y, (0, 2, 1)))

        def fir_conv(x, filt):
            b, l, h, d = x.shape
            kk = filt.shape[-1]
            xt = jnp.transpose(x, (0, 2, 3, 1)).reshape(b, h * d, l)
            xt = jnp.pad(xt, ((0, 0), (0, 0), (kk - 1, 0)))
            y = jax.lax.conv_general_dilated(xt, filt.reshape(h * d, 1, kk), (1,), 'VALID', dimension_numbers=('NCH', 'OIH', 'NCH'), feature_group_count=h * d)
            return jnp.transpose(y.reshape(b, h, d, l), (0, 3, 1, 2))

        def delta_rule_chunkwise(q, k, v, beta, chunk_size=CHUNK):
            b, h, Ltot, dk = q.shape
            dv = v.shape[-1]
            pad = -Ltot % chunk_size
            if pad:
                p4 = ((0, 0), (0, 0), (0, pad), (0, 0))
                q, k, v = (jnp.pad(q, p4), jnp.pad(k, p4), jnp.pad(v, p4))
                beta = jnp.pad(beta, ((0, 0), (0, 0), (0, pad)))
            Lp = Ltot + pad
            n = Lp // chunk_size
            q, k = (l2norm(q), l2norm(k))
            v = v * beta[..., None]
            k_beta = k * beta[..., None]
            resh = lambda t: t.reshape(b, h, n, chunk_size, t.shape[-1])
            q, k, v, k_beta = map(resh, (q, k, v, k_beta))
            tri_strict = jnp.tril(jnp.ones((chunk_size, chunk_size), bool), -1)
            attn = -(k_beta @ jnp.swapaxes(k, -1, -2)) * tri_strict

            def body(i, A):
                row = A[..., i, :]
                upd = jnp.einsum('bhnj,bhnjk->bhnk', row, A)
                new_row = jnp.where(jnp.arange(chunk_size) < i, row + upd, row)
                return A.at[..., i, :].set(new_row)
            attn = jax.lax.fori_loop(1, chunk_size, body, attn)
            attn = attn + jnp.eye(chunk_size, dtype=attn.dtype)
            u = attn @ v
            w = attn @ k_beta
            keep = jnp.tril(jnp.ones((chunk_size, chunk_size), bool))

            def step(S, xs):
                q_i, k_i, u_i, w_i = xs
                attn_local = q_i @ jnp.swapaxes(k_i, -1, -2) * keep
                u_new = u_i - w_i @ S
                o_i = q_i @ S + attn_local @ u_new
                S = S + jnp.swapaxes(k_i, -1, -2) @ u_new
                return (S, o_i)
            xs = tuple((jnp.moveaxis(t, 2, 0) for t in (q, k, u, w)))
            S0 = jnp.zeros((b, h, dk, dv), q.dtype)
            S, o = jax.lax.scan(step, S0, xs)
            o = jnp.moveaxis(o, 0, 2).reshape(b, h, Lp, dv)
            return (o[:, :, :Ltot], S)
        key = jax.random.key(seed)
        ks = jax.random.split(key, 16)
        s = 0.02
        return {'hidden_states': jax.random.normal(ks[0], (B, L, D), jnp.float32), 'q_proj_w': jax.random.normal(ks[1], (H * DK, D), jnp.float32) * s, 'k_proj_w': jax.random.normal(ks[2], (H * DK, D), jnp.float32) * s, 'v_proj_w': jax.random.normal(ks[3], (H * DV, D), jnp.float32) * s, 'b_proj_w': jax.random.normal(ks[4], (H, D), jnp.float32) * s, 'q_conv_w': jax.random.normal(ks[5], (H * DK, 4), jnp.float32) * s, 'k_conv_w': jax.random.normal(ks[6], (H * DK, 4), jnp.float32) * s, 'v_conv_w': jax.random.normal(ks[7], (H * DV, 4), jnp.float32) * s, 'fir_short_w': jax.random.normal(ks[8], (H, DV, 7), jnp.float32) * s, 'fir_long_w': jax.random.normal(ks[9], (H, DV, 31), jnp.float32) * s, 'alpha': jnp.full((H, 1), 0.2, jnp.float32), 'gmix_w1': jax.random.normal(ks[10], (GH, D), jnp.float32) * s, 'gmix_b1': jnp.zeros((GH,), jnp.float32), 'gmix_w2': jax.random.normal(ks[11], (H * 4, GH), jnp.float32) * s, 'gmix_b2': jnp.zeros((H * 4,), jnp.float32).at[H * 2:H * 3].set(0.03), 'o_norm_w': jnp.ones((DV,), jnp.float32), 'o_proj_w': jax.random.normal(ks[12], (D, H * DV), jnp.float32) * s}
    _L0_attn_in = _L0_attn_setup()

    def _L0_ffn_setup():
        import jax, jax.numpy as jnp
        import numpy as np
        TOP_K = 2
        CAP_FACTOR = 1.25
        MIN_CAPACITY = 4
        key = jax.random.key(seed)
        k1, k2, k3, k4 = jax.random.split(key, 4)
        B, T, C, E = (8, 256, 128, 8)
        x = jax.random.normal(k1, (B, T, C), dtype=jnp.float32)
        w_g = jax.random.normal(k2, (E, C), dtype=jnp.float32) * 0.02
        c_fc = jax.random.normal(k3, (E, C, 4 * C), dtype=jnp.float32) * 0.02
        c_proj = jax.random.normal(k4, (E, 4 * C, C), dtype=jnp.float32) * 0.02
        return {'x': x, 'w_g': w_g, 'c_fc': c_fc, 'c_proj': c_proj}
    _L0_ffn_in = _L0_ffn_setup()

    def _L1_attn_setup():
        import jax, jax.numpy as jnp
        import numpy as np
        D_MODEL = 128
        D_QK = 128
        NUM_HEADS = 16
        HEAD_DIM = D_QK // NUM_HEADS
        V_DIM = D_MODEL // NUM_HEADS
        B, S = (2, 256)
        key = jax.random.key(seed)
        ks = jax.random.split(key, 9)
        sc = 0.02
        return {'x': jax.random.normal(ks[0], (B, S, D_MODEL), dtype=jnp.float32), 'Wqk': jax.random.normal(ks[1], (D_MODEL, 2 * D_QK), dtype=jnp.float32) * sc, 'bqk': jax.random.normal(ks[2], (2 * D_QK,), dtype=jnp.float32) * sc, 'Wv': jax.random.normal(ks[3], (D_MODEL, D_MODEL), dtype=jnp.float32) * sc, 'bv': jax.random.normal(ks[4], (D_MODEL,), dtype=jnp.float32) * sc, 'Wn': jax.random.normal(ks[5], (D_MODEL, NUM_HEADS), dtype=jnp.float32) * sc, 'bn': jax.random.normal(ks[6], (NUM_HEADS,), dtype=jnp.float32) * sc, 'Wo': jax.random.normal(ks[7], (D_MODEL, D_MODEL), dtype=jnp.float32) * sc, 'bo': jax.random.normal(ks[8], (D_MODEL,), dtype=jnp.float32) * sc}
    _L1_attn_in = _L1_attn_setup()

    def _L1_ffn_setup():
        import jax, jax.numpy as jnp
        import numpy as np
        B, S, H, E, DFF = (4, 512, 128, 8, 512)
        key = jax.random.key(seed)
        k0, k1, k2, k3 = jax.random.split(key, 4)
        hidden_states = jax.random.normal(k0, (B, S, H), dtype=jnp.float32)
        gate_w = jax.random.normal(k1, (E, H), dtype=jnp.float32) * 0.02
        w1 = jax.random.normal(k2, (E, H, DFF), dtype=jnp.float32) * 0.02
        b1 = jnp.zeros((E, DFF), dtype=jnp.float32)
        w2 = jax.random.normal(k3, (E, DFF, H), dtype=jnp.float32) * 0.02
        b2 = jnp.zeros((E, H), dtype=jnp.float32)
        return {'hidden_states': hidden_states, 'gate_w': gate_w, 'w1': w1, 'b1': b1, 'w2': w2, 'b2': b2}
    _L1_ffn_in = _L1_ffn_setup()
    _d = {'L0_attn_hidden_states': _L0_attn_in['hidden_states'], 'L0_attn_q_proj_w': _L0_attn_in['q_proj_w'], 'L0_attn_k_proj_w': _L0_attn_in['k_proj_w'], 'L0_attn_v_proj_w': _L0_attn_in['v_proj_w'], 'L0_attn_b_proj_w': _L0_attn_in['b_proj_w'], 'L0_attn_q_conv_w': _L0_attn_in['q_conv_w'], 'L0_attn_k_conv_w': _L0_attn_in['k_conv_w'], 'L0_attn_v_conv_w': _L0_attn_in['v_conv_w'], 'L0_attn_fir_short_w': _L0_attn_in['fir_short_w'], 'L0_attn_fir_long_w': _L0_attn_in['fir_long_w'], 'L0_attn_alpha': _L0_attn_in['alpha'], 'L0_attn_gmix_w1': _L0_attn_in['gmix_w1'], 'L0_attn_gmix_b1': _L0_attn_in['gmix_b1'], 'L0_attn_gmix_w2': _L0_attn_in['gmix_w2'], 'L0_attn_gmix_b2': _L0_attn_in['gmix_b2'], 'L0_attn_o_norm_w': _L0_attn_in['o_norm_w'], 'L0_attn_o_proj_w': _L0_attn_in['o_proj_w'], 'L0_ffn_w_g': _L0_ffn_in['w_g'], 'L0_ffn_c_fc': _L0_ffn_in['c_fc'], 'L0_ffn_c_proj': _L0_ffn_in['c_proj'], 'L1_attn_Wqk': _L1_attn_in['Wqk'], 'L1_attn_bqk': _L1_attn_in['bqk'], 'L1_attn_Wv': _L1_attn_in['Wv'], 'L1_attn_bv': _L1_attn_in['bv'], 'L1_attn_Wn': _L1_attn_in['Wn'], 'L1_attn_bn': _L1_attn_in['bn'], 'L1_attn_Wo': _L1_attn_in['Wo'], 'L1_attn_bo': _L1_attn_in['bo'], 'L1_ffn_gate_w': _L1_ffn_in['gate_w'], 'L1_ffn_w1': _L1_ffn_in['w1'], 'L1_ffn_b1': _L1_ffn_in['b1'], 'L1_ffn_w2': _L1_ffn_in['w2'], 'L1_ffn_b2': _L1_ffn_in['b2']}
    _x0 = _d['L0_attn_hidden_states']
    _d['L0_attn_hidden_states'] = jax.random.normal(jax.random.fold_in(jax.random.key(seed), 1), (16, 512, 128), dtype=_x0.dtype)
    del _x0
    return _d

def reference(L0_attn_hidden_states, L0_attn_q_proj_w, L0_attn_k_proj_w, L0_attn_v_proj_w, L0_attn_b_proj_w, L0_attn_q_conv_w, L0_attn_k_conv_w, L0_attn_v_conv_w, L0_attn_fir_short_w, L0_attn_fir_long_w, L0_attn_alpha, L0_attn_gmix_w1, L0_attn_gmix_b1, L0_attn_gmix_w2, L0_attn_gmix_b2, L0_attn_o_norm_w, L0_attn_o_proj_w, L0_ffn_w_g, L0_ffn_c_fc, L0_ffn_c_proj, L1_attn_Wqk, L1_attn_bqk, L1_attn_Wv, L1_attn_bv, L1_attn_Wn, L1_attn_bn, L1_attn_Wo, L1_attn_bo, L1_ffn_gate_w, L1_ffn_w1, L1_ffn_b1, L1_ffn_w2, L1_ffn_b2):

    def _L0_attn_ref(hidden_states, q_proj_w, k_proj_w, v_proj_w, b_proj_w, q_conv_w, k_conv_w, v_conv_w, fir_short_w, fir_long_w, alpha, gmix_w1, gmix_b1, gmix_w2, gmix_b2, o_norm_w, o_proj_w):
        import jax, jax.numpy as jnp
        import numpy as np
        CHUNK = 32
        B, L, D, H = (4, 256, 128, 4)
        DK, DV = (D // H, D // H)
        GH = D * 2

        def l2norm(x):
            return x / jnp.linalg.norm(x, axis=-1, keepdims=True)

        def short_conv(x, w):
            kk = w.shape[-1]
            xt = jnp.transpose(x, (0, 2, 1))
            xt = jnp.pad(xt, ((0, 0), (0, 0), (kk - 1, 0)))
            y = jax.lax.conv_general_dilated(xt, w[:, None, :], (1,), 'VALID', dimension_numbers=('NCH', 'OIH', 'NCH'), feature_group_count=w.shape[0])
            return jax.nn.silu(jnp.transpose(y, (0, 2, 1)))

        def fir_conv(x, filt):
            b, l, h, d = x.shape
            kk = filt.shape[-1]
            xt = jnp.transpose(x, (0, 2, 3, 1)).reshape(b, h * d, l)
            xt = jnp.pad(xt, ((0, 0), (0, 0), (kk - 1, 0)))
            y = jax.lax.conv_general_dilated(xt, filt.reshape(h * d, 1, kk), (1,), 'VALID', dimension_numbers=('NCH', 'OIH', 'NCH'), feature_group_count=h * d)
            return jnp.transpose(y.reshape(b, h, d, l), (0, 3, 1, 2))

        def delta_rule_chunkwise(q, k, v, beta, chunk_size=CHUNK):
            b, h, Ltot, dk = q.shape
            dv = v.shape[-1]
            pad = -Ltot % chunk_size
            if pad:
                p4 = ((0, 0), (0, 0), (0, pad), (0, 0))
                q, k, v = (jnp.pad(q, p4), jnp.pad(k, p4), jnp.pad(v, p4))
                beta = jnp.pad(beta, ((0, 0), (0, 0), (0, pad)))
            Lp = Ltot + pad
            n = Lp // chunk_size
            q, k = (l2norm(q), l2norm(k))
            v = v * beta[..., None]
            k_beta = k * beta[..., None]
            resh = lambda t: t.reshape(b, h, n, chunk_size, t.shape[-1])
            q, k, v, k_beta = map(resh, (q, k, v, k_beta))
            tri_strict = jnp.tril(jnp.ones((chunk_size, chunk_size), bool), -1)
            attn = -(k_beta @ jnp.swapaxes(k, -1, -2)) * tri_strict

            def body(i, A):
                row = A[..., i, :]
                upd = jnp.einsum('bhnj,bhnjk->bhnk', row, A)
                new_row = jnp.where(jnp.arange(chunk_size) < i, row + upd, row)
                return A.at[..., i, :].set(new_row)
            attn = jax.lax.fori_loop(1, chunk_size, body, attn)
            attn = attn + jnp.eye(chunk_size, dtype=attn.dtype)
            u = attn @ v
            w = attn @ k_beta
            keep = jnp.tril(jnp.ones((chunk_size, chunk_size), bool))

            def step(S, xs):
                q_i, k_i, u_i, w_i = xs
                attn_local = q_i @ jnp.swapaxes(k_i, -1, -2) * keep
                u_new = u_i - w_i @ S
                o_i = q_i @ S + attn_local @ u_new
                S = S + jnp.swapaxes(k_i, -1, -2) @ u_new
                return (S, o_i)
            xs = tuple((jnp.moveaxis(t, 2, 0) for t in (q, k, u, w)))
            S0 = jnp.zeros((b, h, dk, dv), q.dtype)
            S, o = jax.lax.scan(step, S0, xs)
            o = jnp.moveaxis(o, 0, 2).reshape(b, h, Lp, dv)
            return (o[:, :, :Ltot], S)
        b, l, d = hidden_states.shape
        h = b_proj_w.shape[0]
        dk = q_proj_w.shape[0] // h
        dv = v_proj_w.shape[0] // h
        q = short_conv(hidden_states @ q_proj_w.T, q_conv_w).reshape(b, l, h, dk)
        k = short_conv(hidden_states @ k_proj_w.T, k_conv_w).reshape(b, l, h, dk)
        v = short_conv(hidden_states @ v_proj_w.T, v_conv_w).reshape(b, l, h, dv)
        beta = jax.nn.sigmoid(hidden_states @ b_proj_w.T)
        delta_out, _S = delta_rule_chunkwise(jnp.transpose(q, (0, 2, 1, 3)), jnp.transpose(k, (0, 2, 1, 3)), jnp.transpose(v, (0, 2, 1, 3)), jnp.transpose(beta, (0, 2, 1)))
        delta_out = jnp.transpose(delta_out, (0, 2, 1, 3))
        fir_s = fir_conv(v, fir_short_w)
        fir_l = fir_conv(v, fir_long_w)
        branches = jnp.stack([fir_s, fir_l, delta_out, v], axis=-2)
        mu = branches.mean(-1)
        std = jnp.std(branches, axis=-1, ddof=1)
        mx = branches.max(-1)
        stat_scalar = jnp.stack([mu, std, mx], -1).mean(-1)
        gate = jax.nn.gelu(hidden_states @ gmix_w1.T + gmix_b1, approximate=False) @ gmix_w2.T + gmix_b2
        gate = jnp.transpose(gate.reshape(b, l, 4, h), (0, 1, 3, 2))
        logits = gate + alpha[None, None, :, :] * stat_scalar
        wts = jax.nn.softmax(logits, axis=-1)
        o = jnp.einsum('blhc,blhcd->blhd', wts, branches)
        o = o * jax.lax.rsqrt(jnp.mean(o * o, axis=-1, keepdims=True) + 1e-05) * o_norm_w
        return o.reshape(b, l, h * dv) @ o_proj_w.T

    def _L0_ffn_ref(x, w_g, c_fc, c_proj):
        import jax, jax.numpy as jnp
        import numpy as np
        TOP_K = 2
        CAP_FACTOR = 1.25
        MIN_CAPACITY = 4
        B, T, C = x.shape
        E = w_g.shape[0]
        N = B * T
        capacity = max(MIN_CAPACITY, int(CAP_FACTOR * N * TOP_K / E))
        xf = x.reshape(N, C)
        logits = xf @ w_g.T
        top_logits, top_idx = jax.lax.top_k(logits, TOP_K)
        router_probs = jax.nn.softmax(top_logits, axis=-1)
        oh = jax.nn.one_hot(top_idx, E, dtype=jnp.int32)
        oh_t = oh.transpose(1, 0, 2).reshape(TOP_K * N, E)
        pos = jnp.cumsum(oh_t, axis=0).reshape(TOP_K, N, E).transpose(1, 0, 2)
        rank = jnp.sum((pos - 1) * oh, axis=-1)
        valid = rank < capacity
        probs_masked = router_probs * valid.astype(router_probs.dtype)
        rank_c = jnp.clip(rank, 0, capacity - 1)
        contrib = xf[:, None, :] * valid[..., None].astype(xf.dtype)
        buf = jnp.zeros((E, capacity, C), dtype=xf.dtype).at[top_idx, rank_c].add(contrib)
        h = jnp.einsum('ecd,edf->ecf', buf, c_fc)
        h = jnp.square(jax.nn.relu(h))
        expert_out = jnp.einsum('ecf,efd->ecd', h, c_proj)
        gathered = expert_out[top_idx, rank_c]
        out = jnp.sum(gathered * probs_masked[..., None], axis=1)
        return out.reshape(B, T, C)

    def _L1_attn_ref(x, Wqk, bqk, Wv, bv, Wn, bn, Wo, bo):
        import jax, jax.numpy as jnp
        import numpy as np
        D_MODEL = 128
        D_QK = 128
        NUM_HEADS = 16
        HEAD_DIM = D_QK // NUM_HEADS
        V_DIM = D_MODEL // NUM_HEADS
        B, S = (2, 256)
        b, s, _ = x.shape
        qk = x @ Wqk + bqk
        v = x @ Wv + bv
        n = x @ Wn + bn
        qk = qk.reshape(b, s, 2, NUM_HEADS, HEAD_DIM)
        q, k = (qk[:, :, 0], qk[:, :, 1])
        v = v.reshape(b, s, NUM_HEADS, V_DIM)
        scores = jnp.einsum('bthd,bshd->bhts', q, k)
        mask = jnp.tril(jnp.ones((s, s), dtype=scores.dtype))
        n_exp = jnp.exp(jnp.transpose(n, (0, 2, 1)))
        attn = scores * mask / n_exp[:, :, :, None]
        ctx = jnp.einsum('bhts,bshd->bthd', attn, v)
        ctx = ctx.reshape(b, s, D_MODEL)
        return ctx @ Wo + bo

    def _L1_ffn_ref(hidden_states, gate_w, w1, b1, w2, b2):
        import jax, jax.numpy as jnp
        import numpy as np
        B, S, H, E, DFF = (4, 512, 128, 8, 512)
        b, s, h = hidden_states.shape
        x = hidden_states.reshape(-1, h)
        gate_logits = x @ gate_w.T
        gate_probs = jax.nn.softmax(gate_logits, axis=-1)
        expert_idx = jnp.argmax(gate_probs, axis=-1)
        expert_w = jnp.take_along_axis(gate_probs, expert_idx[:, None], axis=1)[:, 0]
        out = jnp.zeros_like(x)
        n_experts = w1.shape[0]
        for e in range(n_experts):
            ye = jax.nn.relu(x @ w1[e] + b1[e]) @ w2[e] + b2[e]
            sel = (expert_idx == e)[:, None]
            out = out + jnp.where(sel, ye * expert_w[:, None], 0.0)
        return out.reshape(b, s, h)
    x = L0_attn_hidden_states
    xn = _layernorm(x, axis=-1)
    x = x + _L0_attn_ref(xn, L0_attn_q_proj_w, L0_attn_k_proj_w, L0_attn_v_proj_w, L0_attn_b_proj_w, L0_attn_q_conv_w, L0_attn_k_conv_w, L0_attn_v_conv_w, L0_attn_fir_short_w, L0_attn_fir_long_w, L0_attn_alpha, L0_attn_gmix_w1, L0_attn_gmix_b1, L0_attn_gmix_w2, L0_attn_gmix_b2, L0_attn_o_norm_w, L0_attn_o_proj_w) + _L0_ffn_ref(xn, L0_ffn_w_g, L0_ffn_c_fc, L0_ffn_c_proj)
    xn = _layernorm(x, axis=-1)
    x = x + _L1_attn_ref(xn, L1_attn_Wqk, L1_attn_bqk, L1_attn_Wv, L1_attn_bv, L1_attn_Wn, L1_attn_bn, L1_attn_Wo, L1_attn_bo) + _L1_ffn_ref(xn, L1_ffn_gate_w, L1_ffn_w1, L1_ffn_b1, L1_ffn_w2, L1_ffn_b2)
    return x

_drawn_inputs = setup_inputs


def setup_inputs(seed=0):
    import zlib

    import numpy as np

    out = dict(_drawn_inputs(seed))
    spreads = {'L0_attn_alpha': (0.20000000298023224, 0.6),
     'L0_attn_gmix_b1': (0.0, 0.8),
     'L0_attn_o_norm_w': (1.0, 0.6),
     'L1_ffn_b1': (0.0, 0.8),
     'L1_ffn_b2': (0.0, 0.464)}
    factors = {'L0_attn_b_proj_w': 8.0,
     'L0_attn_fir_short_w': 8.0,
     'L0_attn_fir_long_w': 6.225,
     'L0_attn_gmix_w1': 8.0,
     'L0_attn_gmix_w2': 8.0,
     'L0_attn_gmix_b2': 8.0,
     'L0_ffn_w_g': 3.142,
     'L0_ffn_c_fc': 2.999,
     'L0_ffn_c_proj': 2.765,
     'L1_attn_bn': 8.0,
     'L1_attn_bo': 2.796,
     'L1_ffn_gate_w': 2.754,
     'L1_ffn_w1': 5.487,
     'L1_ffn_w2': 4.294}
    for name, (base, spread) in spreads.items():
        noise = np.random.default_rng([zlib.crc32(name.encode()), seed]).standard_normal(out[name].shape)
        drawn = base * np.exp(spread * noise) if base else spread * noise
        out[name] = jnp.asarray(drawn.astype(out[name].dtype))
    for name, factor in factors.items():
        out[name] = (out[name] * factor).astype(out[name].dtype)
    return out
```

```python
from contextlib import ExitStack

import concourse.bass as bass
from concourse import mybir

ALU = mybir.AluOpType
ACT = mybir.ActivationFunctionType
F32 = mybir.dt.float32
I32 = mybir.dt.int32
U32 = mybir.dt.uint32
AX_X = mybir.AxisListType.X

P = 128
SEQS, LEN, D = 16, 512, 128
TILES = LEN // P
NT = SEQS * TILES
NTOK = SEQS * LEN
PAIRS = SEQS // 2
C = 32
NCH = LEN // C
H = 4
QD = 4
HEADS1 = 16
SUB = 4
E = 8
FF = 512
FT = FF // P
GS = 512
CAP0 = 2560
G0 = E * CAP0 // GS
G1 = NTOK // GS + E
TAPS = 4
KS, KL = 7, 31
EPS = 1e-5
START = 1


class Chain:

    def __init__(self, eng, sem):
        self.eng, self.sem, self.count = eng, sem, 0

    def step(self, ins):
        self.count += 1
        ins.then_inc(self.sem, 1)
        return self.count

    def wait(self, count=None):
        self.eng.wait_ge(self.sem, self.count if count is None else count)

    def link(self, ins):
        self.step(ins)
        self.wait()

    def restart(self):
        self.wait()
        self.eng.sem_clear(self.sem)
        self.count = 0


class Signals:

    def __init__(self, nc, ctx):
        self.nc, self.ctx, self.all, self.chains = nc, ctx, [], []

    def one(self, name):
        self.all.append(self.ctx.enter_context(self.nc.semaphore(name)))
        return self.all[-1]

    def own(self, name):
        self.chains.append(self.one(name))
        return self.chains[-1]

    def two(self, name):
        return [self.one(f"{name}_{b}") for b in range(2)]

    def clear(self):
        nums = sorted(s.num for s in self.all)
        starts = [n for n in nums if n - 1 not in nums]
        with self.nc.Block() as block:
            @block.sync
            def _(sp):
                for start in starts:
                    stop = start
                    while stop in nums:
                        stop += 1
                    sp.sem_clear(range(start, stop))

    def block(self):
        rest = [s for s in self.all if s not in self.chains]
        with self.nc.Block() as block:
            @block.sync
            def _(sp):
                for s in rest[0::2]:
                    sp.sem_inc(s, START)

            @block.tensor
            def _(pe):
                for s in rest[1::2]:
                    pe.sem_inc(s, START)

        self.ctx.callback(self.clear)
        return self.ctx.enter_context(self.nc.Block())


def quad(q):
    return slice(C * q, C * q + C)


def phase_project(nc, dram, keep):
    with ExitStack() as ctx:
        def sb(name, shape, dt=F32):
            return ctx.enter_context(nc.sbuf_tensor(name, shape, dt))

        def ps(name, shape, dt=F32):
            return ctx.enter_context(nc.psum_tensor(name, shape, dt))

        signals = Signals(nc, ctx)
        sem, sem2 = signals.one, signals.two

        ident, logits0 = keep["ident"], keep["logits"]
        w_qkv = sb("w_qkv", [P, 3, D])
        w_mix1 = sb("w_mix1", [P, 2, P])
        w_gate = sb("w_gate", [P, 2, P])
        w_beta = sb("w_beta", [P, P])
        w_rout = sb("w_rout", [P, E])
        taps = sb("taps", [P, 3, TAPS])
        b_mix1 = sb("b_mix1", [P, 2])
        b_gate = sb("b_gate", [P, 1])
        power = sb("power", [P, TILES])
        zeros = sb("zeros", [P, 2048])
        xt = [sb(f"xt{b}", [P, TILES, D]) for b in range(2)]
        stats = [sb(f"stats{b}", [P, TILES, 6]) for b in range(2)]
        moments = [sb(f"moments{b}", [P, TILES, 2]) for b in range(2)]
        var = [sb(f"var{b}", [P, TILES]) for b in range(2)]
        rstd = [sb(f"rstd{b}", [P, TILES]) for b in range(2)]
        xn = [sb(f"xn{b}", [P, TILES, D]) for b in range(2)]
        xnT = [sb(f"xnT{b}", [P, LEN]) for b in range(2)]
        conv = [sb(f"conv{b}", [P, 3, LEN]) for b in range(2)]
        chan = [sb(f"chan{b}", [P, 4, LEN]) for b in range(2)]
        hid = [sb(f"hid{b}", [P, 2, LEN]) for b in range(2)]
        head = [sb(f"head{b}", [P, 4, LEN]) for b in range(2)]

        psT = ps("psT", [P, LEN])
        psR = ps("psR", [P, TILES, E])
        psQKV = ps("psQKV", [P, 3, LEN])
        psH = ps("psH", [P, 2, LEN])
        psG = ps("psG", [P, LEN])

        weights_in = sem("weights_in")
        zeroed = sem("zeroed")
        slots_zeroed = keep["slots_zeroed"]
        power_set = sem("power_set")
        x_in = sem2("x_in")
        ln_stats = sem2("ln_stats")
        rstd_ready = sem2("rstd_ready")
        xn_ready = sem2("xn_ready")
        xn_stored = sem2("xn_stored")
        xnT_made = sem2("xnT_made")
        xnT_ready = sem2("xnT_ready")
        logits_made = sem2("logits_made")
        logits_kept = sem2("logits_kept")
        proj_made = sem2("proj_made")
        mix1_made = sem2("mix1_made")
        tap0_ready = sem2("tap0_ready")
        conv_ready = sem2("conv_ready")
        act_ready = sem2("act_ready")
        hid_ready = sem2("hid_ready")
        gate_made = sem2("gate_made")
        gate_ready = sem2("gate_ready")
        head_ready = sem2("head_ready")
        head_stored = sem2("head_stored")
        dve_own = signals.own("dve_own")
        pool_own = signals.own("pool_own")

        W_IN = 9 * 16
        pool_passed = signals.one("pool_passed")
        block = signals.block()

        @block.sync
        def _(sp):
            for dst, src in ((w_qkv, "w_qkv"), (w_mix1, "w_mix1"), (w_gate, "w_gate"), (w_beta, "w_beta"),
                             (w_rout, "w_rout0"), (taps, "taps"), (b_mix1, "b_mix1"), (b_gate, "b_gate"),
                             (ident, "ident")):
                sp.dma_start(dst[:], dram[src]).then_inc(weights_in, 16)

            def load(b, n):
                sp.dma_start(xt[b][:], dram["x"][bass.ds(n, 1)].rearrange("a (t p) d -> p (a t) d", p=P)
                             ).then_inc(x_in[b], 16)

            def store_xn(b, i):
                sp.wait_ge(xn_ready[b], START + i + 1)
                sp.dma_start(dram["xn"][bass.ds(2 * i + b, 1)].rearrange("a (t p) d -> p (a t) d", p=P),
                             xn[b][:]).then_inc(xn_stored[b], 16)

            def store_head(b, i):
                sp.wait_ge(head_ready[b], START + i + 1)
                sp.dma_start(dram["head"][bass.ds(2 * i + b, 1)].rearrange("a p k t -> p (a k) t"),
                             head[b][:]).then_inc(head_stored[b], 16)

            for b in range(2):
                load(b, b)
            with sp.Fori(0, PAIRS - 1) as i:
                for b in range(2):
                    store_xn(b, i)
                    load(b, 2 * i + 2 + b)
                for b in range(2):
                    store_head(b, i)
            for b in range(2):
                store_xn(b, PAIRS - 1)
            for b in range(2):
                store_head(b, PAIRS - 1)
            for b in range(2):
                sp.wait_ge(xn_stored[b], START + 16 * PAIRS)
                sp.wait_ge(head_stored[b], START + 16 * PAIRS)

        @block.gpsimd
        def _(pool):
            def wait(signal, value):
                pool.wait_ge(signal, value)
                pool.sem_inc(pool_passed, 1)

            own = Chain(pool, pool_own)
            nc.gpsimd.memset(power[:], -0.5).then_inc(power_set, 1)
            nc.gpsimd.memset(zeros[:], 0.0).then_inc(zeroed, 1)
            pool.wait_ge(power_set, START + 1)
            pool.wait_ge(zeroed, START + 1)
            for name, rows in (("slots0", G0 * GS), ("slots1", G1 * GS)):
                step = 2048 // D * P
                flat = dram[name].rearrange("(g p r) d -> g p (r d)", p=P, r=2048 // D)
                for g in range(rows // step):
                    pool.dma_start(flat[g], zeros[:]).then_inc(slots_zeroed, 16)
            with pool.Fori(0, PAIRS) as i:
                for b in range(2):
                    wait(ln_stats[b], START + i + 1)
                    own.link(nc.gpsimd.tensor_scalar(var[b][:], moments[b][:, :, 1], EPS, None, ALU.add))
                    nc.gpsimd.tensor_tensor(rstd[b][:], var[b][:], power[:], ALU.pow).then_inc(rstd_ready[b], 1)
                own.restart()
            pool.wait_ge(slots_zeroed, 16 * ((G0 + G1) * GS // (2048 // D * P)))

        @block.vector
        def _(dve):
            own = Chain(dve, dve_own)
            with dve.Fori(0, PAIRS) as i:
                for b in range(2):
                    dve.wait_ge(x_in[b], START + 16 * (i + 1))
                    for t in range(TILES):
                        own.step(nc.vector.bn_stats(stats[b][:, t, :], xt[b][:, t, :]))
                    own.wait()
                    for t in range(TILES):
                        ins = nc.vector.bn_aggr(moments[b][:, t, :], stats[b][:, t, :])
                    ins.then_inc(ln_stats[b], 1)
                for b in range(2):
                    dve.wait_ge(rstd_ready[b], START + i + 1)
                    dve.wait_ge(xn_stored[b], START + 16 * i)
                    dve.wait_ge(xnT_made[b], START + i)
                    for t in range(TILES):
                        ins = nc.vector.tensor_scalar(xn[b][:, t, :], xt[b][:, t, :], moments[b][:, t, 0:1],
                                                      rstd[b][:, t:t + 1], ALU.subtract, ALU.mult)
                    ins.then_inc(xn_ready[b], 1)
                for b in range(2):
                    dve.wait_ge(logits_made[b], START + i + 1)
                    nc.vector.tensor_copy(logits0[:, bass.ds((2 * i + b) * TILES * E, TILES * E)],
                                          psR[:].rearrange("p t e -> p (t e)")).then_inc(logits_kept[b], 1)
                    dve.wait_ge(tap0_ready[b], START + i + 1)
                    if b == 0:
                        dve.wait_ge(weights_in, START + W_IN)
                    last = [None] * 3
                    for lag in range(1, TAPS):
                        for j in range(3):
                            if last[j]:
                                own.wait(last[j])
                            last[j] = own.step(nc.vector.scalar_tensor_tensor(
                                out=conv[b][:, j, lag:LEN], in0=psQKV[:, j, 0:LEN - lag],
                                scalar=taps[:, j, TAPS - 1 - lag:TAPS - lag], in1=conv[b][:, j, lag:LEN],
                                op0=ALU.mult, op1=ALU.add))
                    own.wait()
                    dve.sem_inc(conv_ready[b], 1)
                for b in range(2):
                    dve.wait_ge(head_stored[b], START + 16 * i)
                    dve.wait_ge(act_ready[b], START + i + 1)
                    for j in range(3):
                        nc.vector.transpose(head[b][:, j, :], chan[b][:, j, :])
                    dve.wait_ge(gate_ready[b], START + i + 1)
                    nc.vector.transpose(head[b][:, 3, :], chan[b][:, 3, :]).then_inc(head_ready[b], 1)
                own.restart()

        @block.scalar
        def _(act):
            with act.Fori(0, PAIRS) as i:
                for b in range(2):
                    act.wait_ge(xnT_made[b], START + i + 1)
                    act.wait_ge(gate_made[b], START + i)
                    nc.scalar.copy(xnT[b][:], psT[:]).then_inc(xnT_ready[b], 1)
                for b in range(2):
                    act.wait_ge(proj_made[b], START + i + 1)
                    act.wait_ge(act_ready[b], START + i)
                    if b == 0:
                        act.wait_ge(weights_in, START + W_IN)
                    for j in range(3):
                        ins = nc.scalar.activation(conv[b][:, j, :], psQKV[:, j, :], ACT.Copy,
                                                   scale=taps[:, j, TAPS - 1:TAPS])
                    ins.then_inc(tap0_ready[b], 1)
                    act.wait_ge(mix1_made[b], START + i + 1)
                    for k in range(2):
                        ins = nc.scalar.activation(hid[b][:, k, :], psH[:, k, :], ACT.Gelu, bias=b_mix1[:, k:k + 1])
                    ins.then_inc(hid_ready[b], 1)
                for b in range(2):
                    act.wait_ge(gate_made[b], START + i + 1)
                    act.wait_ge(head_ready[b], START + i)
                    nc.scalar.activation(chan[b][:, 3, :], psG[:], ACT.Identity, bias=b_gate[:, 0:1]
                                         ).then_inc(gate_ready[b], 1)
                for b in range(2):
                    act.wait_ge(conv_ready[b], START + i + 1)
                    nc.scalar.activation(chan[b][:, 0:3, :], conv[b][:], ACT.Silu).then_inc(act_ready[b], 1)

        @block.tensor
        def _(pe):
            pe.wait_ge(weights_in, START + W_IN)
            with pe.Fori(0, PAIRS) as i:
                for b in range(2):
                    o = 1 - b
                    before = i + b
                    pe.wait_ge(xn_ready[b], START + i + 1)
                    pe.wait_ge(xnT_ready[o], START + before)
                    for t in range(TILES):
                        ins = nc.tensor.transpose(psT[:, bass.ts(t, P)], xn[b][:, t, :], ident[:])
                    ins.then_inc(xnT_made[b], 1)
                for b in range(2):
                    o = 1 - b
                    before = i + b
                    pe.wait_ge(xnT_ready[b], START + i + 1)
                    pe.wait_ge(logits_kept[o], START + before)
                    for t in range(TILES):
                        ins = nc.tensor.matmul(psR[:, t, :], xnT[b][:, bass.ts(t, P)], w_rout[:], start=True, stop=True)
                    ins.then_inc(logits_made[b], 1)
                    pe.wait_ge(conv_ready[o], START + before)
                    for j in range(3):
                        ins = nc.tensor.matmul(psQKV[:, j, :], w_qkv[:, j, :], xnT[b][:], start=True, stop=True)
                    ins.then_inc(proj_made[b], 1)
                    pe.wait_ge(hid_ready[o], START + before)
                    for k in range(2):
                        ins = nc.tensor.matmul(psH[:, k, :], w_mix1[:, k, :], xnT[b][:], start=True, stop=True)
                    ins.then_inc(mix1_made[b], 1)
                for b in range(2):
                    o = 1 - b
                    before = i + b
                    pe.wait_ge(hid_ready[b], START + i + 1)
                    pe.wait_ge(gate_ready[o], START + before)
                    nc.tensor.matmul(psG[:], w_beta[:], xnT[b][:], start=True, stop=False)
                    nc.tensor.matmul(psG[:], w_gate[:, 0, :], hid[b][:, 0, :], start=False, stop=False)
                    nc.tensor.matmul(psG[:], w_gate[:, 1, :], hid[b][:, 1, :], start=False, stop=True
                                     ).then_inc(gate_made[b], 1)


def phase_fir(nc, dram, keep):
    with ExitStack() as ctx:
        def sb(name, shape, dt=F32):
            return ctx.enter_context(nc.sbuf_tensor(name, shape, dt))

        signals = Signals(nc, ctx)
        sem, sem2 = signals.one, signals.two

        v_all = sb("v_all", [P, SEQS, NCH, C])
        toep = sb("toep", [P, C, 2, 2 * C])
        diag = [sb(f"diag{b}", [P, 2, 2, P]) for b in range(2)]
        fir = sb("fir", [P, SEQS, 2, NCH, C])
        psF = [ctx.enter_context(nc.psum_tensor(f"psF{b}", [P, 2, 2, SEQS, NCH], F32)) for b in range(2)]

        inputs_in = sem("fir_inputs_in")
        diag_clear = sem("diag_clear")
        diag_dve = sem2("diag_dve")
        diag_pool = sem2("diag_pool")
        diag_act = sem2("diag_act")
        fir_made = sem2("fir_made")
        fir_kept = sem2("fir_kept")
        fir_act = sem2("fir_act")
        fir_stored = sem("fir_stored")
        pool_passed = signals.one("pool_passed")
        block = signals.block()

        @block.sync
        def _(sp):
            sp.dma_start(toep[:], dram["toep"]).then_inc(inputs_in, 16)
            for n in range(SEQS):
                sp.dma_start(v_all[:, n].rearrange("p c d -> p (c d)"), dram["head"][n, :, 2, :]).then_inc(inputs_in, 16)
            for b in range(2):
                sp.wait_ge(fir_kept[b], START + C // 2)
                sp.wait_ge(fir_act[b], START + C // 2)
            for n in range(SEQS):
                sp.dma_start(dram["fir"][n], fir[:, n].rearrange("p f c d -> p f (c d)")).then_inc(fir_stored, 16)
            sp.wait_ge(fir_stored, START + 16 * SEQS)

        IN = 16 * (1 + SEQS)

        def blocks_of(copy, qs, b, d):
            for q in qs:
                ins = copy(diag[b][quad(q), :, :, quad(q)],
                           toep[quad(q), bass.ds(d, 1)].rearrange("p a f (k m) -> p (a f) k m", m=C))
            return ins

        @block.gpsimd
        def _(pool):
            def wait(signal, value):
                pool.wait_ge(signal, value)
                pool.sem_inc(pool_passed, 1)

            for b in range(2):
                nc.gpsimd.memset(diag[b][:], 0.0).then_inc(diag_clear, 1)
            pool.wait_ge(diag_clear, START + 2)
            pool.wait_ge(inputs_in, START + IN)
            with pool.Fori(0, C // 2) as i:
                for b in range(2):
                    wait(fir_made[b], START + i)
                    blocks_of(nc.gpsimd.tensor_copy, (0,), b, 2 * i + b).then_inc(diag_pool[b], 1)

        @block.scalar
        def _(act):
            act.wait_ge(diag_clear, START + 2)
            act.wait_ge(inputs_in, START + IN)
            with act.Fori(0, C // 2) as i:
                for b in range(2):
                    act.wait_ge(fir_made[b], START + i)
                    blocks_of(nc.scalar.copy, (1,), b, 2 * i + b).then_inc(diag_act[b], 1)
                for b in range(2):
                    act.wait_ge(fir_made[b], START + i + 1)
                    nc.scalar.copy(fir[:, :, 1, :, bass.ds(2 * i + b, 1)].rearrange("p s c a -> p s (c a)"),
                                   psF[b][:, 1, 0]).then_inc(fir_act[b], 1)

        @block.vector
        def _(dve):
            dve.wait_ge(diag_clear, START + 2)
            dve.wait_ge(inputs_in, START + IN)
            with dve.Fori(0, C // 2) as i:
                for b in range(2):
                    dve.wait_ge(fir_made[b], START + i)
                    blocks_of(nc.vector.tensor_copy, (2, 3), b, 2 * i + b).then_inc(diag_dve[b], 1)
                for b in range(2):
                    dve.wait_ge(fir_made[b], START + i + 1)
                    nc.vector.tensor_copy(fir[:, :, 0, :, bass.ds(2 * i + b, 1)].rearrange("p s c a -> p s (c a)"),
                                          psF[b][:, 0, 0]).then_inc(fir_kept[b], 1)

        @block.tensor
        def _(pe):
            pe.wait_ge(inputs_in, START + IN)
            with pe.Fori(0, C // 2) as i:
                for b in range(2):
                    d = 2 * i + b
                    for ready in (diag_pool, diag_act, diag_dve):
                        pe.wait_ge(ready[b], START + i + 1)
                    pe.wait_ge(fir_kept[b], START + i)
                    pe.wait_ge(fir_act[b], START + i)
                    for f in range(2):
                        v_d = v_all[:, :, :, bass.ds(d, 1)].rearrange("p s c a -> p s (c a)")
                        v_before = v_all[:, :, 0:NCH - 1, bass.ds(d, 1)].rearrange("p s c a -> p s (c a)")
                        nc.tensor.matmul(psF[b][:, f, 0], diag[b][:, f, 0, :], v_d, start=True, stop=False)
                        ins = nc.tensor.matmul(psF[b][:, f, 0, :, 1:NCH], diag[b][:, f, 1, :], v_before,
                                               start=False, stop=True)
                    ins.then_inc(fir_made[b], 1)


def phase_delta(nc, dram, keep):
    with ExitStack() as ctx:
        def sb(name, shape, dt=F32):
            return ctx.enter_context(nc.sbuf_tensor(name, shape, dt))

        def sb2(name, shape, dt=F32):
            return [sb(f"{name}{b}", shape, dt) for b in range(2)]

        def ps2(name, shape):
            return [ctx.enter_context(nc.psum_tensor(f"{name}{b}", shape, F32)) for b in range(2)]

        signals = Signals(nc, ctx)
        sem, sem2 = signals.one, signals.two

        masks = sb("masks", [P, 4, C])
        w_o = sb("w_o", [P, D])
        w_os = sb("w_os", [P, D])
        o_norm = sb("o_norm", [P, 1])
        alpha = sb("alpha", [P, 1])
        alpha3 = sb("alpha3", [P, 1])
        expo = sb("expo", [P, 2, 4 * NCH])
        qk = sb2("qk", [P, 2, NCH, C])
        gates = sb2("gates", [P, NCH, C])
        branch = sb2("branch", [P, 4, NCH, C])
        squares = sb2("squares", [P, 4, NCH, C])
        norm2 = sb2("norm2", [P, 2 * NCH])
        rnorm = sb2("rnorm", [P, 2, NCH])
        ebeta = sb2("ebeta", [P, NCH])
        beta = sb2("beta", [P, NCH])
        qn = sb2("qn", [P, NCH, C])
        ka = sb2("ka", [P, NCH, 2, C])
        vk = sb2("vk", [P, NCH, 2, C])
        cm = sb2("cm", [P, NCH, 3, C])
        work = sb2("work", [P, 4, NCH, C])
        rows = [[work[b][:, 2 * k:2 * k + 2].rearrange("p a c d -> p (a c d)").rearrange(
            "p (c k d) -> p c k d", k=2, d=C) for b in range(2)] for k in range(2)]
        cen = work
        power = sb2("apower", [P, NCH, C])
        diag = [sb2(f"diag{k}", [P, NCH, P]) for k in range(4)]
        uw = sb2("uw", [P, NCH, 2, C])
        imq = sb2("imq", [P, NCH, 2, C])
        state = sb2("state", [P, NCH, C])
        sums = sb2("sums", [P, 4 * NCH])
        maxs = sb2("maxs", [P, 4 * NCH])
        dev2 = sb2("dev2", [P, 4 * NCH])
        std = sb2("std", [P, 4 * NCH])
        logit = sb2("logit", [P, 4, NCH])
        lmax = sb2("lmax", [P, NCH])
        prob = sb2("bprob", [P, 4, NCH])
        psum_ = sb2("probsum", [P, NCH])
        mix = sb2("mix", [P, NCH, C])
        mix2 = sb2("mix2", [P, NCH])
        mixr = sb2("mixr", [P, NCH])
        mixT = [qn[b][:].rearrange("p c d -> p (c d)") for b in range(2)]
        xres = sb2("xres", [P, TILES, D])
        x1 = xres

        psA = ps2("psA", [P, NCH, 2, C])
        psS = ps2("psS", [P, 2, LEN])

        const_in = sem("const_in")
        set_up = sem("set_up")
        clear = sem("clear")
        head_in = sem2("head_in")
        x_in = sem2("xres_in")
        squared = sem2("squared")
        norm2_ready = sem2("norm2_ready")
        rnorm_ready = sem2("rnorm_ready")
        ebeta_ready = sem2("ebeta_ready")
        source = sem2("source")
        diag_act = sem2("diag_act")
        diag_pool = sem2("diag_pool")
        diag_dve = sem2("diag_dve")
        made = sem2("made")
        kept = sem2("kept")
        state_made = sem2("state_made")
        state_ready = sem2("state_ready")
        cen_ready = sem2("cen_ready")
        cen_squared = sem2("cen_squared")
        dev2_ready = sem2("dev2_ready")
        std_ready = sem2("std_ready")
        logit_ready = sem2("logit_ready")
        exp_ready = sem2("exp_ready")
        mix_ready = sem2("mix_ready")
        mix_squared = sem2("mix_squared")
        mix2_ready = sem2("mix2_ready")
        mixr_ready = sem2("mixr_ready")
        mixT_ready = sem2("mixT_ready")
        out_made = sem2("out_made")
        x1_ready = sem2("x1_ready")
        x1_stored = sem2("x1_stored")
        dve_own = signals.own("dve_own")
        pool_own = signals.own("pool_own")
        pool_passed = signals.one("pool_passed")
        block = signals.block()

        KT, K, A, A2, A4, A8, A16, TT, ATT, W, IM, QE = range(12)
        DIAGS = 12
        BUF = {KT: 0, K: 3, A: 1, A2: 0, A4: 1, A8: 0, A16: 1, TT: 2, ATT: 0, W: 1, IM: 2, QE: 1}
        GRAM, SQ0, SQ1, SQ2, SQ3, SQ4, UW, MW, OUT = range(9)
        STEPS = 9

        def src(e, b):
            return {KT: cm[b][:, :, 0], K: ka[b][:, :, 0], TT: rows[1][b][:, :, 1], ATT: ka[b][:, :, 1],
                    W: uw[b][:, :, 1], IM: imq[b][:, :, 0], QE: imq[b][:, :, 1]}.get(e, power[b][:])

        def spread(wait, copy, qs, e, b, i, done):
            wait(source[b], START + DIAGS * i + e + 1)
            if e in (KT, K):
                wait(made[b], START + STEPS * i)
            for q in qs:
                ins = copy(diag[BUF[e]][b][quad(q), :, quad(q)], src(e, b)[quad(q)])
            ins.then_inc(done[b], 1)

        @block.sync
        def _(sp):
            for dst, name in ((masks, "masks"), (w_o, "w_o0"), (o_norm, "o_norm"), (alpha, "alpha")):
                sp.dma_start(dst[:], dram[name]).then_inc(const_in, 16)

            def load(b, n, i):
                sp.dma_start(qk[b][:].rearrange("p k c d -> p k (c d)"), dram["head"][bass.ds(n, 1), :, 0:2].rearrange(
                    "a p k t -> p (a k) t")).then_inc(head_in[b], 16)
                sp.dma_start(gates[b][:].rearrange("p c d -> p (c d)"), dram["head"][bass.ds(n, 1), :, 3:4].rearrange(
                    "a p k t -> p (a k t)")).then_inc(head_in[b], 16)
                sp.dma_start(branch[b][:, 3:4].rearrange("p k c d -> p k (c d)"), dram["head"][
                    bass.ds(n, 1), :, 2:3].rearrange("a p k t -> p (a k) t")).then_inc(head_in[b], 16)
                sp.dma_start(branch[b][:, 0:2].rearrange("p k c d -> p k (c d)"), dram["fir"][bass.ds(n, 1)].rearrange(
                    "a p k t -> p (a k) t")).then_inc(head_in[b], 16)

            with sp.Fori(0, PAIRS) as i:
                for b in range(2):
                    n = 2 * i + b
                    sp.wait_ge(mix_ready[b], START + i)
                    load(b, n, i)
                    sp.wait_ge(x1_stored[b], START + 16 * i)
                    sp.dma_start(xres[b][:], dram["x"][bass.ds(n, 1)].rearrange("a (t p) d -> p (a t) d", p=P)
                                 ).then_inc(x_in[b], 16)
                for b in range(2):
                    sp.wait_ge(x1_ready[b], START + i + 1)
                    sp.dma_start(dram["x1"][bass.ds(2 * i + b, 1)].rearrange("a (t p) d -> p (a t) d", p=P), x1[b][:]
                                 ).then_inc(x1_stored[b], 16)
            for b in range(2):
                sp.wait_ge(x1_stored[b], START + 16 * PAIRS)

        @block.gpsimd
        def _(pool):
            def wait(signal, value):
                pool.wait_ge(signal, value)
                pool.sem_inc(pool_passed, 1)

            own = Chain(pool, pool_own)
            for b in range(2):
                for k in range(4):
                    nc.gpsimd.memset(diag[k][b][:], 0.0).then_inc(clear, 1)
            nc.gpsimd.memset(expo[:, 0], -0.5).then_inc(clear, 1)
            nc.gpsimd.memset(expo[:, 1], 0.5).then_inc(clear, 1)
            pool.wait_ge(clear, START + 10)
            copy = nc.gpsimd.tensor_copy

            def expand(es, i):
                for e in es:
                    for b in range(2):
                        spread(wait, copy, (2,), e, b, i, diag_pool)

            with pool.Fori(0, PAIRS) as i:
                for b in range(2):
                    wait(norm2_ready[b], START + i + 1)
                    own.link(nc.gpsimd.tensor_tensor(rnorm[b][:].rearrange("p k c -> p (k c)"), norm2[b][:],
                                                     expo[:, 0, 0:2 * NCH], ALU.pow))
                    pool.sem_inc(rnorm_ready[b], 1)
                expand(range(DIAGS), i)
                for b in range(2):
                    wait(diag_pool[b], START + DIAGS * (i + 1))
                for b in range(2):
                    wait(dev2_ready[b], START + i + 1)
                    own.link(nc.gpsimd.tensor_scalar(std[b][:], dev2[b][:], 1.0 / (C - 1), None, ALU.mult))
                    own.link(nc.gpsimd.tensor_tensor(std[b][:], std[b][:], expo[:, 1], ALU.pow))
                    pool.sem_inc(std_ready[b], 1)
                for b in range(2):
                    wait(mix2_ready[b], START + i + 1)
                    own.link(nc.gpsimd.tensor_scalar(mixr[b][:], mix2[b][:], 1.0 / C, EPS, ALU.mult, ALU.add))
                    own.link(nc.gpsimd.tensor_tensor(mixr[b][:], mixr[b][:], expo[:, 0, 0:NCH], ALU.pow))
                    pool.sem_inc(mixr_ready[b], 1)
                own.restart()

        @block.scalar
        def _(act):
            act.wait_ge(clear, START + 10)

            def expand(es, i):
                for e in es:
                    for b in range(2):
                        spread(act.wait_ge, nc.scalar.copy, (0, 1), e, b, i, diag_act)

            with act.Fori(0, PAIRS) as i:
                for b in range(2):
                    act.wait_ge(head_in[b], START + 64 * (i + 1))
                    nc.scalar.activation(squares[b][:, 0:2], qk[b][:], ACT.Square).then_inc(squared[b], 1)
                    nc.scalar.activation(ebeta[b][:], gates[b][:, :, 4], ACT.Exp, scale=-1.0).then_inc(ebeta_ready[b], 1)
                expand(range(9), i)
                for b in range(2):
                    act.wait_ge(made[b], START + STEPS * i + UW + 1)
                    nc.scalar.copy(uw[b][:], psA[b][:]).then_inc(kept[b], 1)
                    act.wait_ge(kept[b], START + STEPS * i + UW + 1)
                    act.sem_inc(source[b], 1)
                expand((W, IM, QE), i)
                for u in range(NCH - 1):
                    for b in range(2):
                        act.wait_ge(state_made[b], START + (NCH - 1) * i + u + 1)
                        nc.scalar.copy(state[b][:, u + 1], psS[b][:, u % 2, 0:C]).then_inc(state_ready[b], 1)
                for b in range(2):
                    act.wait_ge(cen_ready[b], START + i + 1)
                    nc.scalar.activation(squares[b][:], cen[b][:], ACT.Square).then_inc(cen_squared[b], 1)
                for b in range(2):
                    act.wait_ge(logit_ready[b], START + i + 1)
                    nc.scalar.activation(prob[b][:], logit[b][:], ACT.Exp).then_inc(exp_ready[b], 1)
                for b in range(2):
                    act.wait_ge(mix_ready[b], START + i + 1)
                    nc.scalar.activation(squares[b][:, 0], mix[b][:], ACT.Square).then_inc(mix_squared[b], 1)

        @block.vector
        def _(dve):
            own = Chain(dve, dve_own)
            V = nc.vector

            def expand(es, i):
                for e in es:
                    for b in range(2):
                        spread(dve.wait_ge, V.tensor_copy, (3,), e, b, i, diag_dve)

            def mask(k):
                return masks[:, k:k + 1, :].to_broadcast([P, NCH, C])

            def over_channels(ap):
                return ap.unsqueeze(2).to_broadcast([P, NCH, C])

            dve.wait_ge(const_in, START + 64)
            dve.wait_ge(clear, START + 10)
            V.tensor_scalar(w_os[:], w_o[:], o_norm[:, 0:1], None, ALU.mult).then_inc(set_up, 1)
            V.tensor_scalar(alpha3[:], alpha[:], 1.0 / 3.0, None, ALU.mult).then_inc(set_up, 1)
            dve.wait_ge(set_up, START + 2)
            with dve.Fori(0, PAIRS) as i:
                for b in range(2):
                    dve.wait_ge(squared[b], START + i + 1)
                    V.tensor_reduce(norm2[b][:], squares[b][:, 0:2].rearrange("p k c d -> p (k c) d"), AX_X, ALU.add
                                    ).then_inc(norm2_ready[b], 1)
                    dve.wait_ge(ebeta_ready[b], START + i + 1)
                    own.link(V.tensor_scalar(ebeta[b][:], ebeta[b][:], 1.0, None, ALU.add))
                    own.link(V.reciprocal(beta[b][:], ebeta[b][:]))
                for b in range(2):
                    dve.wait_ge(rnorm_ready[b], START + i + 1)
                    own.step(V.tensor_tensor(ka[b][:, :, 0], qk[b][:, 1], over_channels(rnorm[b][:, 1]), ALU.mult))
                    own.step(V.tensor_tensor(vk[b][:, :, 0], branch[b][:, 3], over_channels(beta[b][:]), ALU.mult))
                    own.link(V.tensor_tensor(qn[b][:], qk[b][:, 0], over_channels(rnorm[b][:, 0]), ALU.mult))
                    own.link(V.tensor_tensor(vk[b][:, :, 1], ka[b][:, :, 0], over_channels(beta[b][:]), ALU.mult))
                    own.step(V.transpose(cm[b][:, :, 0], ka[b][:, :, 0]))
                    own.step(V.transpose(cm[b][:, :, 1], vk[b][:, :, 1]))
                    own.link(V.transpose(cm[b][:, :, 2], qn[b][:]))
                    dve.sem_inc(source[b], 2)
                expand((KT, K), i)
                for b in range(2):
                    dve.wait_ge(made[b], START + STEPS * i + GRAM + 1)
                    own.step(V.tensor_tensor(rows[0][b][:, :, 0], psA[b][:, :, 0], mask(0), ALU.mult))
                    own.link(V.tensor_tensor(ka[b][:, :, 1], psA[b][:, :, 1], mask(1), ALU.mult))
                    own.step(V.transpose(power[b][:], rows[0][b][:, :, 0]))
                    own.link(V.tensor_tensor(rows[1][b][:, :, 1], rows[0][b][:, :, 0], mask(2), ALU.add))
                    dve.sem_inc(source[b], 1)
                    dve.sem_inc(kept[b], 1)
                expand((A,), i)
                for lv in range(5):
                    old, new = rows[lv % 2], rows[1 - lv % 2]
                    for b in range(2):
                        dve.wait_ge(made[b], START + STEPS * i + SQ0 + lv + 1)
                        if lv < 4:
                            own.step(V.transpose(power[b][:], psA[b][:, :, 0]))
                        if lv < 3:
                            own.step(V.tensor_copy(new[b][:, :, 0], psA[b][:, :, 0]))
                        if lv > 0:
                            own.step(V.tensor_tensor(new[b][:, :, 1], old[b][:, :, 1], psA[b][:, :, 1], ALU.add))
                        own.wait()
                        dve.sem_inc(source[b], 2 if lv == 4 else 1)
                        dve.sem_inc(kept[b], 1)
                    expand((A2 + lv,) if lv < 4 else (TT, ATT), i)
                expand((W,), i)
                for b in range(2):
                    dve.wait_ge(made[b], START + STEPS * i + MW + 1)
                    own.step(V.tensor_tensor(imq[b][:, :, 0], mask(2), psA[b][:, :, 0], ALU.subtract))
                    own.link(V.tensor_tensor(imq[b][:, :, 1], cm[b][:, :, 2], psA[b][:, :, 1], ALU.subtract))
                    dve.sem_inc(source[b], 2)
                    dve.sem_inc(kept[b], 1)
                expand((IM, QE), i)
                for b in range(2):
                    dve.wait_ge(made[b], START + STEPS * i + OUT + 1)
                    own.link(V.tensor_copy(branch[b][:, 2], psA[b][:].rearrange("p c k d -> p (c k) d")[:, 0:NCH]))
                    dve.sem_inc(kept[b], 1)
                    flat = branch[b][:].rearrange("p k c d -> p (k c) d")
                    own.step(V.tensor_reduce(maxs[b][:], flat, AX_X, ALU.max))
                    own.link(V.tensor_reduce(sums[b][:], flat, AX_X, ALU.add))
                    V.scalar_tensor_tensor(out=cen[b][:].rearrange("p k c d -> p (k c) d"),
                                           in0=sums[b][:].unsqueeze(2).to_broadcast([P, 4 * NCH, C]),
                                           scalar=-1.0 / C, in1=flat, op0=ALU.mult, op1=ALU.add
                                           ).then_inc(cen_ready[b], 1)
                for b in range(2):
                    dve.wait_ge(cen_squared[b], START + i + 1)
                    V.tensor_reduce(dev2[b][:], squares[b][:].rearrange("p k c d -> p (k c) d"), AX_X, ALU.add
                                    ).then_inc(dev2_ready[b], 1)
                    own.link(V.scalar_tensor_tensor(out=maxs[b][:], in0=sums[b][:], scalar=1.0 / C, in1=maxs[b][:],
                                                    op0=ALU.mult, op1=ALU.add))
                for b in range(2):
                    dve.wait_ge(std_ready[b], START + i + 1)
                    own.link(V.tensor_tensor(maxs[b][:], maxs[b][:], std[b][:], ALU.add))
                    own.link(V.scalar_tensor_tensor(
                        out=logit[b][:], in0=maxs[b][:].rearrange("p (k c) -> p k c", k=4), scalar=alpha3[:, 0:1],
                        in1=gates[b][:, :, 0:4].rearrange("p c k -> p k c"), op0=ALU.mult, op1=ALU.add))
                    own.link(V.tensor_reduce(lmax[b][:], logit[b][:].rearrange("p k c -> p c k"), AX_X, ALU.max))
                    V.tensor_tensor(logit[b][:], logit[b][:], lmax[b][:].unsqueeze(1).to_broadcast([P, 4, NCH]),
                                    ALU.subtract).then_inc(logit_ready[b], 1)
                for b in range(2):
                    dve.wait_ge(exp_ready[b], START + i + 1)
                    own.link(V.tensor_reduce(psum_[b][:], prob[b][:].rearrange("p k c -> p c k"), AX_X, ALU.add))
                    own.link(V.reciprocal(lmax[b][:], psum_[b][:]))
                    own.link(V.tensor_tensor(prob[b][:], prob[b][:], lmax[b][:].unsqueeze(1).to_broadcast([P, 4, NCH]),
                                             ALU.mult))
                    own.link(V.tensor_tensor(cen[b][:].rearrange("p k c d -> p (k c) d"),
                                             branch[b][:].rearrange("p k c d -> p (k c) d"),
                                             prob[b][:].rearrange("p k c -> p (k c)").unsqueeze(2).to_broadcast(
                                                 [P, 4 * NCH, C]), ALU.mult))
                    V.tensor_reduce(mix[b][:].rearrange("p c d -> p (c d)"),
                                    cen[b][:].rearrange("p k c d -> p (c d) k"), AX_X, ALU.add
                                    ).then_inc(mix_ready[b], 1)
                for b in range(2):
                    dve.wait_ge(mix_squared[b], START + i + 1)
                    V.tensor_reduce(mix2[b][:], squares[b][:, 0], AX_X, ALU.add).then_inc(mix2_ready[b], 1)
                for b in range(2):
                    dve.wait_ge(mixr_ready[b], START + i + 1)
                    own.link(V.tensor_tensor(mix[b][:], mix[b][:], over_channels(mixr[b][:]), ALU.mult))
                    V.transpose(mixT[b], mix[b][:].rearrange("p c d -> p (c d)")).then_inc(mixT_ready[b], 1)
                for b in range(2):
                    dve.wait_ge(out_made[b], START + i + 1)
                    dve.wait_ge(x_in[b], START + 16 * (i + 1))
                    V.tensor_tensor(x1[b][:].rearrange("p t d -> p (t d)"), psS[b][:, 0], xres[b][:].rearrange(
                        "p t d -> p (t d)"), ALU.add).then_inc(x1_ready[b], 1)
                own.restart()

        @block.tensor
        def _(pe):
            mm = nc.tensor.matmul

            def ready(b, i, e, step):
                for s in (diag_act, diag_pool, diag_dve):
                    pe.wait_ge(s[b], START + DIAGS * i + e + 1)
                pe.wait_ge(kept[b], START + STEPS * i + step)

            pe.wait_ge(set_up, START + 2)
            with pe.Fori(0, PAIRS) as i:
                for b in range(2):
                    ready(b, i, KT, GRAM)
                    for u in range(NCH):
                        ins = mm(psA[b][:, u], diag[BUF[KT]][b][:, u], cm[b][:, u, 1:3], start=True, stop=True)
                    ins.then_inc(made[b], 1)
                for lv in range(5):
                    part = slice(0, 1) if lv == 0 else slice(1, 2) if lv == 4 else slice(0, 2)
                    for b in range(2):
                        ready(b, i, A + lv, SQ0 + lv)
                        for u in range(NCH):
                            ins = mm(psA[b][:, u, part], diag[BUF[A + lv]][b][:, u], rows[lv % 2][b][:, u, part],
                                     start=True, stop=True)
                        ins.then_inc(made[b], 1)
                for e, step, rhs in ((TT, UW, vk), (W, MW, ka)):
                    for b in range(2):
                        ready(b, i, e, step)
                        for u in range(NCH):
                            ins = mm(psA[b][:, u], diag[BUF[e]][b][:, u], rhs[b][:, u], start=True, stop=True)
                        ins.then_inc(made[b], 1)
                for b in range(2):
                    ready(b, i, QE, OUT)
                    pe.wait_ge(x1_ready[b], START + i)
                for u in range(NCH):
                    for b in range(2):
                        if u < NCH - 1:
                            mm(psS[b][:, u % 2, 0:C], diag[BUF[K]][b][:, u], uw[b][:, u, 0], start=True, stop=(u == 0)
                               ).then_inc(state_made[b], 1) if u == 0 else \
                                mm(psS[b][:, u % 2, 0:C], diag[BUF[K]][b][:, u], uw[b][:, u, 0], start=True, stop=False)
                        if u:
                            pe.wait_ge(state_ready[b], START + (NCH - 1) * i + u)
                            if u < NCH - 1:
                                mm(psS[b][:, u % 2, 0:C], diag[BUF[IM]][b][:, u], state[b][:, u], start=False, stop=True
                                   ).then_inc(state_made[b], 1)
                    for b in range(2):
                        out = psA[b][:].rearrange("p c k d -> p (c k) d")[:, u]
                        ins = mm(out, diag[BUF[ATT]][b][:, u], uw[b][:, u, 0], start=True, stop=(u == 0))
                        if u:
                            ins = mm(out, diag[BUF[QE]][b][:, u], state[b][:, u], start=False, stop=True)
                        if u == NCH - 1:
                            ins.then_inc(made[b], 1)
                for b in range(2):
                    pe.wait_ge(mixT_ready[b], START + i + 1)
                    for t in range(TILES):
                        ins = mm(psS[b][:, 0, bass.ts(t, P)], mixT[b][:, bass.ts(t, P)], w_os[:], start=True, stop=True)
                    ins.then_inc(out_made[b], 1)


def phase_route(nc, dram, keep, layer):
    K = 2 if layer == 0 else 1
    G = G0 if layer == 0 else G1
    BIG = float(1 << 20)
    with ExitStack() as ctx:
        def sb(name, shape, dt=F32):
            return ctx.enter_context(nc.sbuf_tensor(f"{name}_l{layer}", shape, dt))

        signals = Signals(nc, ctx)
        sem, sem2 = signals.one, signals.two

        tri = sb("tri", [P, P])
        ones = sb("ones", [P, P])
        expert = sb("expert", [P, E])
        desc = sb("desc", [P, E])
        starts = sb("starts", [P, G0])
        best = [sb(f"best{k}", [P, NT]) for k in range(2)]
        first = sb("first", [P, NT])
        flag = sb("flag", [P, NT, E])
        rest = sb("rest", [P, NT, E])
        sel = [sb(f"sel{k}", [P, NT, E]) for k in range(K)]
        run = [sb(f"run{k}", [P, E, NT]) for k in range(K)]
        place = sb("place", [P, NT, E])
        rank = sb("rank", [P, NT])
        base = sb("base", [P, NT])
        over = sb("over", [P, NT])
        row = sb("row", [P, NT])
        pexp = sb("pexp", [P, NT, E])
        pone = sb("pone", [P, NT])
        padf = sb("padf", [P, E])
        padi = sb("padi", [P, E], I32)
        ends = sb("ends", [P, E])
        past = sb("past", [P, G0, E])
        gidf = sb("gidf", [P, G0])
        index = [sb(f"index{b}", [P, TILES, K], U32) for b in range(2)]
        xn = [sb(f"xnr{b}", [P, TILES, D]) for b in range(2)]
        psC = [ctx.enter_context(nc.psum_tensor(f"psC{k}_l{layer}", [P, NT, E], F32)) for k in range(K)]
        psN = [ctx.enter_context(nc.psum_tensor(f"psN{k}_l{layer}", [P, NT, E], F32)) for k in range(K)]

        const_in = sem("route_const_in")
        ones_set = sem("ones_set")
        chosen = sem("chosen")
        counted = sem("counted")
        gaps_ready = sem("gaps_ready")
        exp_ready = sem("route_exp_ready")
        routed = sem("routed")
        xn_in = sem2("xnr_in")
        index_ready = sem2("index_ready")
        rows_free = sem2("rows_free")
        scattered = keep["scattered"][layer]
        dve_own = signals.own("dve_own")
        pool_passed = signals.one("pool_passed")
        block = signals.block()

        @block.sync
        def _(sp):
            consts = [(tri, "tri"), (expert, "expert"), (starts, "starts")]
            if layer == 0:
                consts.append((keep["group"], "group0"))
            for dst, name in consts:
                sp.dma_start(dst[:], dram[name]).then_inc(const_in, 16)
            source = dram["xn" if layer == 0 else "xn1"]
            with sp.Fori(0, PAIRS) as i:
                for b in range(2):
                    sp.wait_ge(rows_free[b], START + i)
                    sp.dma_start(xn[b][:], source[bass.ds(2 * i + b, 1)].rearrange("a (t p) d -> p (a t) d", p=P)
                                 ).then_inc(xn_in[b], 16)

        CONSTS = 16 * (4 if layer == 0 else 3)

        @block.gpsimd
        def _(pool):
            def wait(signal, value):
                pool.wait_ge(signal, value)
                pool.sem_inc(pool_passed, 1)

            nc.gpsimd.memset(ones[:], 1.0).then_inc(ones_set, 1)
            with pool.Fori(0, PAIRS) as i:
                for b in range(2):
                    wait(index_ready[b], START + i + 1)
                    wait(xn_in[b], START + 16 * (i + 1))
                    for t in range(TILES):
                        for k in range(K):
                            pool.indirect_dma_start(
                                out=dram[f"slots{layer}"][:, :],
                                out_offset=bass.IndirectOffsetOnAxis(ap=index[b][:, t, k:k + 1], axis=0),
                                in_=xn[b][:, t, :], in_offset=None, bounds_check=G * GS - 1, oob_is_err=False
                            ).then_inc(scattered[b], 16)
                for b in range(2):
                    wait(scattered[b], 16 * K * TILES * (i + 1))
                    pool.sem_inc(rows_free[b], 1)
            for b in range(2):
                pool.wait_ge(scattered[b], 16 * K * TILES * PAIRS)

        @block.scalar
        def _(act):
            act.wait_ge(gaps_ready, START + 1)
            if layer == 0:
                nc.scalar.activation(over[:], row[:], ACT.Exp).then_inc(exp_ready, 1)
            else:
                nc.scalar.activation(pexp[:], rest[:], ACT.Exp).then_inc(exp_ready, 1)

        @block.tensor
        def _(pe):
            pe.wait_ge(ones_set, START + 1)
            pe.wait_ge(const_in, START + CONSTS)
            for k in range(K):
                pe.wait_ge(chosen, START + k + 1)
                flat = sel[k][:].rearrange("p t e -> p (t e)")
                nc.tensor.matmul(psC[k][:].rearrange("p t e -> p (t e)"), tri[:], flat, start=True, stop=True)
                nc.tensor.matmul(psN[k][:].rearrange("p t e -> p (t e)"), ones[:], flat, start=True, stop=True
                                 ).then_inc(counted, 1)

        @block.vector
        def _(dve):
            own = Chain(dve, dve_own)
            V = nc.vector
            logits = keep["logits"][:].rearrange("p (t e) -> p t e", e=E)

            def by_token(ap):
                return ap.unsqueeze(2).to_broadcast([P, NT, E])

            def by_expert(ap):
                return ap.unsqueeze(1).to_broadcast([P, NT, E])

            def choose(values, k):
                own.link(V.tensor_reduce(best[k][:], values, AX_X, ALU.max))
                own.link(V.tensor_tensor(flag[:], values, by_token(best[k][:]), ALU.is_equal))
                own.link(V.tensor_tensor(flag[:], flag[:], by_expert(desc[:]), ALU.mult))
                own.link(V.tensor_reduce(first[:], flag[:], AX_X, ALU.max))
                own.link(V.tensor_tensor(sel[k][:], by_expert(desc[:]), by_token(first[:]), ALU.is_equal))
                dve.sem_inc(chosen, 1)

            dve.wait_ge(const_in, START + CONSTS)
            dve.wait_ge(ones_set, START + 1)
            own.link(V.tensor_scalar(desc[:], expert[:], -1.0, float(E), ALU.mult, ALU.add))
            choose(logits, 0)
            if layer == 0:
                own.link(V.scalar_tensor_tensor(out=rest[:], in0=sel[0][:], scalar=-1e30, in1=logits,
                                                op0=ALU.mult, op1=ALU.add))
                choose(rest[:], 1)
                own.link(V.tensor_tensor(row[:], best[1][:], best[0][:], ALU.subtract))
            else:
                own.link(V.tensor_tensor(rest[:], logits, by_token(best[0][:]), ALU.subtract))
            dve.sem_inc(gaps_ready, 1)
            dve.wait_ge(exp_ready, START + 1)
            if layer == 0:
                own.link(V.tensor_scalar(pone[:], over[:], 1.0, None, ALU.add))
                own.link(V.reciprocal(keep["prob"][:, :, 0], pone[:]))
                own.link(V.tensor_tensor(keep["prob"][:, :, 1], over[:], keep["prob"][:, :, 0], ALU.mult))
            else:
                own.link(V.tensor_reduce(pone[:], pexp[:], AX_X, ALU.add))
                own.link(V.reciprocal(keep["prob"][:, :, 0], pone[:]))
            for k in range(K):
                dve.wait_ge(counted, START + k + 1)
                for e in range(E):
                    own.step(V.tensor_tensor_scan(run[k][:, e, :], ones[:, 0:NT], psN[k][:, :, e],
                                                  0.0 if k == 0 else run[0][:, e, NT - 1:NT], ALU.mult, ALU.add))
                own.wait()
            if layer == 1:
                own.link(V.tensor_scalar(padf[:], run[0][:, :, NT - 1], float(GS - 1), None, ALU.add))
                own.link(V.tensor_copy(padi[:], padf[:]))
                shift = GS.bit_length() - 1
                own.link(V.tensor_scalar(padi[:], padi[:], shift, shift, ALU.arith_shift_right,
                                         ALU.logical_shift_left))
                own.link(V.tensor_copy(padf[:], padi[:]))
                own.link(V.tensor_tensor_scan(ends[:], ones[:, 0:E], padf[:], 0.0, ALU.mult, ALU.add))
                own.link(V.tensor_tensor(past[:], starts[:].unsqueeze(2).to_broadcast([P, G0, E]),
                                         ends[:].unsqueeze(1).to_broadcast([P, G0, E]), ALU.is_ge))
                own.link(V.tensor_reduce(gidf[:], past[:], AX_X, ALU.add))
                own.link(V.tensor_scalar(gidf[:], gidf[:], float(E - 1), None, ALU.min))
                own.link(V.tensor_copy(keep["group"][:], gidf[:]))
                own.link(V.tensor_tensor(ends[:], ends[:], padf[:], ALU.subtract))
                begins = ends
            else:
                own.link(V.tensor_scalar(ends[:], expert[:], float(CAP0), None, ALU.mult))
                begins = ends
            for k in range(K):
                runs = run[k][:].rearrange("p e t -> p t e")
                own.link(V.tensor_tensor(place[:], runs, psN[k][:], ALU.subtract))
                own.link(V.tensor_tensor(place[:], place[:], psC[k][:], ALU.add))
                own.link(V.tensor_tensor(place[:], place[:], sel[k][:], ALU.mult))
                own.link(V.tensor_reduce(rank[:], place[:], AX_X, ALU.add))
                own.link(V.tensor_scalar(rank[:], rank[:], -1.0, None, ALU.add))
                own.link(V.tensor_tensor(flag[:], sel[k][:], by_expert(begins[:]), ALU.mult))
                own.link(V.tensor_reduce(base[:], flag[:], AX_X, ALU.add))
                if layer == 0:
                    own.link(V.tensor_scalar(over[:], rank[:], float(CAP0), BIG, ALU.is_ge, ALU.mult))
                    own.link(V.tensor_tensor(row[:], base[:], rank[:], ALU.add))
                    own.link(V.tensor_tensor(row[:], row[:], over[:], ALU.add))
                    own.link(V.tensor_copy(keep["slot"][:, :, k], row[:]))
                    own.link(V.tensor_scalar(over[:], rank[:], float(CAP0), None, ALU.is_lt))
                    own.link(V.tensor_tensor(keep["prob"][:, :, k], keep["prob"][:, :, k], over[:], ALU.mult))
                    own.link(V.tensor_scalar(rank[:], rank[:], float(CAP0 - 1), None, ALU.min))
                own.link(V.tensor_tensor(row[:], base[:], rank[:], ALU.add))
                if layer == 1:
                    own.link(V.tensor_copy(keep["slot"][:, :, 0], row[:]))
                own.link(V.tensor_copy(keep["slot"][:, :, 2 + k], row[:]))
            own.restart()
            with dve.Fori(0, PAIRS) as i:
                for b in range(2):
                    dve.wait_ge(rows_free[b], START + i)
                    V.tensor_copy(index[b][:], keep["slot"][:, bass.ds((2 * i + b) * TILES, TILES), 0:K]
                                  ).then_inc(index_ready[b], 1)


def phase_experts(nc, dram, keep, layer):
    G = G0 if layer == 0 else G1
    with ExitStack() as ctx:
        def sb2(name, shape, dt=F32):
            return [ctx.enter_context(nc.sbuf_tensor(f"{name}{b}_l{layer}", shape, dt)) for b in range(2)]

        signals = Signals(nc, ctx)
        sem2 = signals.two

        ident = keep["ident"]
        rows = sb2("rows", [P, GS // P, D])
        rowsT = sb2("rowsT", [P, GS])
        w_up = sb2("w_up", [P, FF])
        w_down = sb2("w_down", [P, FT, D])
        b_up = sb2("b_up", [P, FT])
        b_down = sb2("b_down", [P, D])
        relu = sb2("relu", [P, FT, GS])
        hid = sb2("ehid", [P, FT, GS])
        outs = sb2("outs", [P, GS // P, D])
        psT = ctx.enter_context(nc.psum_tensor(f"psXT_l{layer}", [P, GS], F32))
        psH = ctx.enter_context(nc.psum_tensor(f"psEH_l{layer}", [P, FT, GS], F32))
        psY = [ctx.enter_context(nc.psum_tensor(f"psY{b}_l{layer}", [P, GS // P, D], F32)) for b in range(2)]

        rows_in = sem2("rows_in")
        up_in = sem2("up_in")
        down_in = sem2("down_in")
        rowsT_made = sem2("rowsT_made")
        rowsT_ready = sem2("rowsT_ready")
        up_made = sem2("up_made")
        relu_ready = sem2("relu_ready")
        hid_act = sem2("hid_act")
        hid_dve = sem2("hid_dve")
        down_made = sem2("down_made")
        outs_ready = sem2("outs_ready")
        outs_stored = sem2("outs_stored")
        pool_passed = signals.one("pool_passed")
        block = signals.block()
        DOWN_IN = 16 if layer == 0 else 48

        @block.sync
        def _(sp):
            slots = dram[f"slots{layer}"].rearrange("(g t p) d -> g p t d", p=P, t=GS // P)
            done = dram[f"rows{layer}"].rearrange("(g t p) d -> g p t d", p=P, t=GS // P)

            def load(b, g, c):
                sp.wait_ge(rowsT_made[b], START + c)
                sp.dma_start(rows[b][:], slots[bass.ds(g, 1)].rearrange("a p t d -> p (a t) d")
                             ).then_inc(rows_in[b], 16)
                e = sp.value_load(keep["group"][0:1, bass.ds(g, 1)], min_val=0, max_val=E - 1)
                sp.wait_ge(up_made[b], START + FT * c)
                sp.dma_start(w_up[b][:], dram[f"w_fc{layer}"][bass.ds(e, 1)].rearrange("a c f -> c (a f)")
                             ).then_inc(up_in[b], 16)
                sp.wait_ge(down_made[b], START + c)
                sp.dma_start(w_down[b][:], dram[f"w_down{layer}"][bass.ds(e, 1)].rearrange(
                    "a (k p) d -> p (a k) d", p=P)).then_inc(down_in[b], 16)
                if layer == 1:
                    sp.wait_ge(hid_act[b], START + c)
                    sp.wait_ge(hid_dve[b], START + c)
                    sp.dma_start(b_up[b][:], dram["b_fc1"][bass.ds(e, 1)].rearrange("a p k -> p (a k)")
                                 ).then_inc(down_in[b], 16)
                    sp.wait_ge(outs_ready[b], START + c)
                    sp.dma_start(b_down[b][:], dram["b_down1"][bass.ds(e, 1)].rearrange(
                        "a k d -> (a k) d").to_broadcast([P, D])).then_inc(down_in[b], 16)

            def store(b, g, c):
                sp.wait_ge(outs_ready[b], START + c + 1)
                sp.dma_start(done[bass.ds(g, 1)].rearrange("a p t d -> p (a t) d"), outs[b][:]
                             ).then_inc(outs_stored[b], 16)

            for b in range(2):
                load(b, b, 0)
            with sp.Fori(0, G // 2 - 1) as i:
                for b in range(2):
                    load(b, 2 * i + 2 + b, i + 1)
                    store(b, 2 * i + b, i)
            for b in range(2):
                store(b, G - 2 + b, G // 2 - 1)
            for b in range(2):
                sp.wait_ge(outs_stored[b], START + 16 * (G // 2))

        @block.scalar
        def _(act):
            with act.Fori(0, G // 2) as i:
                for b in range(2):
                    act.wait_ge(rowsT_made[b], START + i + 1)
                    act.wait_ge(up_made[b], START + FT * i)
                    nc.scalar.copy(rowsT[b][:], psT[:]).then_inc(rowsT_ready[b], 1)
                    if layer == 1:
                        act.wait_ge(down_in[b], START + DOWN_IN * (i + 1))
                        act.wait_ge(down_made[b], START + i)
                    else:
                        act.wait_ge(hid_dve[b], START + i)
                    for m in range(FT if layer == 0 else 2):
                        act.wait_ge(up_made[b], START + FT * i + m + 1)
                        if layer == 0:
                            nc.scalar.activation(relu[b][:, m], psH[:, m], ACT.Relu).then_inc(relu_ready[b], 1)
                        else:
                            ins = nc.scalar.activation(hid[b][:, m], psH[:, m], ACT.Relu, bias=b_up[b][:, m:m + 1])
                    if layer == 1:
                        ins.then_inc(hid_act[b], 1)

        @block.vector
        def _(dve):
            def evacuate(b, c):
                dve.wait_ge(down_made[b], START + c + 1)
                dve.wait_ge(outs_stored[b], START + 16 * c)
                if layer == 0:
                    ins = nc.vector.tensor_copy(outs[b][:], psY[b][:])
                else:
                    ins = nc.vector.tensor_tensor(outs[b][:], psY[b][:], b_down[b][:].unsqueeze(1).to_broadcast(
                        [P, GS // P, D]), ALU.add)
                ins.then_inc(outs_ready[b], 1)

            def activate(b, c):
                dve.wait_ge(down_made[b], START + c)
                if layer == 1:
                    dve.wait_ge(down_in[b], START + DOWN_IN * (c + 1))
                for m in range(0 if layer == 0 else 2, FT):
                    if layer == 0:
                        dve.wait_ge(relu_ready[b], START + FT * c + m + 1)
                        ins = nc.vector.tensor_tensor(hid[b][:, m], relu[b][:, m], relu[b][:, m], ALU.mult)
                    else:
                        dve.wait_ge(up_made[b], START + FT * c + m + 1)
                        ins = nc.vector.tensor_scalar(hid[b][:, m], psH[:, m], b_up[b][:, m:m + 1], 0.0,
                                                      ALU.add, ALU.max)
                ins.then_inc(hid_dve[b], 1)

            activate(0, 0)
            with dve.Fori(0, G // 2 - 1) as i:
                activate(1, i)
                evacuate(0, i)
                activate(0, i + 1)
                evacuate(1, i)
            activate(1, G // 2 - 1)
            evacuate(0, G // 2 - 1)
            evacuate(1, G // 2 - 1)

        @block.tensor
        def _(pe):
            mm = nc.tensor.matmul

            def turn(b, c):
                pe.wait_ge(rows_in[b], START + 16 * (c + 1))
                pe.wait_ge(rowsT_ready[1 - b], START + c + b)
                for t in range(GS // P):
                    ins = nc.tensor.transpose(psT[:, bass.ts(t, P)], rows[b][:, t, :], ident[:])
                ins.then_inc(rowsT_made[b], 1)

            def up(b, c):
                pe.wait_ge(rowsT_ready[b], START + c + 1)
                pe.wait_ge(up_in[b], START + 16 * (c + 1))
                if layer == 0:
                    pe.wait_ge(relu_ready[1 - b], START + FT * (c + b))
                else:
                    pe.wait_ge(hid_act[1 - b], START + c + b)
                    pe.wait_ge(hid_dve[1 - b], START + c + b)
                for m in range(FT):
                    mm(psH[:, m], w_up[b][:, bass.ts(m, P)], rowsT[b][:], start=True, stop=True).then_inc(up_made[b], 1)

            def down(b, c):
                if layer == 1:
                    pe.wait_ge(hid_act[b], START + c + 1)
                pe.wait_ge(hid_dve[b], START + c + 1)
                pe.wait_ge(down_in[b], START + DOWN_IN * (c + 1))
                pe.wait_ge(outs_ready[b], START + c)
                for t in range(GS // P):
                    for m in range(FT):
                        ins = mm(psY[b][:, t], hid[b][:, m, bass.ts(t, P)], w_down[b][:, m], start=(m == 0),
                                 stop=(m == FT - 1))
                ins.then_inc(down_made[b], 1)

            turn(0, 0)
            up(0, 0)
            turn(1, 0)
            with pe.Fori(0, G // 2 - 1) as i:
                up(1, i)
                turn(0, i + 1)
                down(0, i)
                up(0, i + 1)
                turn(1, i + 1)
                down(1, i)
            up(1, G // 2 - 1)
            down(0, G // 2 - 1)
            down(1, G // 2 - 1)


def phase_route0(nc, dram, keep):
    phase_route(nc, dram, keep, 0)


def phase_route1(nc, dram, keep):
    phase_route(nc, dram, keep, 1)


def phase_experts0(nc, dram, keep):
    phase_experts(nc, dram, keep, 0)


def phase_experts1(nc, dram, keep):
    phase_experts(nc, dram, keep, 1)


def phase_linear(nc, dram, keep):
    W = C // SUB
    with ExitStack() as ctx:
        def sb(name, shape, dt=F32):
            return ctx.enter_context(nc.sbuf_tensor(name, shape, dt))

        def sb2(name, shape, dt=F32):
            return [sb(f"{name}{b}", shape, dt) for b in range(2)]

        signals = Signals(nc, ctx)
        sem, sem2 = signals.one, signals.two

        ident = keep["ident"]
        w_in = sb("w_in1", [P, 4, D])
        b_qkv = sb("b_qkv1", [P, 3])
        b_n = sb("b_n1", [P, 1])
        neg_b_n = sb("neg_b_n1", [P, 1])
        w_out = sb("w_out1", [P, D])
        b_out = sb("b_out1", [1, D])
        w_rout = sb("w_rout1s", [P, E])
        masks = sb("masks1", [P, 4, C])
        subs = sb("subs", [P, SUB])
        ones = sb("ones1", [1, P])
        half = sb("neg_half", [P, TILES])
        index = sb2("index1", [P, TILES, 2], U32)
        share = sb2("share1", [P, TILES, 2])
        got = [sb2(f"got{k}", [P, TILES, D]) for k in range(2)]
        x2 = sb2("x2s", [P, TILES, D])
        stats = sb2("stats1", [P, TILES, 6])
        moments = sb2("moments1", [P, TILES, 2])
        var = sb2("var1", [P, TILES])
        rstd = sb2("rstd1", [P, TILES])
        xn = sb2("xn1s", [P, TILES, D])
        xnT = sb2("xnT1", [P, LEN])
        qkv = sb2("qkv1", [P, 3, NCH, C])
        norm = sb2("norm1", [P, LEN])
        kv = sb2("kv1", [P, 2, NCH, C])
        diag = [sb2(f"ldiag{k}", [P, NCH, P]) for k in range(2)]
        v_sub = sb2("v_sub", [P, NCH, SUB * (P + W)])
        q_sub = sb2("q_sub", [P, NCH, SUB, C])
        score = q_sub
        score = sb2("score", [P, NCH // 2, SUB, C])
        sums = [sb2(f"zsum{k}", [P, NCH, C]) for k in range(2)]
        ctxT = norm

        bank = [[ctx.enter_context(nc.psum_tensor(f"bank{k}_{b}", [P, 512], F32)) for b in range(2)] for k in range(4)]

        const_in = sem("lin_const_in")
        clear = sem("lin_clear")
        set_up = sem("lin_set_up")
        index_ready = sem2("lin_index")
        gathered = keep["gathered"][0]
        x_in = sem2("lin_x_in")
        ln_stats = sem2("lin_stats")
        rstd_ready = sem2("lin_rstd")
        xn_ready = sem2("lin_xn")
        xn_stored = sem2("lin_xn_stored")
        xnT_made = sem2("lin_xnT_made")
        xnT_ready = sem2("lin_xnT")
        logits_made = sem2("lin_logits_made")
        logits_kept = sem2("lin_logits_kept")
        proj_made = sem2("lin_proj_made")
        proj_ready = sem2("lin_proj_ready")
        norm_ready = sem2("lin_norm_ready")
        source = sem2("lin_source")
        diag_act = sem2("lin_diag_act")
        diag_pool = sem2("lin_diag_pool")
        diag_dve = sem2("lin_diag_dve")
        score_made = sem2("score_made")
        score_ready = sem2("score_ready")
        z_made = sem2("z_made")
        ctx_made = sem2("ctx_made")
        ctx_ready = sem2("ctx_ready")
        out_made = sem2("lin_out_made")
        x3_ready = sem2("x3_ready")
        x3_stored = sem2("x3_stored")
        dve_own = signals.own("dve_own")
        pool_own = signals.own("pool_own")
        pool_passed = signals.one("pool_passed")
        block = signals.block()

        KT, V, K, Z = range(4)
        DIAGS = 4
        HALF = NCH // 2
        CONSTS = 16 * 11
        v_cols = [v_sub[b][:].rearrange("p c (s w) -> p c s w", s=SUB) for b in range(2)]

        def spread(wait, copy, qs, e, b, i, done):
            if e == KT:
                wait(proj_ready[b], START + i + 1)
            else:
                wait(source[b], START + 3 * i + e)
            if e in (KT, V, K):
                wait(ctx_made[b], START + 2 * i)
            else:
                wait(score_made[b], START + 2 * (i + 1))
            for q in qs:
                if e == V:
                    ins = copy(v_cols[b][quad(q), :, :, C * q:C * q + W],
                               kv[b][quad(q), 1].rearrange("p c (s w) -> p c s w", w=W))
                elif e == Z:
                    ins = copy(diag[0][b][quad(q), 1:NCH, quad(q)], sums[0][b][quad(q), 0:NCH - 1])
                else:
                    ins = copy(diag[0 if e == KT else 1][b][quad(q), :, quad(q)],
                               (qkv if e == KT else kv)[b][quad(q), 1 if e == KT else 0])
            ins.then_inc(done[b], 1)

        @block.sync
        def _(sp):
            for dst, name in ((w_in[:, 0], "w_q1"), (w_in[:, 1], "w_k1"), (w_in[:, 2], "w_v1"), (w_in[:, 3], "w_n1"),
                              (b_qkv[:], "b_qkv1"), (b_n[:], "b_n1"), (w_out[:], "w_o1"), (b_out[:], "b_o1"),
                              (w_rout[:], "w_rout1"), (masks[:], "masks"), (subs[:], "subs")):
                sp.dma_start(dst, dram[name]).then_inc(const_in, 16)

            def rows(name, n):
                return dram[name][bass.ds(n, 1)].rearrange("a (t p) d -> p (a t) d", p=P)

            with sp.Fori(0, PAIRS) as i:
                for b in range(2):
                    sp.wait_ge(x3_stored[b], START + 16 * i)
                    sp.dma_start(x2[b][:], rows("x1", 2 * i + b)).then_inc(x_in[b], 16)
                for b in range(2):
                    sp.wait_ge(xn_ready[b], START + i + 1)
                    sp.dma_start(rows("xn1", 2 * i + b), xn[b][:]).then_inc(xn_stored[b], 16)
                for b in range(2):
                    sp.wait_ge(x3_ready[b], START + i + 1)
                    sp.dma_start(rows("x3", 2 * i + b), x2[b][:]).then_inc(x3_stored[b], 16)
            for b in range(2):
                sp.wait_ge(xn_stored[b], START + 16 * PAIRS)
                sp.wait_ge(x3_stored[b], START + 16 * PAIRS)

        @block.gpsimd
        def _(pool):
            def wait(signal, value):
                pool.wait_ge(signal, value)
                pool.sem_inc(pool_passed, 1)

            own = Chain(pool, pool_own)
            for b in range(2):
                for ap in (diag[0][b][:], diag[1][b][:], v_sub[b][:]):
                    nc.gpsimd.memset(ap, 0.0).then_inc(clear, 1)
            nc.gpsimd.memset(half[:], -0.5).then_inc(clear, 1)
            nc.gpsimd.memset(ones[:], 1.0).then_inc(clear, 1)
            pool.wait_ge(clear, START + 8)

            def gather(b, c):
                wait(index_ready[b], START + c + 1)
                for t in range(TILES):
                    for k in range(2):
                        pool.indirect_dma_start(
                            out=got[k][b][:, t, :], out_offset=None, in_=dram["rows0"][:, :],
                            in_offset=bass.IndirectOffsetOnAxis(ap=index[b][:, t, k:k + 1], axis=0),
                            bounds_check=G0 * GS - 1, oob_is_err=False).then_inc(gathered[b], 16)

            with pool.Fori(0, PAIRS) as i:
                for b in range(2):
                    gather(b, i)
                for b in range(2):
                    wait(ln_stats[b], START + i + 1)
                    own.link(nc.gpsimd.tensor_scalar(var[b][:], moments[b][:, :, 1], EPS, None, ALU.add))
                    own.link(nc.gpsimd.tensor_tensor(rstd[b][:], var[b][:], half[:], ALU.pow))
                    pool.sem_inc(rstd_ready[b], 1)
                for e in range(DIAGS):
                    for b in range(2):
                        spread(wait, nc.gpsimd.tensor_copy, (2,), e, b, i, diag_pool)
                for b in range(2):
                    wait(diag_pool[b], START + DIAGS * (i + 1))
                own.restart()

        @block.scalar
        def _(act):
            act.wait_ge(set_up, START + 1)
            act.wait_ge(clear, START + 8)

            def expand(es, i):
                for e in es:
                    for b in range(2):
                        spread(act.wait_ge, nc.scalar.copy, (0, 1), e, b, i, diag_act)

            with act.Fori(0, PAIRS) as i:
                for b in range(2):
                    act.wait_ge(xnT_made[b], START + i + 1)
                    nc.scalar.copy(xnT[b][:], bank[0][b][:]).then_inc(xnT_ready[b], 1)
                for b in range(2):
                    for j, k in ((0, 2), (1, 3), (2, 0)):
                        act.wait_ge(proj_made[b], START + 4 * i + j + 1)
                        ins = nc.scalar.activation(qkv[b][:, j].rearrange("p c d -> p (c d)"), bank[k][b][:],
                                                   ACT.Identity, bias=b_qkv[:, j:j + 1])
                    ins.then_inc(proj_ready[b], 1)
                    act.wait_ge(proj_ready[b], START + i + 1)
                    act.wait_ge(proj_made[b], START + 4 * i + 4)
                    nc.scalar.activation(norm[b][:], bank[1][b][:], ACT.Exp, bias=neg_b_n[:, 0:1], scale=-1.0
                                         ).then_inc(norm_ready[b], 1)
                    for s in range(SUB):
                        ins = nc.scalar.activation(q_sub[b][:, :, s], qkv[b][:, 0], ACT.Copy, scale=subs[:, s:s + 1])
                    ins.then_inc(norm_ready[b], 1)
                expand((KT, V, K, Z), i)

        @block.vector
        def _(dve):
            own = Chain(dve, dve_own)
            Ve = nc.vector

            def expand(es, i):
                for e in es:
                    for b in range(2):
                        spread(dve.wait_ge, Ve.tensor_copy, (3,), e, b, i, diag_dve)

            dve.wait_ge(const_in, START + CONSTS)
            dve.wait_ge(clear, START + 8)
            Ve.tensor_scalar(neg_b_n[:], b_n[:], -1.0, None, ALU.mult).then_inc(set_up, 1)
            with dve.Fori(0, PAIRS) as i:
                for b in range(2):
                    n = 2 * i + b
                    own.link(Ve.tensor_copy(share[b][:], keep["prob"][:, bass.ds(n * TILES, TILES), :]))
                    Ve.tensor_copy(index[b][:], keep["slot"][:, bass.ds(n * TILES, TILES), 2:4]
                                   ).then_inc(index_ready[b], 1)
                for b in range(2):
                    dve.wait_ge(x_in[b], START + 16 * (i + 1))
                    dve.wait_ge(gathered[b], 16 * 2 * TILES * (i + 1))
                    for k in range(2):
                        for t in range(TILES):
                            own.step(Ve.scalar_tensor_tensor(out=x2[b][:, t], in0=got[k][b][:, t],
                                                             scalar=share[b][:, t, k:k + 1], in1=x2[b][:, t],
                                                             op0=ALU.mult, op1=ALU.add))
                        own.wait()
                    for t in range(TILES):
                        own.step(Ve.bn_stats(stats[b][:, t, :], x2[b][:, t, :]))
                    own.wait()
                    for t in range(TILES):
                        ins = Ve.bn_aggr(moments[b][:, t, :], stats[b][:, t, :])
                    ins.then_inc(ln_stats[b], 1)
                for b in range(2):
                    dve.wait_ge(rstd_ready[b], START + i + 1)
                    dve.wait_ge(xn_stored[b], START + 16 * i)
                    dve.wait_ge(xnT_made[b], START + i)
                    for t in range(TILES):
                        ins = Ve.tensor_scalar(xn[b][:, t, :], x2[b][:, t, :], moments[b][:, t, 0:1],
                                               rstd[b][:, t:t + 1], ALU.subtract, ALU.mult)
                    ins.then_inc(xn_ready[b], 1)
                for b in range(2):
                    dve.wait_ge(logits_made[b], START + i + 1)
                    Ve.tensor_copy(keep["logits"][:, bass.ds((2 * i + b) * TILES * E, TILES * E)],
                                   bank[1][b][:, 0:TILES * E]).then_inc(logits_kept[b], 1)
                for b in range(2):
                    dve.wait_ge(proj_ready[b], START + i + 1)
                    dve.wait_ge(ctx_made[b], START + 2 * i)
                    own.step(Ve.transpose(kv[b][:, 1], qkv[b][:, 2]))
                    own.link(Ve.transpose(kv[b][:, 0], qkv[b][:, 1]))
                    dve.sem_inc(source[b], 2)
                expand((KT, V, K), i)
                for b in range(2):
                    dve.wait_ge(z_made[b], START + i + 1)
                    own.link(Ve.tensor_tensor(sums[0][b][:], bank[2][b][:].rearrange("p (c d) -> p c d", d=C),
                                              masks[:, 3:4, :].to_broadcast([P, NCH, C]), ALU.mult))
                    dve.sem_inc(score_ready[b], 1)
                for lv in range(4):
                    reach = 1 << lv
                    old, new = sums[lv % 2], sums[1 - lv % 2]
                    for b in range(2):
                        own.step(Ve.tensor_copy(new[b][:, 0:reach], old[b][:, 0:reach]))
                        own.link(Ve.tensor_tensor(new[b][:, reach:NCH], old[b][:, reach:NCH],
                                                  old[b][:, 0:NCH - reach], ALU.add))
                for h in range(2):
                    if h == 0:
                        for b in range(2):
                            dve.sem_inc(source[b], 1)
                    for b in range(2):
                        dve.wait_ge(score_made[b], START + 2 * i + h + 1)
                        dve.wait_ge(ctx_made[b], START + 2 * i + h)
                        for k in range(2):
                            ins = Ve.tensor_tensor(
                                score[b][:, k * HALF // 2:(k + 1) * HALF // 2].rearrange("p c s d -> p (c s) d"),
                                bank[k][b][:].rearrange("p (c d) -> p c d", d=C),
                                masks[:, 1:2, :].to_broadcast([P, NCH, C]), ALU.mult)
                        ins.then_inc(score_ready[b], 1)
                    if h == 0:
                        expand((Z,), i)
                for b in range(2):
                    dve.wait_ge(ctx_made[b], START + 2 * (i + 1))
                    Ve.tensor_tensor(ctxT[b][:], bank[2][b][:], norm[b][:], ALU.mult).then_inc(ctx_ready[b], 1)
                for b in range(2):
                    dve.wait_ge(out_made[b], START + i + 1)
                    Ve.tensor_tensor(x2[b][:].rearrange("p t d -> p (t d)"), bank[3][b][:],
                                     x2[b][:].rearrange("p t d -> p (t d)"), ALU.add).then_inc(x3_ready[b], 1)
                own.restart()

        @block.tensor
        def _(pe):
            mm = nc.tensor.matmul
            pe.wait_ge(const_in, START + CONSTS)
            pe.wait_ge(clear, START + 8)

            def ready(b, i, e):
                for s in (diag_act, diag_pool, diag_dve):
                    pe.wait_ge(s[b], START + DIAGS * i + e + 1)

            with pe.Fori(0, PAIRS) as i:
                for b in range(2):
                    pe.wait_ge(xn_ready[b], START + i + 1)
                    for t in range(TILES):
                        ins = nc.tensor.transpose(bank[0][b][:, bass.ts(t, P)], xn[b][:, t, :], ident[:])
                    ins.then_inc(xnT_made[b], 1)
                for b in range(2):
                    pe.wait_ge(xnT_ready[b], START + i + 1)
                    for t in range(TILES):
                        ins = mm(bank[1][b][:, t * E:t * E + E], xnT[b][:, bass.ts(t, P)], w_rout[:], start=True, stop=True)
                    ins.then_inc(logits_made[b], 1)
                    pe.wait_ge(x3_ready[b], START + i)
                    mm(bank[2][b][:], w_in[:, 0], xnT[b][:], start=True, stop=True).then_inc(proj_made[b], 1)
                    mm(bank[3][b][:], w_in[:, 1], xnT[b][:], start=True, stop=True).then_inc(proj_made[b], 1)
                    mm(bank[0][b][:], w_in[:, 2], xnT[b][:], start=True, stop=True).then_inc(proj_made[b], 1)
                    pe.wait_ge(logits_kept[b], START + i + 1)
                    mm(bank[1][b][:], w_in[:, 3], xnT[b][:], start=True, stop=True).then_inc(proj_made[b], 1)

                def scores(b, h):
                    for u in range(HALF):
                        ins = mm(bank[u // 4][b][:, bass.ts(u % 4, P)], diag[0][b][:, h * HALF + u],
                                 q_sub[b][:, h * HALF + u].rearrange("p s d -> p (s d)"), start=True, stop=True)
                    ins.then_inc(score_made[b], 1)

                def contexts(b, h):
                    for u in range(h * HALF, (h + 1) * HALF):
                        out = bank[2][b][:, bass.ts(u, C)]
                        for s in range(SUB):
                            ins = mm(out, v_sub[b][:, u, P * s:P * s + P], score[b][:, u - h * HALF, s],
                                     start=(s == 0), stop=(s == SUB - 1 and u == 0))
                        if u:
                            ins = mm(out, diag[0][b][:, u], qkv[b][:, 0, u], start=False, stop=True)
                    ins.then_inc(ctx_made[b], 1)

                for b in range(2):
                    ready(b, i, KT)
                    pe.wait_ge(norm_ready[b], START + 2 * (i + 1))
                    scores(b, 0)
                for b in range(2):
                    ready(b, i, K)
                    for u in range(NCH):
                        ins = mm(bank[2][b][:, bass.ts(u, C)], diag[1][b][:, u], kv[b][:, 1, u], start=True, stop=True)
                    ins.then_inc(z_made[b], 1)
                for b in range(2):
                    pe.wait_ge(score_ready[b], START + 3 * i + 2)
                    scores(b, 1)
                for b in range(2):
                    ready(b, i, Z)
                    contexts(b, 0)
                for b in range(2):
                    pe.wait_ge(score_ready[b], START + 3 * (i + 1))
                    contexts(b, 1)
                for b in range(2):
                    pe.wait_ge(ctx_ready[b], START + i + 1)
                    for t in range(TILES):
                        mm(bank[3][b][:, bass.ts(t, P)], ctxT[b][:, bass.ts(t, P)], w_out[:], start=True, stop=False)
                        ins = mm(bank[3][b][:, bass.ts(t, P)], ones[0:1, :], b_out[0:1, :], start=False, stop=True)
                    ins.then_inc(out_made[b], 1)


def phase_finish(nc, dram, keep):
    with ExitStack() as ctx:
        def sb2(name, shape, dt=F32):
            return [ctx.enter_context(nc.sbuf_tensor(f"{name}{b}", shape, dt)) for b in range(2)]

        signals = Signals(nc, ctx)
        sem2 = signals.two

        index = sb2("index2", [P, TILES], U32)
        share = sb2("share2", [P, TILES])
        got = sb2("got2", [P, TILES, D])
        x3 = sb2("x3f", [P, TILES, D])
        index_ready = sem2("fin_index")
        gathered = keep["gathered"][1]
        x_in = sem2("fin_x_in")
        out_ready = sem2("fin_ready")
        out_stored = sem2("fin_stored")
        dve_own = signals.own("dve_own")
        pool_passed = signals.one("pool_passed")
        block = signals.block()

        @block.sync
        def _(sp):
            def rows(name, n):
                return dram[name][bass.ds(n, 1)].rearrange("a (t p) d -> p (a t) d", p=P)

            with sp.Fori(0, PAIRS) as i:
                for b in range(2):
                    sp.wait_ge(out_stored[b], START + 16 * i)
                    sp.dma_start(x3[b][:], rows("x3", 2 * i + b)).then_inc(x_in[b], 16)
                for b in range(2):
                    sp.wait_ge(out_ready[b], START + i + 1)
                    sp.dma_start(rows("out", 2 * i + b), x3[b][:]).then_inc(out_stored[b], 16)
            for b in range(2):
                sp.wait_ge(out_stored[b], START + 16 * PAIRS)

        @block.gpsimd
        def _(pool):
            def wait(signal, value):
                pool.wait_ge(signal, value)
                pool.sem_inc(pool_passed, 1)

            with pool.Fori(0, PAIRS) as i:
                for b in range(2):
                    wait(index_ready[b], START + i + 1)
                    for t in range(TILES):
                        pool.indirect_dma_start(
                            out=got[b][:, t, :], out_offset=None, in_=dram["rows1"][:, :],
                            in_offset=bass.IndirectOffsetOnAxis(ap=index[b][:, t:t + 1], axis=0),
                            bounds_check=G1 * GS - 1, oob_is_err=False).then_inc(gathered[b], 16)

        @block.vector
        def _(dve):
            own = Chain(dve, dve_own)
            V = nc.vector

            def route(b, n, c):
                own.link(V.tensor_copy(share[b][:], keep["prob"][:, bass.ds(n * TILES, TILES), 0]))
                V.tensor_copy(index[b][:], keep["slot"][:, bass.ds(n * TILES, TILES), 2]).then_inc(index_ready[b], 1)

            def add(b, c):
                dve.wait_ge(x_in[b], START + 16 * (c + 1))
                dve.wait_ge(gathered[b], 16 * TILES * (c + 1))
                for t in range(TILES):
                    own.step(V.scalar_tensor_tensor(out=x3[b][:, t], in0=got[b][:, t], scalar=share[b][:, t:t + 1],
                                                    in1=x3[b][:, t], op0=ALU.mult, op1=ALU.add))
                own.wait()
                dve.sem_inc(out_ready[b], 1)

            for b in range(2):
                route(b, b, 0)
            own.restart()
            with dve.Fori(0, PAIRS - 1) as i:
                for b in range(2):
                    add(b, i)
                    route(b, 2 * i + 2 + b, i + 1)
                own.restart()
            for b in range(2):
                add(b, PAIRS - 1)


PHASES = [phase_project, phase_fir, phase_delta, phase_route0, phase_experts0, phase_linear, phase_route1,
          phase_experts1, phase_finish]

def build(nc, dram, phases=99):
    with ExitStack() as ctx:
        keep = {
            "ident": ctx.enter_context(nc.sbuf_tensor("ident", [P, P], F32)),
            "logits": ctx.enter_context(nc.sbuf_tensor("logits", [P, NT * E], F32)),
            "slot": ctx.enter_context(nc.sbuf_tensor("slot", [P, NT, 4], U32)),
            "prob": ctx.enter_context(nc.sbuf_tensor("prob", [P, NT, 2], F32)),
            "group": ctx.enter_context(nc.sbuf_tensor("group", [P, G0], I32)),
            "slots_zeroed": ctx.enter_context(nc.semaphore("slots_zeroed")),
            "scattered": [[ctx.enter_context(nc.semaphore(f"scattered{k}_{b}")) for b in range(2)] for k in range(2)],
            "gathered": [[ctx.enter_context(nc.semaphore(f"gathered{k}_{b}")) for b in range(2)] for k in range(2)],
        }
        for k, phase in enumerate(PHASES):
            if k < phases:
                phase(nc, dram, keep)


def layout(np, x):
    f = {k: np.asarray(v) for k, v in x.items()}
    out = {"x": f["L0_attn_hidden_states"]}
    out["w_qkv"] = np.stack([f[f"L0_attn_{n}_proj_w"].T for n in "qkv"], axis=1)
    out["w_mix1"] = f["L0_attn_gmix_w1"].T.reshape(P, 2, P)
    gate = np.zeros((P, 2, P), np.float32)
    beta = np.zeros((P, P), np.float32)
    b_gate = np.zeros((P, 1), np.float32)
    for h in range(H):
        for j in range(4):
            gate[:, :, C * h + j] = f["L0_attn_gmix_w2"][j * H + h].reshape(2, P).T
            b_gate[C * h + j, 0] = f["L0_attn_gmix_b2"][j * H + h]
        beta[:, C * h + 4] = f["L0_attn_b_proj_w"][h]
    out["w_gate"], out["w_beta"], out["b_gate"] = gate, beta, b_gate
    out["w_rout0"] = f["L0_ffn_w_g"].T
    out["taps"] = np.stack([f[f"L0_attn_{n}_conv_w"] for n in "qkv"], axis=1)
    out["b_mix1"] = f["L0_attn_gmix_b1"].reshape(2, P).T
    toep = np.zeros((H, C, C, 2, 2 * C), np.float32)
    for p in range(C):
        toep[:, p, :, 0, p:p + KS] = f["L0_attn_fir_short_w"][:, :, ::-1]
        toep[:, p, :, 1, p:p + KL] = f["L0_attn_fir_long_w"][:, :, ::-1]
    out["toep"] = toep.reshape(P, C, 2, 2 * C)
    out["alpha"] = np.repeat(f["L0_attn_alpha"], C, axis=0)
    out["o_norm"] = np.tile(f["L0_attn_o_norm_w"], H).reshape(P, 1)
    out["w_o0"] = f["L0_attn_o_proj_w"].T
    out["w_fc0"], out["w_down0"] = f["L0_ffn_c_fc"], f["L0_ffn_c_proj"]
    out["w_q1"] = f["L1_attn_Wqk"][:, 0:P]
    out["w_k1"] = f["L1_attn_Wqk"][:, P:]
    out["w_v1"] = f["L1_attn_Wv"]
    out["b_qkv1"] = np.stack([f["L1_attn_bqk"][0:P], f["L1_attn_bqk"][P:], f["L1_attn_bv"]], axis=1)
    out["w_n1"] = np.repeat(f["L1_attn_Wn"], P // HEADS1, axis=1)
    out["b_n1"] = np.repeat(f["L1_attn_bn"], P // HEADS1).reshape(P, 1)
    out["w_o1"] = f["L1_attn_Wo"]
    out["b_o1"] = f["L1_attn_bo"].reshape(1, P)
    out["w_rout1"] = f["L1_ffn_gate_w"].T
    out["w_fc1"], out["w_down1"] = f["L1_ffn_w1"], f["L1_ffn_w2"]
    out["b_fc1"] = f["L1_ffn_b1"].reshape(E, FT, P).transpose(0, 2, 1)
    out["b_down1"] = f["L1_ffn_b2"].reshape(E, 1, P)
    p, j = np.arange(P)[:, None], np.arange(C)[None, :]
    t = p % C
    out["ident"] = np.eye(P, dtype=np.float32)
    out["tri"] = (p <= np.arange(P)[None, :]).astype(np.float32)
    out["masks"] = np.stack([-(j > t).astype(np.float32), (j >= t).astype(np.float32),
                             (j == t).astype(np.float32),
                             (j // (C // SUB) == t // (C // SUB)).astype(np.float32)], axis=1)
    out["subs"] = (t // (C // SUB) == np.arange(SUB)[None, :]).astype(np.float32)
    out["expert"] = np.tile(np.arange(E, dtype=np.float32), (P, 1))
    out["group0"] = np.tile((np.arange(G0) * GS // CAP0).astype(np.int32), (P, 1))
    out["starts"] = np.tile(np.arange(G0, dtype=np.float32) * GS, (P, 1))
    return {k: np.ascontiguousarray(v) for k, v in out.items()}


SCRATCH = {"xn": [SEQS, LEN, D], "head": [SEQS, P, 4, LEN], "fir": [SEQS, P, 2, LEN], "x1": [SEQS, LEN, D],
           "xn1": [SEQS, LEN, D], "x2": [SEQS, LEN, D], "x3": [SEQS, LEN, D],
           "slots0": [G0 * GS, D], "rows0": [G0 * GS, D], "slots1": [G1 * GS, D], "rows1": [G1 * GS, D]}


def kernel(**inputs):
    import numpy as np
    import concourse.bacc as bacc
    from concourse.bass_utils import run_bass_kernel_spmd

    nc = bacc.Bacc("TRN2", target_bir_lowering=False, num_devices=1)
    arrays, dram = {}, {}
    for name, a in layout(np, inputs).items():
        arrays[f"in_{name}"] = a
        dram[name] = nc.dram_tensor(f"in_{name}", a.shape, mybir.dt.from_np(a.dtype), kind="ExternalInput").ap()
    for name, shape in SCRATCH.items():
        dram[name] = nc.dram_tensor(f"scratch_{name}", shape, F32, kind="Internal").ap()
    dram["out"] = nc.dram_tensor("out_dram", [SEQS, LEN, D], F32, kind="ExternalOutput").ap()
    build(nc, dram)
    r = run_bass_kernel_spmd(nc, [arrays], core_ids=[0])
    return r.results[0]["out_dram"]
```

```python
from contextlib import ExitStack

import concourse.bass as bass
from concourse import mybir

ALU = mybir.AluOpType
ACT = mybir.ActivationFunctionType
F32 = mybir.dt.float32
I32 = mybir.dt.int32
U32 = mybir.dt.uint32
AX_X = mybir.AxisListType.X

P = 128
SEQS, LEN, D = 16, 512, 128
TILES = LEN // P
NT = SEQS * TILES
NTOK = SEQS * LEN
PAIRS = SEQS // 2
C = 32
NCH = LEN // C
H = 4
QD = 4
HEADS1 = 16
SUB = 4
E = 8
FF = 512
FT = FF // P
GS = 512
CAP0 = 2560
G0 = E * CAP0 // GS
G1 = NTOK // GS + E
TAPS = 4
KS, KL = 7, 31
EPS = 1e-5
START = 1


class Chain:

    def __init__(self, eng, sem):
        self.eng, self.sem, self.count = eng, sem, 0

    def step(self, ins):
        self.count += 1
        ins.then_inc(self.sem, 1)
        return self.count

    def wait(self, count=None):
        self.eng.wait_ge(self.sem, self.count if count is None else count)

    def link(self, ins):
        self.step(ins)
        self.wait()

    def restart(self):
        self.wait()
        self.eng.sem_clear(self.sem)
        self.count = 0


class Signals:

    def __init__(self, nc, ctx):
        self.nc, self.ctx, self.all, self.chains = nc, ctx, [], []

    def one(self, name):
        self.all.append(self.ctx.enter_context(self.nc.semaphore(name)))
        return self.all[-1]

    def own(self, name):
        self.chains.append(self.one(name))
        return self.chains[-1]

    def two(self, name):
        return [self.one(f"{name}_{b}") for b in range(2)]

    def clear(self):
        nums = sorted(s.num for s in self.all)
        starts = [n for n in nums if n - 1 not in nums]
        with self.nc.Block() as block:
            @block.sync
            def _(sp):
                for start in starts:
                    stop = start
                    while stop in nums:
                        stop += 1
                    sp.sem_clear(range(start, stop))

    def block(self):
        rest = [s for s in self.all if s not in self.chains]
        with self.nc.Block() as block:
            @block.sync
            def _(sp):
                for s in rest[0::2]:
                    sp.sem_inc(s, START)

            @block.tensor
            def _(pe):
                for s in rest[1::2]:
                    pe.sem_inc(s, START)

        self.ctx.callback(self.clear)
        return self.ctx.enter_context(self.nc.Block())


def quad(q):
    return slice(C * q, C * q + C)


def phase_project(nc, dram, keep):
    with ExitStack() as ctx:
        def sb(name, shape, dt=F32):
            return ctx.enter_context(nc.sbuf_tensor(name, shape, dt))

        def ps(name, shape, dt=F32):
            return ctx.enter_context(nc.psum_tensor(name, shape, dt))

        signals = Signals(nc, ctx)
        sem, sem2 = signals.one, signals.two

        ident, logits0 = keep["ident"], keep["logits"]
        w_qkv = sb("w_qkv", [P, 3, D])
        w_mix1 = sb("w_mix1", [P, 2, P])
        w_gate = sb("w_gate", [P, 2, P])
        w_beta = sb("w_beta", [P, P])
        w_rout = sb("w_rout", [P, E])
        taps = sb("taps", [P, 3, TAPS])
        b_mix1 = sb("b_mix1", [P, 2])
        b_gate = sb("b_gate", [P, 1])
        power = sb("power", [P, TILES])
        zeros = sb("zeros", [P, 2048])
        xt = [sb(f"xt{b}", [P, TILES, D]) for b in range(2)]
        stats = [sb(f"stats{b}", [P, TILES, 6]) for b in range(2)]
        moments = [sb(f"moments{b}", [P, TILES, 2]) for b in range(2)]
        var = [sb(f"var{b}", [P, TILES]) for b in range(2)]
        rstd = [sb(f"rstd{b}", [P, TILES]) for b in range(2)]
        xn = [sb(f"xn{b}", [P, TILES, D]) for b in range(2)]
        xnT = [sb(f"xnT{b}", [P, LEN]) for b in range(2)]
        conv = [sb(f"conv{b}", [P, 3, LEN]) for b in range(2)]
        chan = [sb(f"chan{b}", [P, 4, LEN]) for b in range(2)]
        hid = [sb(f"hid{b}", [P, 2, LEN]) for b in range(2)]
        head = [sb(f"head{b}", [P, 4, LEN]) for b in range(2)]

        psT = ps("psT", [P, LEN])
        psR = ps("psR", [P, TILES, E])
        psQKV = ps("psQKV", [P, 3, LEN])
        psH = ps("psH", [P, 2, LEN])
        psG = ps("psG", [P, LEN])

        weights_in = sem("weights_in")
        zeroed = sem("zeroed")
        slots_zeroed = keep["slots_zeroed"]
        power_set = sem("power_set")
        x_in = sem2("x_in")
        ln_stats = sem2("ln_stats")
        rstd_ready = sem2("rstd_ready")
        xn_ready = sem2("xn_ready")
        xn_stored = sem2("xn_stored")
        xnT_made = sem2("xnT_made")
        xnT_ready = sem2("xnT_ready")
        logits_made = sem2("logits_made")
        logits_kept = sem2("logits_kept")
        proj_made = sem2("proj_made")
        mix1_made = sem2("mix1_made")
        tap0_ready = sem2("tap0_ready")
        conv_ready = sem2("conv_ready")
        act_ready = sem2("act_ready")
        hid_ready = sem2("hid_ready")
        gate_made = sem2("gate_made")
        gate_ready = sem2("gate_ready")
        head_ready = sem2("head_ready")
        head_stored = sem2("head_stored")
        dve_own = signals.own("dve_own")
        pool_own = signals.own("pool_own")

        W_IN = 9 * 16
        pool_passed = signals.one("pool_passed")
        block = signals.block()

        @block.sync
        def _(sp):
            for dst, src in ((w_qkv, "w_qkv"), (w_mix1, "w_mix1"), (w_gate, "w_gate"), (w_beta, "w_beta"),
                             (w_rout, "w_rout0"), (taps, "taps"), (b_mix1, "b_mix1"), (b_gate, "b_gate"),
                             (ident, "ident")):
                sp.dma_start(dst[:], dram[src]).then_inc(weights_in, 16)

            def load(b, n):
                sp.dma_start(xt[b][:], dram["x"][bass.ds(n, 1)].rearrange("a (t p) d -> p (a t) d", p=P)
                             ).then_inc(x_in[b], 16)

            def store_xn(b, i):
                sp.wait_ge(xn_ready[b], START + i + 1)
                sp.dma_start(dram["xn"][bass.ds(2 * i + b, 1)].rearrange("a (t p) d -> p (a t) d", p=P),
                             xn[b][:]).then_inc(xn_stored[b], 16)

            def store_head(b, i):
                sp.wait_ge(head_ready[b], START + i + 1)
                sp.dma_start(dram["head"][bass.ds(2 * i + b, 1)].rearrange("a p k t -> p (a k) t"),
                             head[b][:]).then_inc(head_stored[b], 16)

            for b in range(2):
                load(b, b)
            with sp.Fori(0, PAIRS - 1) as i:
                for b in range(2):
                    store_xn(b, i)
                    load(b, 2 * i + 2 + b)
                for b in range(2):
                    store_head(b, i)
            for b in range(2):
                store_xn(b, PAIRS - 1)
            for b in range(2):
                store_head(b, PAIRS - 1)
            for b in range(2):
                sp.wait_ge(xn_stored[b], START + 16 * PAIRS)
                sp.wait_ge(head_stored[b], START + 16 * PAIRS)

        @block.gpsimd
        def _(pool):
            def wait(signal, value):
                pool.wait_ge(signal, value)
                pool.sem_inc(pool_passed, 1)

            own = Chain(pool, pool_own)
            nc.gpsimd.memset(power[:], -0.5).then_inc(power_set, 1)
            nc.gpsimd.memset(zeros[:], 0.0).then_inc(zeroed, 1)
            pool.wait_ge(power_set, START + 1)
            pool.wait_ge(zeroed, START + 1)
            for name, rows in (("slots0", G0 * GS), ("slots1", G1 * GS)):
                step = 2048 // D * P
                flat = dram[name].rearrange("(g p r) d -> g p (r d)", p=P, r=2048 // D)
                for g in range(rows // step):
                    pool.dma_start(flat[g], zeros[:]).then_inc(slots_zeroed, 16)
            with pool.Fori(0, PAIRS) as i:
                for b in range(2):
                    wait(ln_stats[b], START + i + 1)
                    own.link(nc.gpsimd.tensor_scalar(var[b][:], moments[b][:, :, 1], EPS, None, ALU.add))
                    nc.gpsimd.tensor_tensor(rstd[b][:], var[b][:], power[:], ALU.pow).then_inc(rstd_ready[b], 1)
                own.restart()
            pool.wait_ge(slots_zeroed, 16 * ((G0 + G1) * GS // (2048 // D * P)))

        @block.vector
        def _(dve):
            own = Chain(dve, dve_own)
            with dve.Fori(0, PAIRS) as i:
                for b in range(2):
                    dve.wait_ge(x_in[b], START + 16 * (i + 1))
                    for t in range(TILES):
                        own.step(nc.vector.bn_stats(stats[b][:, t, :], xt[b][:, t, :]))
                    own.wait()
                    for t in range(TILES):
                        ins = nc.vector.bn_aggr(moments[b][:, t, :], stats[b][:, t, :])
                    ins.then_inc(ln_stats[b], 1)
                for b in range(2):
                    dve.wait_ge(rstd_ready[b], START + i + 1)
                    dve.wait_ge(xn_stored[b], START + 16 * i)
                    dve.wait_ge(xnT_made[b], START + i)
                    for t in range(TILES):
                        ins = nc.vector.tensor_scalar(xn[b][:, t, :], xt[b][:, t, :], moments[b][:, t, 0:1],
                                                      rstd[b][:, t:t + 1], ALU.subtract, ALU.mult)
                    ins.then_inc(xn_ready[b], 1)
                for b in range(2):
                    dve.wait_ge(logits_made[b], START + i + 1)
                    nc.vector.tensor_copy(logits0[:, bass.ds((2 * i + b) * TILES * E, TILES * E)],
                                          psR[:].rearrange("p t e -> p (t e)")).then_inc(logits_kept[b], 1)
                    dve.wait_ge(tap0_ready[b], START + i + 1)
                    if b == 0:
                        dve.wait_ge(weights_in, START + W_IN)
                    last = [None] * 3
                    for lag in range(1, TAPS):
                        for j in range(3):
                            if last[j]:
                                own.wait(last[j])
                            last[j] = own.step(nc.vector.scalar_tensor_tensor(
                                out=conv[b][:, j, lag:LEN], in0=psQKV[:, j, 0:LEN - lag],
                                scalar=taps[:, j, TAPS - 1 - lag:TAPS - lag], in1=conv[b][:, j, lag:LEN],
                                op0=ALU.mult, op1=ALU.add))
                    own.wait()
                    dve.sem_inc(conv_ready[b], 1)
                for b in range(2):
                    dve.wait_ge(head_stored[b], START + 16 * i)
                    dve.wait_ge(act_ready[b], START + i + 1)
                    for j in range(3):
                        nc.vector.transpose(head[b][:, j, :], chan[b][:, j, :])
                    dve.wait_ge(gate_ready[b], START + i + 1)
                    nc.vector.transpose(head[b][:, 3, :], chan[b][:, 3, :]).then_inc(head_ready[b], 1)
                own.restart()

        @block.scalar
        def _(act):
            with act.Fori(0, PAIRS) as i:
                for b in range(2):
                    act.wait_ge(xnT_made[b], START + i + 1)
                    act.wait_ge(gate_made[b], START + i)
                    nc.scalar.copy(xnT[b][:], psT[:]).then_inc(xnT_ready[b], 1)
                for b in range(2):
                    act.wait_ge(proj_made[b], START + i + 1)
                    act.wait_ge(act_ready[b], START + i)
                    if b == 0:
                        act.wait_ge(weights_in, START + W_IN)
                    for j in range(3):
                        ins = nc.scalar.activation(conv[b][:, j, :], psQKV[:, j, :], ACT.Copy,
                                                   scale=taps[:, j, TAPS - 1:TAPS])
                    ins.then_inc(tap0_ready[b], 1)
                    act.wait_ge(mix1_made[b], START + i + 1)
                    for k in range(2):
                        ins = nc.scalar.activation(hid[b][:, k, :], psH[:, k, :], ACT.Gelu, bias=b_mix1[:, k:k + 1])
                    ins.then_inc(hid_ready[b], 1)
                for b in range(2):
                    act.wait_ge(gate_made[b], START + i + 1)
                    act.wait_ge(head_ready[b], START + i)
                    nc.scalar.activation(chan[b][:, 3, :], psG[:], ACT.Identity, bias=b_gate[:, 0:1]
                                         ).then_inc(gate_ready[b], 1)
                for b in range(2):
                    act.wait_ge(conv_ready[b], START + i + 1)
                    nc.scalar.activation(chan[b][:, 0:3, :], conv[b][:], ACT.Silu).then_inc(act_ready[b], 1)

        @block.tensor
        def _(pe):
            pe.wait_ge(weights_in, START + W_IN)
            with pe.Fori(0, PAIRS) as i:
                for b in range(2):
                    o = 1 - b
                    before = i + b
                    pe.wait_ge(xn_ready[b], START + i + 1)
                    pe.wait_ge(xnT_ready[o], START + before)
                    for t in range(TILES):
                        ins = nc.tensor.transpose(psT[:, bass.ts(t, P)], xn[b][:, t, :], ident[:])
                    ins.then_inc(xnT_made[b], 1)
                for b in range(2):
                    o = 1 - b
                    before = i + b
                    pe.wait_ge(xnT_ready[b], START + i + 1)
                    pe.wait_ge(logits_kept[o], START + before)
                    for t in range(TILES):
                        ins = nc.tensor.matmul(psR[:, t, :], xnT[b][:, bass.ts(t, P)], w_rout[:], start=True, stop=True)
                    ins.then_inc(logits_made[b], 1)
                    pe.wait_ge(conv_ready[o], START + before)
                    for j in range(3):
                        ins = nc.tensor.matmul(psQKV[:, j, :], w_qkv[:, j, :], xnT[b][:], start=True, stop=True)
                    ins.then_inc(proj_made[b], 1)
                    pe.wait_ge(hid_ready[o], START + before)
                    for k in range(2):
                        ins = nc.tensor.matmul(psH[:, k, :], w_mix1[:, k, :], xnT[b][:], start=True, stop=True)
                    ins.then_inc(mix1_made[b], 1)
                for b in range(2):
                    o = 1 - b
                    before = i + b
                    pe.wait_ge(hid_ready[b], START + i + 1)
                    pe.wait_ge(gate_ready[o], START + before)
                    nc.tensor.matmul(psG[:], w_beta[:], xnT[b][:], start=True, stop=False)
                    nc.tensor.matmul(psG[:], w_gate[:, 0, :], hid[b][:, 0, :], start=False, stop=False)
                    nc.tensor.matmul(psG[:], w_gate[:, 1, :], hid[b][:, 1, :], start=False, stop=True
                                     ).then_inc(gate_made[b], 1)


def phase_fir(nc, dram, keep):
    with ExitStack() as ctx:
        def sb(name, shape, dt=F32):
            return ctx.enter_context(nc.sbuf_tensor(name, shape, dt))

        signals = Signals(nc, ctx)
        sem, sem2 = signals.one, signals.two

        v_all = sb("v_all", [P, SEQS, NCH, C])
        toep = sb("toep", [P, C, 2, 2 * C])
        diag = [sb(f"diag{b}", [P, 2, 2, P]) for b in range(2)]
        fir = sb("fir", [P, SEQS, 2, NCH, C])
        psF = [ctx.enter_context(nc.psum_tensor(f"psF{b}", [P, 2, 2, SEQS, NCH], F32)) for b in range(2)]

        inputs_in = sem("fir_inputs_in")
        diag_clear = sem("diag_clear")
        diag_dve = sem2("diag_dve")
        diag_pool = sem2("diag_pool")
        diag_act = sem2("diag_act")
        fir_made = sem2("fir_made")
        fir_kept = sem2("fir_kept")
        fir_act = sem2("fir_act")
        fir_stored = sem("fir_stored")
        pool_passed = signals.one("pool_passed")
        block = signals.block()

        @block.sync
        def _(sp):
            sp.dma_start(toep[:], dram["toep"]).then_inc(inputs_in, 16)
            for n in range(SEQS):
                sp.dma_start(v_all[:, n].rearrange("p c d -> p (c d)"), dram["head"][n, :, 2, :]).then_inc(inputs_in, 16)
            for b in range(2):
                sp.wait_ge(fir_kept[b], START + C // 2)
                sp.wait_ge(fir_act[b], START + C // 2)
            for n in range(SEQS):
                sp.dma_start(dram["fir"][n], fir[:, n].rearrange("p f c d -> p f (c d)")).then_inc(fir_stored, 16)
            sp.wait_ge(fir_stored, START + 16 * SEQS)

        IN = 16 * (1 + SEQS)

        def blocks_of(copy, qs, b, d):
            for q in qs:
                ins = copy(diag[b][quad(q), :, :, quad(q)],
                           toep[quad(q), bass.ds(d, 1)].rearrange("p a f (k m) -> p (a f) k m", m=C))
            return ins

        @block.gpsimd
        def _(pool):
            def wait(signal, value):
                pool.wait_ge(signal, value)
                pool.sem_inc(pool_passed, 1)

            for b in range(2):
                nc.gpsimd.memset(diag[b][:], 0.0).then_inc(diag_clear, 1)
            pool.wait_ge(diag_clear, START + 2)
            pool.wait_ge(inputs_in, START + IN)
            with pool.Fori(0, C // 2) as i:
                for b in range(2):
                    wait(fir_made[b], START + i)
                    blocks_of(nc.gpsimd.tensor_copy, (0,), b, 2 * i + b).then_inc(diag_pool[b], 1)

        @block.scalar
        def _(act):
            act.wait_ge(diag_clear, START + 2)
            act.wait_ge(inputs_in, START + IN)
            with act.Fori(0, C // 2) as i:
                for b in range(2):
                    act.wait_ge(fir_made[b], START + i)
                    blocks_of(nc.scalar.copy, (1,), b, 2 * i + b).then_inc(diag_act[b], 1)
                for b in range(2):
                    act.wait_ge(fir_made[b], START + i + 1)
                    nc.scalar.copy(fir[:, :, 1, :, bass.ds(2 * i + b, 1)].rearrange("p s c a -> p s (c a)"),
                                   psF[b][:, 1, 0]).then_inc(fir_act[b], 1)

        @block.vector
        def _(dve):
            dve.wait_ge(diag_clear, START + 2)
            dve.wait_ge(inputs_in, START + IN)
            with dve.Fori(0, C // 2) as i:
                for b in range(2):
                    dve.wait_ge(fir_made[b], START + i)
                    blocks_of(nc.vector.tensor_copy, (2, 3), b, 2 * i + b).then_inc(diag_dve[b], 1)
                for b in range(2):
                    dve.wait_ge(fir_made[b], START + i + 1)
                    nc.vector.tensor_copy(fir[:, :, 0, :, bass.ds(2 * i + b, 1)].rearrange("p s c a -> p s (c a)"),
                                          psF[b][:, 0, 0]).then_inc(fir_kept[b], 1)

        @block.tensor
        def _(pe):
            pe.wait_ge(inputs_in, START + IN)
            with pe.Fori(0, C // 2) as i:
                for b in range(2):
                    d = 2 * i + b
                    for ready in (diag_pool, diag_act, diag_dve):
                        pe.wait_ge(ready[b], START + i + 1)
                    pe.wait_ge(fir_kept[b], START + i)
                    pe.wait_ge(fir_act[b], START + i)
                    for f in range(2):
                        v_d = v_all[:, :, :, bass.ds(d, 1)].rearrange("p s c a -> p s (c a)")
                        v_before = v_all[:, :, 0:NCH - 1, bass.ds(d, 1)].rearrange("p s c a -> p s (c a)")
                        nc.tensor.matmul(psF[b][:, f, 0], diag[b][:, f, 0, :], v_d, start=True, stop=False)
                        ins = nc.tensor.matmul(psF[b][:, f, 0, :, 1:NCH], diag[b][:, f, 1, :], v_before,
                                               start=False, stop=True)
                    ins.then_inc(fir_made[b], 1)


def phase_delta(nc, dram, keep):
    with ExitStack() as ctx:
        def sb(name, shape, dt=F32):
            return ctx.enter_context(nc.sbuf_tensor(name, shape, dt))

        def sb2(name, shape, dt=F32):
            return [sb(f"{name}{b}", shape, dt) for b in range(2)]

        def ps2(name, shape):
            return [ctx.enter_context(nc.psum_tensor(f"{name}{b}", shape, F32)) for b in range(2)]

        signals = Signals(nc, ctx)
        sem, sem2 = signals.one, signals.two

        masks = sb("masks", [P, 4, C])
        w_o = sb("w_o", [P, D])
        w_os = sb("w_os", [P, D])
        o_norm = sb("o_norm", [P, 1])
        alpha = sb("alpha", [P, 1])
        alpha3 = sb("alpha3", [P, 1])
        expo = sb("expo", [P, 2, 4 * NCH])
        head = sb2("head_t", [P, 4, NCH, C])
        STATE, SHORT, LONG, DELTA, VALUE = range(5)
        branch = sb2("branch", [P, 5, NCH, C])
        gates = sb2("gates", [P, NCH, 4])
        squares = sb2("squares", [P, 4, NCH, C])
        norm2 = sb2("norm2", [P, 2 * NCH])
        rnorm = sb2("rnorm", [P, 2, NCH])
        ebeta = sb2("ebeta", [P, NCH])
        beta = sb2("beta", [P, NCH])
        qn = sb2("qn", [P, NCH, C])
        ka = sb2("ka", [P, NCH, 2, C])
        vk = sb2("vk", [P, NCH, 2, C])
        cm = sb2("cm", [P, NCH, 3, C])
        rows = [sb2(f"arows{k}", [P, NCH, 2, C]) for k in range(2)]
        power = sb2("apower", [P, NCH, C])
        uw = sb2("uw", [P, NCH, 2, C])
        imq = sb2("imq", [P, NCH, 2, C])
        cen = sb2("cen", [P, 4, NCH, C])
        sums = sb2("sums", [P, 4 * NCH])
        maxs = sb2("maxs", [P, 4 * NCH])
        dev2 = sb2("dev2", [P, 4 * NCH])
        std = sb2("std", [P, 4 * NCH])
        logit = sb2("logit", [P, 4, NCH])
        lmax = sb2("lmax", [P, NCH])
        prob = sb2("bprob", [P, 4, NCH])
        psum_ = sb2("probsum", [P, NCH])
        mix = sb2("mix", [P, NCH, C])
        mix2 = sb2("mix2", [P, NCH])
        mixr = sb2("mixr", [P, NCH])
        mixT = [qn[b][:].rearrange("p c d -> p (c d)") for b in range(2)]
        xres = sb2("xres", [P, TILES, D])
        x1 = xres

        psA = ps2("psA", [P, NCH, 2, C])
        psS = ps2("psS", [P, 2, LEN // (2 * C), 2, C])

        const_in = sem("const_in")
        set_up = sem("set_up")
        clear = sem("clear")
        head_in = sem2("head_in")
        fir_in = sem2("fir_in")
        x_in = sem2("xres_in")
        squared = sem2("squared")
        norm2_ready = sem2("norm2_ready")
        rnorm_ready = sem2("rnorm_ready")
        ebeta_ready = sem2("ebeta_ready")
        prepared = sem2("prepared")
        made = sem2("made")
        kept = sem2("kept")
        state_made = sem2("state_made")
        state_ready = sem2("state_ready")
        mix_copied = sem2("mix_copied")
        cen_ready = sem2("cen_ready")
        cen_squared = sem2("cen_squared")
        dev2_ready = sem2("dev2_ready")
        std_ready = sem2("std_ready")
        logit_ready = sem2("logit_ready")
        exp_ready = sem2("exp_ready")
        mix_ready = sem2("mix_ready")
        mix_squared = sem2("mix_squared")
        mix2_ready = sem2("mix2_ready")
        mixr_ready = sem2("mixr_ready")
        mixT_ready = sem2("mixT_ready")
        out_made = sem2("out_made")
        x1_ready = sem2("x1_ready")
        x1_stored = sem2("x1_stored")
        dve_own = signals.own("dve_own")
        pool_own = signals.own("pool_own")
        pool_passed = signals.one("pool_passed")
        pe_passed = signals.one("pe_passed")
        block = signals.block()

        GRAM, SQ0, SQ1, SQ2, SQ3, SQ4, UW, MW = range(8)
        STEPS = 8
        LAST = PAIRS - 1

        @block.sync
        def _(sp):
            for dst, name in ((masks, "masks"), (w_o, "w_o0"), (o_norm, "o_norm"), (alpha, "alpha")):
                sp.dma_start(dst[:], dram[name]).then_inc(const_in, 16)

            def load_head(i):
                for b in range(2):
                    if not isinstance(i, int) or i:
                        sp.wait_ge(mix_copied[b], START + 2 * i)
                    sp.dma_start(head[b][:].rearrange("p k c d -> p k (c d)"), dram["head"][
                        bass.ds(2 * i + b, 1)].rearrange("a p k t -> p (a k) t")).then_inc(head_in[b], 16)

            def load_branches(i):
                for b in range(2):
                    sp.wait_ge(mix_ready[b], START + i)
                    sp.dma_start(branch[b][:, SHORT:LONG + 1].rearrange("p k c d -> p k (c d)"), dram["fir"][
                        bass.ds(2 * i + b, 1)].rearrange("a p k t -> p (a k) t")).then_inc(fir_in[b], 16)

            def load_x(i):
                for b in range(2):
                    sp.wait_ge(x1_stored[b], START + 16 * i)
                    sp.dma_start(xres[b][:], dram["x"][bass.ds(2 * i + b, 1)].rearrange(
                        "a (t p) d -> p (a t) d", p=P)).then_inc(x_in[b], 16)

            def store(i):
                for b in range(2):
                    sp.wait_ge(x1_ready[b], START + i + 1)
                    sp.dma_start(dram["x1"][bass.ds(2 * i + b, 1)].rearrange("a (t p) d -> p (a t) d", p=P), x1[b][:]
                                 ).then_inc(x1_stored[b], 16)

            load_head(0)
            load_branches(0)
            load_x(0)
            load_head(1)
            with sp.Fori(1, LAST) as i:
                load_branches(i)
                load_head(i + 1)
                store(i - 1)
                load_x(i)
            load_branches(LAST)
            store(LAST - 1)
            load_x(LAST)
            store(LAST)
            for b in range(2):
                sp.wait_ge(x1_stored[b], START + 16 * PAIRS)

        @block.gpsimd
        def _(pool):
            def wait(signal, value):
                pool.wait_ge(signal, value)
                pool.sem_inc(pool_passed, 1)

            own = Chain(pool, pool_own)
            nc.gpsimd.memset(expo[:, 0], -0.5).then_inc(clear, 1)
            nc.gpsimd.memset(expo[:, 1], 0.5).then_inc(clear, 1)
            pool.wait_ge(clear, START + 2)

            def key_norms(i):
                for b in range(2):
                    wait(norm2_ready[b], START + i + 1)
                    own.link(nc.gpsimd.tensor_tensor(rnorm[b][:].rearrange("p k c -> p (k c)"), norm2[b][:],
                                                     expo[:, 0, 0:2 * NCH], ALU.pow))
                    pool.sem_inc(rnorm_ready[b], 1)

            def mix_roots(i):
                for b in range(2):
                    wait(dev2_ready[b], START + i + 1)
                    own.link(nc.gpsimd.tensor_tensor(std[b][:], dev2[b][:], expo[:, 1], ALU.pow))
                    pool.sem_inc(std_ready[b], 1)
                for b in range(2):
                    wait(mix2_ready[b], START + i + 1)
                    own.link(nc.gpsimd.tensor_tensor(mixr[b][:], mix2[b][:], expo[:, 0, 0:NCH], ALU.pow))
                    pool.sem_inc(mixr_ready[b], 1)

            key_norms(0)
            key_norms(1)
            own.restart()
            with pool.Fori(1, LAST) as i:
                mix_roots(i - 1)
                key_norms(i + 1)
                own.restart()
            mix_roots(LAST - 1)
            mix_roots(LAST)
            own.restart()

        @block.scalar
        def _(act):
            def head_squares(i):
                for b in range(2):
                    act.wait_ge(head_in[b], START + 16 * (i + 1))
                    if not isinstance(i, int) or i:
                        act.wait_ge(mix2_ready[b], START + (i - 1))
                    nc.scalar.activation(squares[b][:, 0:2], head[b][:, 0:2], ACT.Square).then_inc(squared[b], 1)
                    nc.scalar.activation(ebeta[b][:], head[b][:, 3, :, 4], ACT.Exp, scale=-1.0
                                         ).then_inc(ebeta_ready[b], 1)

            def mix_begin(i):
                for b in range(2):
                    act.wait_ge(cen_ready[b], START + i + 1)
                    nc.scalar.activation(squares[b][:], cen[b][:], ACT.Square).then_inc(cen_squared[b], 1)
                for b in range(2):
                    act.wait_ge(logit_ready[b], START + i + 1)
                    nc.scalar.activation(prob[b][:], logit[b][:], ACT.Exp).then_inc(exp_ready[b], 1)

            def mix_squares(i, b):
                act.wait_ge(mix_ready[b], START + i + 1)
                nc.scalar.activation(squares[b][:, 0], mix[b][:], ACT.Square).then_inc(mix_squared[b], 1)

            def keep_inputs(i, b):
                act.wait_ge(prepared[b], START + i + 1)
                nc.scalar.copy(branch[b][:, VALUE], head[b][:, 2]).then_inc(mix_copied[b], 1)
                nc.scalar.copy(gates[b][:], head[b][:, 3, :, 0:4]).then_inc(mix_copied[b], 1)

            def keep_uw(i, b):
                act.wait_ge(made[b], START + STEPS * i + UW + 1)
                nc.scalar.copy(uw[b][:], psA[b][:]).then_inc(kept[b], 1)

            def turn(i, mixing, more):
                if mixing:
                    mix_begin(i - 1)
                    mix_squares(i - 1, 0)
                keep_inputs(i, 0)
                keep_uw(i, 0)
                keep_uw(i, 1)
                if mixing:
                    mix_squares(i - 1, 1)
                keep_inputs(i, 1)
                if more:
                    head_squares(i + 1)

            head_squares(0)
            turn(0, False, True)
            with act.Fori(1, LAST) as i:
                turn(i, True, True)
            turn(LAST, True, False)
            mix_begin(LAST)
            for b in range(2):
                mix_squares(LAST, b)

        @block.vector
        def _(dve):
            own = Chain(dve, dve_own)
            V = nc.vector

            def mask(k):
                return masks[:, k:k + 1, :].to_broadcast([P, NCH, C])

            def over_channels(ap):
                return ap.unsqueeze(2).to_broadcast([P, NCH, C])

            def norms(i, b):
                dve.wait_ge(squared[b], START + i + 1)
                V.tensor_reduce(norm2[b][:], squares[b][:, 0:2].rearrange("p k c d -> p (k c) d"), AX_X, ALU.add
                                ).then_inc(norm2_ready[b], 1)
                dve.wait_ge(ebeta_ready[b], START + i + 1)
                own.link(V.tensor_scalar(ebeta[b][:], ebeta[b][:], 1.0, None, ALU.add))
                own.link(V.reciprocal(beta[b][:], ebeta[b][:]))

            def prepare(i, b):
                dve.wait_ge(rnorm_ready[b], START + i + 1)
                own.step(V.tensor_tensor(ka[b][:, :, 0], head[b][:, 1], over_channels(rnorm[b][:, 1]), ALU.mult))
                own.step(V.tensor_tensor(vk[b][:, :, 0], head[b][:, 2], over_channels(beta[b][:]), ALU.mult))
                own.link(V.tensor_tensor(qn[b][:], head[b][:, 0], over_channels(rnorm[b][:, 0]), ALU.mult))
                own.link(V.tensor_tensor(vk[b][:, :, 1], ka[b][:, :, 0], over_channels(beta[b][:]), ALU.mult))
                own.step(V.transpose(cm[b][:, :, 0], ka[b][:, :, 0]))
                own.step(V.transpose(cm[b][:, :, 1], vk[b][:, :, 1]))
                own.link(V.transpose(cm[b][:, :, 2], qn[b][:]))
                dve.sem_inc(prepared[b], 1)

            def keep_gram(i, b):
                dve.wait_ge(made[b], START + STEPS * i + GRAM + 1)
                own.step(V.tensor_tensor(rows[0][b][:, :, 0], psA[b][:, :, 0], mask(0), ALU.mult))
                own.link(V.tensor_tensor(ka[b][:, :, 1], psA[b][:, :, 1], mask(1), ALU.mult))
                own.step(V.transpose(power[b][:], rows[0][b][:, :, 0]))
                own.link(V.tensor_tensor(rows[1][b][:, :, 1], rows[0][b][:, :, 0], mask(2), ALU.add))
                dve.sem_inc(kept[b], 1)

            def keep_level(i, b, lv):
                old, new = rows[lv % 2][b], rows[1 - lv % 2][b]
                dve.wait_ge(made[b], START + STEPS * i + SQ0 + lv + 1)
                if lv < 4:
                    own.step(V.transpose(power[b][:], psA[b][:, :, 0]))
                if lv < 3:
                    own.step(V.tensor_copy(new[:, :, 0], psA[b][:, :, 0]))
                if lv > 0:
                    own.step(V.tensor_tensor(new[:, :, 1], old[:, :, 1], psA[b][:, :, 1], ALU.add))
                own.wait()
                dve.sem_inc(kept[b], 1)

            def keep_mw(i, b):
                dve.wait_ge(made[b], START + STEPS * i + MW + 1)
                own.step(V.tensor_tensor(imq[b][:, :, 0], mask(2), psA[b][:, :, 0], ALU.subtract))
                own.link(V.tensor_tensor(imq[b][:, :, 1], cm[b][:, :, 2], psA[b][:, :, 1], ALU.subtract))
                dve.sem_inc(kept[b], 1)

            def keep_state(i, b, u):
                dve.wait_ge(state_made[b], START + NCH * i + u + 1)
                if u < NCH - 1:
                    V.transpose(branch[b][:, STATE:DELTA + 1:DELTA, u], psS[b][:, u % 2, 0]).then_inc(state_ready[b], 1)
                else:
                    V.transpose(branch[b][:, DELTA, u], psS[b][:, u % 2, 0, 1]).then_inc(state_ready[b], 1)

            def centre(i, b):
                dve.wait_ge(state_ready[b], START + NCH * (i + 1))
                dve.wait_ge(fir_in[b], START + 16 * (i + 1))
                dve.wait_ge(mix_copied[b], START + 2 * (i + 1))
                flat = branch[b][:, SHORT:VALUE + 1].rearrange("p k c d -> p (k c) d")
                own.step(V.tensor_reduce(maxs[b][:], flat, AX_X, ALU.max))
                own.link(V.tensor_reduce(sums[b][:], flat, AX_X, ALU.add))
                V.scalar_tensor_tensor(out=cen[b][:].rearrange("p k c d -> p (k c) d"),
                                       in0=sums[b][:].unsqueeze(2).to_broadcast([P, 4 * NCH, C]),
                                       scalar=-1.0 / C, in1=flat, op0=ALU.mult, op1=ALU.add
                                       ).then_inc(cen_ready[b], 1)

            def deviate(i, b):
                dve.wait_ge(cen_squared[b], START + i + 1)
                own.link(V.tensor_reduce(dev2[b][:], squares[b][:].rearrange("p k c d -> p (k c) d"), AX_X, ALU.add))
                V.tensor_scalar(dev2[b][:], dev2[b][:], 1.0 / (C - 1), None, ALU.mult).then_inc(dev2_ready[b], 1)
                own.link(V.scalar_tensor_tensor(out=maxs[b][:], in0=sums[b][:], scalar=1.0 / C, in1=maxs[b][:],
                                                op0=ALU.mult, op1=ALU.add))

            def logits(i, b):
                dve.wait_ge(std_ready[b], START + i + 1)
                own.link(V.tensor_tensor(maxs[b][:], maxs[b][:], std[b][:], ALU.add))
                own.link(V.scalar_tensor_tensor(
                    out=logit[b][:], in0=maxs[b][:].rearrange("p (k c) -> p k c", k=4), scalar=alpha3[:, 0:1],
                    in1=gates[b][:].rearrange("p c k -> p k c"), op0=ALU.mult, op1=ALU.add))
                own.link(V.tensor_reduce(lmax[b][:], logit[b][:].rearrange("p k c -> p c k"), AX_X, ALU.max))
                V.tensor_tensor(logit[b][:], logit[b][:], lmax[b][:].unsqueeze(1).to_broadcast([P, 4, NCH]),
                                ALU.subtract).then_inc(logit_ready[b], 1)

            def weigh(i, b):
                dve.wait_ge(exp_ready[b], START + i + 1)
                own.link(V.tensor_reduce(psum_[b][:], prob[b][:].rearrange("p k c -> p c k"), AX_X, ALU.add))
                own.link(V.reciprocal(lmax[b][:], psum_[b][:]))
                own.link(V.tensor_tensor(prob[b][:], prob[b][:], lmax[b][:].unsqueeze(1).to_broadcast([P, 4, NCH]),
                                         ALU.mult))
                own.link(V.tensor_tensor(cen[b][:].rearrange("p k c d -> p (k c) d"),
                                         branch[b][:, SHORT:VALUE + 1].rearrange("p k c d -> p (k c) d"),
                                         prob[b][:].rearrange("p k c -> p (k c)").unsqueeze(2).to_broadcast(
                                             [P, 4 * NCH, C]), ALU.mult))
                V.tensor_reduce(mix[b][:].rearrange("p c d -> p (c d)"),
                                cen[b][:].rearrange("p k c d -> p (c d) k"), AX_X, ALU.add
                                ).then_inc(mix_ready[b], 1)

            def mean_square(i, b):
                dve.wait_ge(mix_squared[b], START + i + 1)
                own.link(V.tensor_reduce(mix2[b][:], squares[b][:, 0], AX_X, ALU.add))
                V.tensor_scalar(mix2[b][:], mix2[b][:], 1.0 / C, EPS, ALU.mult, ALU.add).then_inc(mix2_ready[b], 1)

            def normalise(i, b):
                dve.wait_ge(mixr_ready[b], START + i + 1)
                own.link(V.tensor_tensor(mix[b][:], mix[b][:], over_channels(mixr[b][:]), ALU.mult))
                V.transpose(mixT[b], mix[b][:].rearrange("p c d -> p (c d)")).then_inc(mixT_ready[b], 1)

            def add_x(i, b):
                dve.wait_ge(out_made[b], START + i + 1)
                dve.wait_ge(x_in[b], START + 16 * (i + 1))
                V.tensor_tensor(x1[b][:].rearrange("p t d -> p (t d)"), psA[b][:, 0:NCH // 2].rearrange(
                    "p c k d -> p (c k d)"), xres[b][:].rearrange("p t d -> p (t d)"), ALU.add
                    ).then_inc(x1_ready[b], 1)

            def turn(i, mixing, more):
                for b in range(2):
                    prepare(i, b)
                for b in range(2):
                    keep_gram(i, b)
                if mixing:
                    centre(i - 1, 0)
                for lv in range(5):
                    for b in range(2):
                        keep_level(i, b, lv)
                    if mixing and lv == 0:
                        centre(i - 1, 1)
                    if mixing and lv == 1:
                        deviate(i - 1, 0)
                        deviate(i - 1, 1)
                    if mixing and lv == 3:
                        logits(i - 1, 0)
                        logits(i - 1, 1)
                    if mixing and lv == 4:
                        weigh(i - 1, 0)
                        weigh(i - 1, 1)
                for b in range(2):
                    keep_mw(i, b)
                for u in range(NCH):
                    for b in range(2):
                        keep_state(i, b, u)
                    if mixing and u in (1, 2):
                        mean_square(i - 1, u - 1)
                    if more and u in (5, 6):
                        norms(i + 1, u - 5)
                    if mixing and u in (8, 9):
                        normalise(i - 1, u - 8)
                    if mixing and u in (13, 14):
                        add_x(i - 1, u - 13)
                own.restart()

            dve.wait_ge(const_in, START + 64)
            dve.wait_ge(clear, START + 2)
            V.tensor_scalar(w_os[:], w_o[:], o_norm[:, 0:1], None, ALU.mult).then_inc(set_up, 1)
            V.tensor_scalar(alpha3[:], alpha[:], 1.0 / 3.0, None, ALU.mult).then_inc(set_up, 1)
            dve.wait_ge(set_up, START + 2)
            for b in range(2):
                norms(0, b)
            turn(0, False, True)
            with dve.Fori(1, LAST) as i:
                turn(i, True, True)
            turn(LAST, True, False)
            for stage in (centre, deviate, logits, weigh, mean_square, normalise, add_x):
                for b in range(2):
                    stage(LAST, b)
            own.restart()

        @block.tensor
        def _(pe):
            mm = nc.tensor.matmul

            def wait(signal, value):
                pe.wait_ge(signal, value)
                pe.sem_inc(pe_passed, 1)

            def product(b, left, right, part=slice(0, 2)):
                for q in range(QD):
                    for u in range(NCH):
                        ins = mm(psA[b][quad(q), u, part], left[quad(q), u], right[quad(q), u, part],
                                 start=True, stop=True)
                ins.then_inc(made[b], 1)

            def project(i, b):
                wait(mixT_ready[b], START + i + 1)
                out = psA[b][:, 0:NCH // 2].rearrange("p c k d -> p (c k d)")
                for t in range(TILES):
                    ins = mm(out[:, bass.ts(t, P)], mixT[b][:, bass.ts(t, P)], w_os[:], start=True, stop=True)
                ins.then_inc(out_made[b], 1)

            def states(i, b, u):
                part = slice(1, 2) if u == NCH - 1 else slice(0, 2)
                after = slice(1, 2) if u == NCH - 2 else slice(0, 2)
                for q in range(QD):
                    if u == 0:
                        ins = mm(psS[b][quad(q), 0, 0], uw[b][quad(q), 0, 0], ka[b][quad(q), 0], start=True, stop=True)
                    else:
                        ins = mm(psS[b][quad(q), u % 2, 0, part], branch[b][quad(q), STATE, u - 1],
                                 imq[b][quad(q), u, part], start=False, stop=True)
                    if q == QD - 1:
                        ins.then_inc(state_made[b], 1)
                    if u < NCH - 1:
                        mm(psS[b][quad(q), (u + 1) % 2, 0, after], uw[b][quad(q), u + 1, 0],
                           ka[b][quad(q), u + 1, after], start=True, stop=False)

            def turn(i, mixing):
                for b in range(2):
                    wait(prepared[b], START + i + 1)
                    if mixing:
                        wait(kept[b], START + STEPS * i)
                        wait(x1_ready[b], START + (i - 1))
                    product(b, cm[b][:, :, 0], cm[b][:, :, 1:3])
                for lv in range(5):
                    for b in range(2):
                        wait(kept[b], START + STEPS * i + SQ0 + lv)
                        product(b, power[b], rows[lv % 2][b],
                                slice(0, 1) if lv == 0 else slice(1, 2) if lv == 4 else slice(0, 2))
                for step, left, right in ((UW, [rows[1][b][:, :, 1] for b in range(2)], vk),
                                          (MW, [uw[b][:, :, 1] for b in range(2)], ka)):
                    for b in range(2):
                        wait(kept[b], START + STEPS * i + step)
                        product(b, left[b], right[b])
                for b in range(2):
                    wait(kept[b], START + STEPS * (i + 1))
                for u in range(NCH):
                    for b in range(2):
                        wait(state_ready[b], START + NCH * i + u)
                        states(i, b, u)
                    if mixing and u == 11:
                        for b in range(2):
                            project(i - 1, b)

            pe.wait_ge(set_up, START + 2)
            turn(0, False)
            with pe.Fori(1, PAIRS) as i:
                turn(i, True)
            for b in range(2):
                project(LAST, b)


def phase_route(nc, dram, keep, layer):
    K = 2 if layer == 0 else 1
    G = G0 if layer == 0 else G1
    BIG = float(1 << 20)
    with ExitStack() as ctx:
        def sb(name, shape, dt=F32):
            return ctx.enter_context(nc.sbuf_tensor(f"{name}_l{layer}", shape, dt))

        signals = Signals(nc, ctx)
        sem, sem2 = signals.one, signals.two

        tri = sb("tri", [P, P])
        ones = sb("ones", [P, P])
        expert = sb("expert", [P, E])
        desc = sb("desc", [P, E])
        starts = sb("starts", [P, G0])
        best = [sb(f"best{k}", [P, NT]) for k in range(2)]
        first = sb("first", [P, NT])
        flag = sb("flag", [P, NT, E])
        rest = sb("rest", [P, NT, E])
        sel = [sb(f"sel{k}", [P, NT, E]) for k in range(K)]
        run = [sb(f"run{k}", [P, E, NT]) for k in range(K)]
        place = sb("place", [P, NT, E])
        rank = sb("rank", [P, NT])
        base = sb("base", [P, NT])
        over = sb("over", [P, NT])
        row = sb("row", [P, NT])
        pexp = sb("pexp", [P, NT, E])
        pone = sb("pone", [P, NT])
        padf = sb("padf", [P, E])
        padi = sb("padi", [P, E], I32)
        ends = sb("ends", [P, E])
        past = sb("past", [P, G0, E])
        gidf = sb("gidf", [P, G0])
        index = [sb(f"index{b}", [P, TILES, K], U32) for b in range(2)]
        xn = [sb(f"xnr{b}", [P, TILES, D]) for b in range(2)]
        psC = [ctx.enter_context(nc.psum_tensor(f"psC{k}_l{layer}", [P, NT, E], F32)) for k in range(K)]
        psN = [ctx.enter_context(nc.psum_tensor(f"psN{k}_l{layer}", [P, NT, E], F32)) for k in range(K)]

        const_in = sem("route_const_in")
        ones_set = sem("ones_set")
        chosen = sem("chosen")
        counted = sem("counted")
        gaps_ready = sem("gaps_ready")
        exp_ready = sem("route_exp_ready")
        routed = sem("routed")
        xn_in = sem2("xnr_in")
        index_ready = sem2("index_ready")
        rows_free = sem2("rows_free")
        scattered = keep["scattered"][layer]
        dve_own = signals.own("dve_own")
        pool_passed = signals.one("pool_passed")
        block = signals.block()

        @block.sync
        def _(sp):
            consts = [(tri, "tri"), (expert, "expert"), (starts, "starts")]
            if layer == 0:
                consts.append((keep["group"], "group0"))
            for dst, name in consts:
                sp.dma_start(dst[:], dram[name]).then_inc(const_in, 16)
            source = dram["xn" if layer == 0 else "xn1"]
            with sp.Fori(0, PAIRS) as i:
                for b in range(2):
                    sp.wait_ge(rows_free[b], START + i)
                    sp.dma_start(xn[b][:], source[bass.ds(2 * i + b, 1)].rearrange("a (t p) d -> p (a t) d", p=P)
                                 ).then_inc(xn_in[b], 16)

        CONSTS = 16 * (4 if layer == 0 else 3)

        @block.gpsimd
        def _(pool):
            def wait(signal, value):
                pool.wait_ge(signal, value)
                pool.sem_inc(pool_passed, 1)

            nc.gpsimd.memset(ones[:], 1.0).then_inc(ones_set, 1)
            with pool.Fori(0, PAIRS) as i:
                for b in range(2):
                    wait(index_ready[b], START + i + 1)
                    wait(xn_in[b], START + 16 * (i + 1))
                    for t in range(TILES):
                        for k in range(K):
                            pool.indirect_dma_start(
                                out=dram[f"slots{layer}"][:, :],
                                out_offset=bass.IndirectOffsetOnAxis(ap=index[b][:, t, k:k + 1], axis=0),
                                in_=xn[b][:, t, :], in_offset=None, bounds_check=G * GS - 1, oob_is_err=False
                            ).then_inc(scattered[b], 16)
                for b in range(2):
                    wait(scattered[b], 16 * K * TILES * (i + 1))
                    pool.sem_inc(rows_free[b], 1)
            for b in range(2):
                pool.wait_ge(scattered[b], 16 * K * TILES * PAIRS)

        @block.scalar
        def _(act):
            act.wait_ge(gaps_ready, START + 1)
            if layer == 0:
                nc.scalar.activation(over[:], row[:], ACT.Exp).then_inc(exp_ready, 1)
            else:
                nc.scalar.activation(pexp[:], rest[:], ACT.Exp).then_inc(exp_ready, 1)

        @block.tensor
        def _(pe):
            pe.wait_ge(ones_set, START + 1)
            pe.wait_ge(const_in, START + CONSTS)
            for k in range(K):
                pe.wait_ge(chosen, START + k + 1)
                flat = sel[k][:].rearrange("p t e -> p (t e)")
                nc.tensor.matmul(psC[k][:].rearrange("p t e -> p (t e)"), tri[:], flat, start=True, stop=True)
                nc.tensor.matmul(psN[k][:].rearrange("p t e -> p (t e)"), ones[:], flat, start=True, stop=True
                                 ).then_inc(counted, 1)

        @block.vector
        def _(dve):
            own = Chain(dve, dve_own)
            V = nc.vector
            logits = keep["logits"][:].rearrange("p (t e) -> p t e", e=E)

            def by_token(ap):
                return ap.unsqueeze(2).to_broadcast([P, NT, E])

            def by_expert(ap):
                return ap.unsqueeze(1).to_broadcast([P, NT, E])

            def choose(values, k):
                own.link(V.tensor_reduce(best[k][:], values, AX_X, ALU.max))
                own.link(V.tensor_tensor(flag[:], values, by_token(best[k][:]), ALU.is_equal))
                own.link(V.tensor_tensor(flag[:], flag[:], by_expert(desc[:]), ALU.mult))
                own.link(V.tensor_reduce(first[:], flag[:], AX_X, ALU.max))
                own.link(V.tensor_tensor(sel[k][:], by_expert(desc[:]), by_token(first[:]), ALU.is_equal))
                dve.sem_inc(chosen, 1)

            dve.wait_ge(const_in, START + CONSTS)
            dve.wait_ge(ones_set, START + 1)
            own.link(V.tensor_scalar(desc[:], expert[:], -1.0, float(E), ALU.mult, ALU.add))
            choose(logits, 0)
            if layer == 0:
                own.link(V.scalar_tensor_tensor(out=rest[:], in0=sel[0][:], scalar=-1e30, in1=logits,
                                                op0=ALU.mult, op1=ALU.add))
                choose(rest[:], 1)
                own.link(V.tensor_tensor(row[:], best[1][:], best[0][:], ALU.subtract))
            else:
                own.link(V.tensor_tensor(rest[:], logits, by_token(best[0][:]), ALU.subtract))
            dve.sem_inc(gaps_ready, 1)
            dve.wait_ge(exp_ready, START + 1)
            if layer == 0:
                own.link(V.tensor_scalar(pone[:], over[:], 1.0, None, ALU.add))
                own.link(V.reciprocal(keep["prob"][:, :, 0], pone[:]))
                own.link(V.tensor_tensor(keep["prob"][:, :, 1], over[:], keep["prob"][:, :, 0], ALU.mult))
            else:
                own.link(V.tensor_reduce(pone[:], pexp[:], AX_X, ALU.add))
                own.link(V.reciprocal(keep["prob"][:, :, 0], pone[:]))
            for k in range(K):
                dve.wait_ge(counted, START + k + 1)
                for e in range(E):
                    own.step(V.tensor_tensor_scan(run[k][:, e, :], ones[:, 0:NT], psN[k][:, :, e],
                                                  0.0 if k == 0 else run[0][:, e, NT - 1:NT], ALU.mult, ALU.add))
                own.wait()
            if layer == 1:
                own.link(V.tensor_scalar(padf[:], run[0][:, :, NT - 1], float(GS - 1), None, ALU.add))
                own.link(V.tensor_copy(padi[:], padf[:]))
                shift = GS.bit_length() - 1
                own.link(V.tensor_scalar(padi[:], padi[:], shift, shift, ALU.arith_shift_right,
                                         ALU.logical_shift_left))
                own.link(V.tensor_copy(padf[:], padi[:]))
                own.link(V.tensor_tensor_scan(ends[:], ones[:, 0:E], padf[:], 0.0, ALU.mult, ALU.add))
                own.link(V.tensor_tensor(past[:], starts[:].unsqueeze(2).to_broadcast([P, G0, E]),
                                         ends[:].unsqueeze(1).to_broadcast([P, G0, E]), ALU.is_ge))
                own.link(V.tensor_reduce(gidf[:], past[:], AX_X, ALU.add))
                own.link(V.tensor_scalar(gidf[:], gidf[:], float(E - 1), None, ALU.min))
                own.link(V.tensor_copy(keep["group"][:], gidf[:]))
                own.link(V.tensor_tensor(ends[:], ends[:], padf[:], ALU.subtract))
                begins = ends
            else:
                own.link(V.tensor_scalar(ends[:], expert[:], float(CAP0), None, ALU.mult))
                begins = ends
            for k in range(K):
                runs = run[k][:].rearrange("p e t -> p t e")
                own.link(V.tensor_tensor(place[:], runs, psN[k][:], ALU.subtract))
                own.link(V.tensor_tensor(place[:], place[:], psC[k][:], ALU.add))
                own.link(V.tensor_tensor(place[:], place[:], sel[k][:], ALU.mult))
                own.link(V.tensor_reduce(rank[:], place[:], AX_X, ALU.add))
                own.link(V.tensor_scalar(rank[:], rank[:], -1.0, None, ALU.add))
                own.link(V.tensor_tensor(flag[:], sel[k][:], by_expert(begins[:]), ALU.mult))
                own.link(V.tensor_reduce(base[:], flag[:], AX_X, ALU.add))
                if layer == 0:
                    own.link(V.tensor_scalar(over[:], rank[:], float(CAP0), BIG, ALU.is_ge, ALU.mult))
                    own.link(V.tensor_tensor(row[:], base[:], rank[:], ALU.add))
                    own.link(V.tensor_tensor(row[:], row[:], over[:], ALU.add))
                    own.link(V.tensor_copy(keep["slot"][:, :, k], row[:]))
                    own.link(V.tensor_scalar(over[:], rank[:], float(CAP0), None, ALU.is_lt))
                    own.link(V.tensor_tensor(keep["prob"][:, :, k], keep["prob"][:, :, k], over[:], ALU.mult))
                    own.link(V.tensor_scalar(rank[:], rank[:], float(CAP0 - 1), None, ALU.min))
                own.link(V.tensor_tensor(row[:], base[:], rank[:], ALU.add))
                if layer == 1:
                    own.link(V.tensor_copy(keep["slot"][:, :, 0], row[:]))
                own.link(V.tensor_copy(keep["slot"][:, :, 2 + k], row[:]))
            own.restart()
            with dve.Fori(0, PAIRS) as i:
                for b in range(2):
                    dve.wait_ge(rows_free[b], START + i)
                    V.tensor_copy(index[b][:], keep["slot"][:, bass.ds((2 * i + b) * TILES, TILES), 0:K]
                                  ).then_inc(index_ready[b], 1)


def phase_experts(nc, dram, keep, layer):
    G = G0 if layer == 0 else G1
    with ExitStack() as ctx:
        def sb2(name, shape, dt=F32):
            return [ctx.enter_context(nc.sbuf_tensor(f"{name}{b}_l{layer}", shape, dt)) for b in range(2)]

        signals = Signals(nc, ctx)
        sem2 = signals.two

        ident = keep["ident"]
        rows = sb2("rows", [P, GS // P, D])
        rowsT = sb2("rowsT", [P, GS])
        w_up = sb2("w_up", [P, FF])
        w_down = sb2("w_down", [P, FT, D])
        b_up = sb2("b_up", [P, FT])
        b_down = sb2("b_down", [P, D])
        relu = sb2("relu", [P, FT, GS])
        hid = sb2("ehid", [P, FT, GS])
        outs = sb2("outs", [P, GS // P, D])
        psT = ctx.enter_context(nc.psum_tensor(f"psXT_l{layer}", [P, GS], F32))
        psH = ctx.enter_context(nc.psum_tensor(f"psEH_l{layer}", [P, FT, GS], F32))
        psY = [ctx.enter_context(nc.psum_tensor(f"psY{b}_l{layer}", [P, GS // P, D], F32)) for b in range(2)]

        rows_in = sem2("rows_in")
        up_in = sem2("up_in")
        down_in = sem2("down_in")
        rowsT_made = sem2("rowsT_made")
        rowsT_ready = sem2("rowsT_ready")
        up_made = sem2("up_made")
        relu_ready = sem2("relu_ready")
        hid_act = sem2("hid_act")
        hid_dve = sem2("hid_dve")
        down_made = sem2("down_made")
        outs_ready = sem2("outs_ready")
        outs_stored = sem2("outs_stored")
        pool_passed = signals.one("pool_passed")
        block = signals.block()
        DOWN_IN = 16 if layer == 0 else 48

        @block.sync
        def _(sp):
            slots = dram[f"slots{layer}"].rearrange("(g t p) d -> g p t d", p=P, t=GS // P)
            done = dram[f"rows{layer}"].rearrange("(g t p) d -> g p t d", p=P, t=GS // P)

            def load(b, g, c):
                sp.wait_ge(rowsT_made[b], START + c)
                sp.dma_start(rows[b][:], slots[bass.ds(g, 1)].rearrange("a p t d -> p (a t) d")
                             ).then_inc(rows_in[b], 16)
                e = sp.value_load(keep["group"][0:1, bass.ds(g, 1)], min_val=0, max_val=E - 1)
                sp.wait_ge(up_made[b], START + FT * c)
                sp.dma_start(w_up[b][:], dram[f"w_fc{layer}"][bass.ds(e, 1)].rearrange("a c f -> c (a f)")
                             ).then_inc(up_in[b], 16)
                sp.wait_ge(down_made[b], START + c)
                sp.dma_start(w_down[b][:], dram[f"w_down{layer}"][bass.ds(e, 1)].rearrange(
                    "a (k p) d -> p (a k) d", p=P)).then_inc(down_in[b], 16)
                if layer == 1:
                    sp.wait_ge(hid_act[b], START + c)
                    sp.wait_ge(hid_dve[b], START + c)
                    sp.dma_start(b_up[b][:], dram["b_fc1"][bass.ds(e, 1)].rearrange("a p k -> p (a k)")
                                 ).then_inc(down_in[b], 16)
                    sp.wait_ge(outs_ready[b], START + c)
                    sp.dma_start(b_down[b][:], dram["b_down1"][bass.ds(e, 1)].rearrange(
                        "a k d -> (a k) d").to_broadcast([P, D])).then_inc(down_in[b], 16)

            def store(b, g, c):
                sp.wait_ge(outs_ready[b], START + c + 1)
                sp.dma_start(done[bass.ds(g, 1)].rearrange("a p t d -> p (a t) d"), outs[b][:]
                             ).then_inc(outs_stored[b], 16)

            for b in range(2):
                load(b, b, 0)
            with sp.Fori(0, G // 2 - 1) as i:
                for b in range(2):
                    load(b, 2 * i + 2 + b, i + 1)
                    store(b, 2 * i + b, i)
            for b in range(2):
                store(b, G - 2 + b, G // 2 - 1)
            for b in range(2):
                sp.wait_ge(outs_stored[b], START + 16 * (G // 2))

        @block.scalar
        def _(act):
            with act.Fori(0, G // 2) as i:
                for b in range(2):
                    act.wait_ge(rowsT_made[b], START + i + 1)
                    act.wait_ge(up_made[b], START + FT * i)
                    nc.scalar.copy(rowsT[b][:], psT[:]).then_inc(rowsT_ready[b], 1)
                    if layer == 1:
                        act.wait_ge(down_in[b], START + DOWN_IN * (i + 1))
                        act.wait_ge(down_made[b], START + i)
                    else:
                        act.wait_ge(hid_dve[b], START + i)
                    for m in range(FT if layer == 0 else 2):
                        act.wait_ge(up_made[b], START + FT * i + m + 1)
                        if layer == 0:
                            nc.scalar.activation(relu[b][:, m], psH[:, m], ACT.Relu).then_inc(relu_ready[b], 1)
                        else:
                            ins = nc.scalar.activation(hid[b][:, m], psH[:, m], ACT.Relu, bias=b_up[b][:, m:m + 1])
                    if layer == 1:
                        ins.then_inc(hid_act[b], 1)

        @block.vector
        def _(dve):
            def evacuate(b, c):
                dve.wait_ge(down_made[b], START + c + 1)
                dve.wait_ge(outs_stored[b], START + 16 * c)
                if layer == 0:
                    ins = nc.vector.tensor_copy(outs[b][:], psY[b][:])
                else:
                    ins = nc.vector.tensor_tensor(outs[b][:], psY[b][:], b_down[b][:].unsqueeze(1).to_broadcast(
                        [P, GS // P, D]), ALU.add)
                ins.then_inc(outs_ready[b], 1)

            def activate(b, c):
                dve.wait_ge(down_made[b], START + c)
                if layer == 1:
                    dve.wait_ge(down_in[b], START + DOWN_IN * (c + 1))
                for m in range(0 if layer == 0 else 2, FT):
                    if layer == 0:
                        dve.wait_ge(relu_ready[b], START + FT * c + m + 1)
                        ins = nc.vector.tensor_tensor(hid[b][:, m], relu[b][:, m], relu[b][:, m], ALU.mult)
                    else:
                        dve.wait_ge(up_made[b], START + FT * c + m + 1)
                        ins = nc.vector.tensor_scalar(hid[b][:, m], psH[:, m], b_up[b][:, m:m + 1], 0.0,
                                                      ALU.add, ALU.max)
                ins.then_inc(hid_dve[b], 1)

            activate(0, 0)
            with dve.Fori(0, G // 2 - 1) as i:
                activate(1, i)
                evacuate(0, i)
                activate(0, i + 1)
                evacuate(1, i)
            activate(1, G // 2 - 1)
            evacuate(0, G // 2 - 1)
            evacuate(1, G // 2 - 1)

        @block.tensor
        def _(pe):
            mm = nc.tensor.matmul

            def turn(b, c):
                pe.wait_ge(rows_in[b], START + 16 * (c + 1))
                pe.wait_ge(rowsT_ready[1 - b], START + c + b)
                for t in range(GS // P):
                    ins = nc.tensor.transpose(psT[:, bass.ts(t, P)], rows[b][:, t, :], ident[:])
                ins.then_inc(rowsT_made[b], 1)

            def up(b, c):
                pe.wait_ge(rowsT_ready[b], START + c + 1)
                pe.wait_ge(up_in[b], START + 16 * (c + 1))
                if layer == 0:
                    pe.wait_ge(relu_ready[1 - b], START + FT * (c + b))
                else:
                    pe.wait_ge(hid_act[1 - b], START + c + b)
                    pe.wait_ge(hid_dve[1 - b], START + c + b)
                for m in range(FT):
                    mm(psH[:, m], w_up[b][:, bass.ts(m, P)], rowsT[b][:], start=True, stop=True).then_inc(up_made[b], 1)

            def down(b, c):
                if layer == 1:
                    pe.wait_ge(hid_act[b], START + c + 1)
                pe.wait_ge(hid_dve[b], START + c + 1)
                pe.wait_ge(down_in[b], START + DOWN_IN * (c + 1))
                pe.wait_ge(outs_ready[b], START + c)
                for t in range(GS // P):
                    for m in range(FT):
                        ins = mm(psY[b][:, t], hid[b][:, m, bass.ts(t, P)], w_down[b][:, m], start=(m == 0),
                                 stop=(m == FT - 1))
                ins.then_inc(down_made[b], 1)

            turn(0, 0)
            up(0, 0)
            turn(1, 0)
            with pe.Fori(0, G // 2 - 1) as i:
                up(1, i)
                turn(0, i + 1)
                down(0, i)
                up(0, i + 1)
                turn(1, i + 1)
                down(1, i)
            up(1, G // 2 - 1)
            down(0, G // 2 - 1)
            down(1, G // 2 - 1)


def phase_route0(nc, dram, keep):
    phase_route(nc, dram, keep, 0)


def phase_route1(nc, dram, keep):
    phase_route(nc, dram, keep, 1)


def phase_experts0(nc, dram, keep):
    phase_experts(nc, dram, keep, 0)


def phase_experts1(nc, dram, keep):
    phase_experts(nc, dram, keep, 1)


def phase_linear(nc, dram, keep):
    W = C // SUB
    with ExitStack() as ctx:
        def sb(name, shape, dt=F32):
            return ctx.enter_context(nc.sbuf_tensor(name, shape, dt))

        def sb2(name, shape, dt=F32):
            return [sb(f"{name}{b}", shape, dt) for b in range(2)]

        signals = Signals(nc, ctx)
        sem, sem2 = signals.one, signals.two

        ident = keep["ident"]
        w_in = sb("w_in1", [P, 4, D])
        b_qkv = sb("b_qkv1", [P, 3])
        b_n = sb("b_n1", [P, 1])
        neg_b_n = sb("neg_b_n1", [P, 1])
        w_out = sb("w_out1", [P, D])
        b_out = sb("b_out1", [1, D])
        w_rout = sb("w_rout1s", [P, E])
        masks = sb("masks1", [P, 4, C])
        subs = sb("subs", [P, SUB])
        ones = sb("ones1", [1, P])
        half = sb("neg_half", [P, TILES])
        index = sb2("index1", [P, TILES, 2], U32)
        share = sb2("share1", [P, TILES, 2])
        got = [sb2(f"got{k}", [P, TILES, D]) for k in range(2)]
        x2 = sb2("x2s", [P, TILES, D])
        stats = sb2("stats1", [P, TILES, 6])
        moments = sb2("moments1", [P, TILES, 2])
        var = sb2("var1", [P, TILES])
        rstd = sb2("rstd1", [P, TILES])
        xn = sb2("xn1s", [P, TILES, D])
        xnT = sb2("xnT1", [P, LEN])
        qkv = sb2("qkv1", [P, 3, NCH, C])
        norm = sb2("norm1", [P, LEN])
        kv = sb2("kv1", [P, 2, NCH, C])
        diag = [sb2(f"ldiag{k}", [P, NCH, P]) for k in range(2)]
        v_sub = sb2("v_sub", [P, NCH, SUB * (P + W)])
        q_sub = sb2("q_sub", [P, NCH, SUB, C])
        score = q_sub
        score = sb2("score", [P, NCH // 2, SUB, C])
        sums = [sb2(f"zsum{k}", [P, NCH, C]) for k in range(2)]
        ctxT = norm

        bank = [[ctx.enter_context(nc.psum_tensor(f"bank{k}_{b}", [P, 512], F32)) for b in range(2)] for k in range(4)]

        const_in = sem("lin_const_in")
        clear = sem("lin_clear")
        set_up = sem("lin_set_up")
        index_ready = sem2("lin_index")
        gathered = keep["gathered"][0]
        x_in = sem2("lin_x_in")
        ln_stats = sem2("lin_stats")
        rstd_ready = sem2("lin_rstd")
        xn_ready = sem2("lin_xn")
        xn_stored = sem2("lin_xn_stored")
        xnT_made = sem2("lin_xnT_made")
        xnT_ready = sem2("lin_xnT")
        logits_made = sem2("lin_logits_made")
        logits_kept = sem2("lin_logits_kept")
        proj_made = sem2("lin_proj_made")
        proj_ready = sem2("lin_proj_ready")
        norm_ready = sem2("lin_norm_ready")
        source = sem2("lin_source")
        diag_act = sem2("lin_diag_act")
        diag_pool = sem2("lin_diag_pool")
        diag_dve = sem2("lin_diag_dve")
        score_made = sem2("score_made")
        score_ready = sem2("score_ready")
        z_made = sem2("z_made")
        ctx_made = sem2("ctx_made")
        ctx_ready = sem2("ctx_ready")
        out_made = sem2("lin_out_made")
        x3_ready = sem2("x3_ready")
        x3_stored = sem2("x3_stored")
        dve_own = signals.own("dve_own")
        pool_own = signals.own("pool_own")
        pool_passed = signals.one("pool_passed")
        block = signals.block()

        KT, V, K, Z = range(4)
        DIAGS = 4
        HALF = NCH // 2
        CONSTS = 16 * 11
        v_cols = [v_sub[b][:].rearrange("p c (s w) -> p c s w", s=SUB) for b in range(2)]

        def spread(wait, copy, qs, e, b, i, done):
            if e == KT:
                wait(proj_ready[b], START + i + 1)
            else:
                wait(source[b], START + 3 * i + e)
            if e in (KT, V, K):
                wait(ctx_made[b], START + 2 * i)
            else:
                wait(score_made[b], START + 2 * (i + 1))
            for q in qs:
                if e == V:
                    ins = copy(v_cols[b][quad(q), :, :, C * q:C * q + W],
                               kv[b][quad(q), 1].rearrange("p c (s w) -> p c s w", w=W))
                elif e == Z:
                    ins = copy(diag[0][b][quad(q), 1:NCH, quad(q)], sums[0][b][quad(q), 0:NCH - 1])
                else:
                    ins = copy(diag[0 if e == KT else 1][b][quad(q), :, quad(q)],
                               (qkv if e == KT else kv)[b][quad(q), 1 if e == KT else 0])
            ins.then_inc(done[b], 1)

        @block.sync
        def _(sp):
            for dst, name in ((w_in[:, 0], "w_q1"), (w_in[:, 1], "w_k1"), (w_in[:, 2], "w_v1"), (w_in[:, 3], "w_n1"),
                              (b_qkv[:], "b_qkv1"), (b_n[:], "b_n1"), (w_out[:], "w_o1"), (b_out[:], "b_o1"),
                              (w_rout[:], "w_rout1"), (masks[:], "masks"), (subs[:], "subs")):
                sp.dma_start(dst, dram[name]).then_inc(const_in, 16)

            def rows(name, n):
                return dram[name][bass.ds(n, 1)].rearrange("a (t p) d -> p (a t) d", p=P)

            with sp.Fori(0, PAIRS) as i:
                for b in range(2):
                    sp.wait_ge(x3_stored[b], START + 16 * i)
                    sp.dma_start(x2[b][:], rows("x1", 2 * i + b)).then_inc(x_in[b], 16)
                for b in range(2):
                    sp.wait_ge(xn_ready[b], START + i + 1)
                    sp.dma_start(rows("xn1", 2 * i + b), xn[b][:]).then_inc(xn_stored[b], 16)
                for b in range(2):
                    sp.wait_ge(x3_ready[b], START + i + 1)
                    sp.dma_start(rows("x3", 2 * i + b), x2[b][:]).then_inc(x3_stored[b], 16)
            for b in range(2):
                sp.wait_ge(xn_stored[b], START + 16 * PAIRS)
                sp.wait_ge(x3_stored[b], START + 16 * PAIRS)

        @block.gpsimd
        def _(pool):
            def wait(signal, value):
                pool.wait_ge(signal, value)
                pool.sem_inc(pool_passed, 1)

            own = Chain(pool, pool_own)
            for b in range(2):
                for ap in (diag[0][b][:], diag[1][b][:], v_sub[b][:]):
                    nc.gpsimd.memset(ap, 0.0).then_inc(clear, 1)
            nc.gpsimd.memset(half[:], -0.5).then_inc(clear, 1)
            nc.gpsimd.memset(ones[:], 1.0).then_inc(clear, 1)
            pool.wait_ge(clear, START + 8)

            def gather(b, c):
                wait(index_ready[b], START + c + 1)
                for t in range(TILES):
                    for k in range(2):
                        pool.indirect_dma_start(
                            out=got[k][b][:, t, :], out_offset=None, in_=dram["rows0"][:, :],
                            in_offset=bass.IndirectOffsetOnAxis(ap=index[b][:, t, k:k + 1], axis=0),
                            bounds_check=G0 * GS - 1, oob_is_err=False).then_inc(gathered[b], 16)

            with pool.Fori(0, PAIRS) as i:
                for b in range(2):
                    gather(b, i)
                for b in range(2):
                    wait(ln_stats[b], START + i + 1)
                    own.link(nc.gpsimd.tensor_scalar(var[b][:], moments[b][:, :, 1], EPS, None, ALU.add))
                    own.link(nc.gpsimd.tensor_tensor(rstd[b][:], var[b][:], half[:], ALU.pow))
                    pool.sem_inc(rstd_ready[b], 1)
                for e in range(DIAGS):
                    for b in range(2):
                        spread(wait, nc.gpsimd.tensor_copy, (2,), e, b, i, diag_pool)
                for b in range(2):
                    wait(diag_pool[b], START + DIAGS * (i + 1))
                own.restart()

        @block.scalar
        def _(act):
            act.wait_ge(set_up, START + 1)
            act.wait_ge(clear, START + 8)

            def expand(es, i):
                for e in es:
                    for b in range(2):
                        spread(act.wait_ge, nc.scalar.copy, (0, 1), e, b, i, diag_act)

            with act.Fori(0, PAIRS) as i:
                for b in range(2):
                    act.wait_ge(xnT_made[b], START + i + 1)
                    nc.scalar.copy(xnT[b][:], bank[0][b][:]).then_inc(xnT_ready[b], 1)
                for b in range(2):
                    for j, k in ((0, 2), (1, 3), (2, 0)):
                        act.wait_ge(proj_made[b], START + 4 * i + j + 1)
                        ins = nc.scalar.activation(qkv[b][:, j].rearrange("p c d -> p (c d)"), bank[k][b][:],
                                                   ACT.Identity, bias=b_qkv[:, j:j + 1])
                    ins.then_inc(proj_ready[b], 1)
                    act.wait_ge(proj_ready[b], START + i + 1)
                    act.wait_ge(proj_made[b], START + 4 * i + 4)
                    nc.scalar.activation(norm[b][:], bank[1][b][:], ACT.Exp, bias=neg_b_n[:, 0:1], scale=-1.0
                                         ).then_inc(norm_ready[b], 1)
                    for s in range(SUB):
                        ins = nc.scalar.activation(q_sub[b][:, :, s], qkv[b][:, 0], ACT.Copy, scale=subs[:, s:s + 1])
                    ins.then_inc(norm_ready[b], 1)
                expand((KT, V, K, Z), i)

        @block.vector
        def _(dve):
            own = Chain(dve, dve_own)
            Ve = nc.vector

            def expand(es, i):
                for e in es:
                    for b in range(2):
                        spread(dve.wait_ge, Ve.tensor_copy, (3,), e, b, i, diag_dve)

            dve.wait_ge(const_in, START + CONSTS)
            dve.wait_ge(clear, START + 8)
            Ve.tensor_scalar(neg_b_n[:], b_n[:], -1.0, None, ALU.mult).then_inc(set_up, 1)
            with dve.Fori(0, PAIRS) as i:
                for b in range(2):
                    n = 2 * i + b
                    own.link(Ve.tensor_copy(share[b][:], keep["prob"][:, bass.ds(n * TILES, TILES), :]))
                    Ve.tensor_copy(index[b][:], keep["slot"][:, bass.ds(n * TILES, TILES), 2:4]
                                   ).then_inc(index_ready[b], 1)
                for b in range(2):
                    dve.wait_ge(x_in[b], START + 16 * (i + 1))
                    dve.wait_ge(gathered[b], 16 * 2 * TILES * (i + 1))
                    for k in range(2):
                        for t in range(TILES):
                            own.step(Ve.scalar_tensor_tensor(out=x2[b][:, t], in0=got[k][b][:, t],
                                                             scalar=share[b][:, t, k:k + 1], in1=x2[b][:, t],
                                                             op0=ALU.mult, op1=ALU.add))
                        own.wait()
                    for t in range(TILES):
                        own.step(Ve.bn_stats(stats[b][:, t, :], x2[b][:, t, :]))
                    own.wait()
                    for t in range(TILES):
                        ins = Ve.bn_aggr(moments[b][:, t, :], stats[b][:, t, :])
                    ins.then_inc(ln_stats[b], 1)
                for b in range(2):
                    dve.wait_ge(rstd_ready[b], START + i + 1)
                    dve.wait_ge(xn_stored[b], START + 16 * i)
                    dve.wait_ge(xnT_made[b], START + i)
                    for t in range(TILES):
                        ins = Ve.tensor_scalar(xn[b][:, t, :], x2[b][:, t, :], moments[b][:, t, 0:1],
                                               rstd[b][:, t:t + 1], ALU.subtract, ALU.mult)
                    ins.then_inc(xn_ready[b], 1)
                for b in range(2):
                    dve.wait_ge(logits_made[b], START + i + 1)
                    Ve.tensor_copy(keep["logits"][:, bass.ds((2 * i + b) * TILES * E, TILES * E)],
                                   bank[1][b][:, 0:TILES * E]).then_inc(logits_kept[b], 1)
                for b in range(2):
                    dve.wait_ge(proj_ready[b], START + i + 1)
                    dve.wait_ge(ctx_made[b], START + 2 * i)
                    own.step(Ve.transpose(kv[b][:, 1], qkv[b][:, 2]))
                    own.link(Ve.transpose(kv[b][:, 0], qkv[b][:, 1]))
                    dve.sem_inc(source[b], 2)
                expand((KT, V, K), i)
                for b in range(2):
                    dve.wait_ge(z_made[b], START + i + 1)
                    own.link(Ve.tensor_tensor(sums[0][b][:], bank[2][b][:].rearrange("p (c d) -> p c d", d=C),
                                              masks[:, 3:4, :].to_broadcast([P, NCH, C]), ALU.mult))
                    dve.sem_inc(score_ready[b], 1)
                for lv in range(4):
                    reach = 1 << lv
                    old, new = sums[lv % 2], sums[1 - lv % 2]
                    for b in range(2):
                        own.step(Ve.tensor_copy(new[b][:, 0:reach], old[b][:, 0:reach]))
                        own.link(Ve.tensor_tensor(new[b][:, reach:NCH], old[b][:, reach:NCH],
                                                  old[b][:, 0:NCH - reach], ALU.add))
                for h in range(2):
                    if h == 0:
                        for b in range(2):
                            dve.sem_inc(source[b], 1)
                    for b in range(2):
                        dve.wait_ge(score_made[b], START + 2 * i + h + 1)
                        dve.wait_ge(ctx_made[b], START + 2 * i + h)
                        for k in range(2):
                            ins = Ve.tensor_tensor(
                                score[b][:, k * HALF // 2:(k + 1) * HALF // 2].rearrange("p c s d -> p (c s) d"),
                                bank[k][b][:].rearrange("p (c d) -> p c d", d=C),
                                masks[:, 1:2, :].to_broadcast([P, NCH, C]), ALU.mult)
                        ins.then_inc(score_ready[b], 1)
                    if h == 0:
                        expand((Z,), i)
                for b in range(2):
                    dve.wait_ge(ctx_made[b], START + 2 * (i + 1))
                    Ve.tensor_tensor(ctxT[b][:], bank[2][b][:], norm[b][:], ALU.mult).then_inc(ctx_ready[b], 1)
                for b in range(2):
                    dve.wait_ge(out_made[b], START + i + 1)
                    Ve.tensor_tensor(x2[b][:].rearrange("p t d -> p (t d)"), bank[3][b][:],
                                     x2[b][:].rearrange("p t d -> p (t d)"), ALU.add).then_inc(x3_ready[b], 1)
                own.restart()

        @block.tensor
        def _(pe):
            mm = nc.tensor.matmul
            pe.wait_ge(const_in, START + CONSTS)
            pe.wait_ge(clear, START + 8)

            def ready(b, i, e):
                for s in (diag_act, diag_pool, diag_dve):
                    pe.wait_ge(s[b], START + DIAGS * i + e + 1)

            with pe.Fori(0, PAIRS) as i:
                for b in range(2):
                    pe.wait_ge(xn_ready[b], START + i + 1)
                    for t in range(TILES):
                        ins = nc.tensor.transpose(bank[0][b][:, bass.ts(t, P)], xn[b][:, t, :], ident[:])
                    ins.then_inc(xnT_made[b], 1)
                for b in range(2):
                    pe.wait_ge(xnT_ready[b], START + i + 1)
                    for t in range(TILES):
                        ins = mm(bank[1][b][:, t * E:t * E + E], xnT[b][:, bass.ts(t, P)], w_rout[:], start=True, stop=True)
                    ins.then_inc(logits_made[b], 1)
                    pe.wait_ge(x3_ready[b], START + i)
                    mm(bank[2][b][:], w_in[:, 0], xnT[b][:], start=True, stop=True).then_inc(proj_made[b], 1)
                    mm(bank[3][b][:], w_in[:, 1], xnT[b][:], start=True, stop=True).then_inc(proj_made[b], 1)
                    mm(bank[0][b][:], w_in[:, 2], xnT[b][:], start=True, stop=True).then_inc(proj_made[b], 1)
                    pe.wait_ge(logits_kept[b], START + i + 1)
                    mm(bank[1][b][:], w_in[:, 3], xnT[b][:], start=True, stop=True).then_inc(proj_made[b], 1)

                def scores(b, h):
                    for u in range(HALF):
                        ins = mm(bank[u // 4][b][:, bass.ts(u % 4, P)], diag[0][b][:, h * HALF + u],
                                 q_sub[b][:, h * HALF + u].rearrange("p s d -> p (s d)"), start=True, stop=True)
                    ins.then_inc(score_made[b], 1)

                def contexts(b, h):
                    for u in range(h * HALF, (h + 1) * HALF):
                        out = bank[2][b][:, bass.ts(u, C)]
                        for s in range(SUB):
                            ins = mm(out, v_sub[b][:, u, P * s:P * s + P], score[b][:, u - h * HALF, s],
                                     start=(s == 0), stop=(s == SUB - 1 and u == 0))
                        if u:
                            ins = mm(out, diag[0][b][:, u], qkv[b][:, 0, u], start=False, stop=True)
                    ins.then_inc(ctx_made[b], 1)

                for b in range(2):
                    ready(b, i, KT)
                    pe.wait_ge(norm_ready[b], START + 2 * (i + 1))
                    scores(b, 0)
                for b in range(2):
                    ready(b, i, K)
                    for u in range(NCH):
                        ins = mm(bank[2][b][:, bass.ts(u, C)], diag[1][b][:, u], kv[b][:, 1, u], start=True, stop=True)
                    ins.then_inc(z_made[b], 1)
                for b in range(2):
                    pe.wait_ge(score_ready[b], START + 3 * i + 2)
                    scores(b, 1)
                for b in range(2):
                    ready(b, i, Z)
                    contexts(b, 0)
                for b in range(2):
                    pe.wait_ge(score_ready[b], START + 3 * (i + 1))
                    contexts(b, 1)
                for b in range(2):
                    pe.wait_ge(ctx_ready[b], START + i + 1)
                    for t in range(TILES):
                        mm(bank[3][b][:, bass.ts(t, P)], ctxT[b][:, bass.ts(t, P)], w_out[:], start=True, stop=False)
                        ins = mm(bank[3][b][:, bass.ts(t, P)], ones[0:1, :], b_out[0:1, :], start=False, stop=True)
                    ins.then_inc(out_made[b], 1)


def phase_finish(nc, dram, keep):
    with ExitStack() as ctx:
        def sb2(name, shape, dt=F32):
            return [ctx.enter_context(nc.sbuf_tensor(f"{name}{b}", shape, dt)) for b in range(2)]

        signals = Signals(nc, ctx)
        sem2 = signals.two

        index = sb2("index2", [P, TILES], U32)
        share = sb2("share2", [P, TILES])
        got = sb2("got2", [P, TILES, D])
        x3 = sb2("x3f", [P, TILES, D])
        index_ready = sem2("fin_index")
        gathered = keep["gathered"][1]
        x_in = sem2("fin_x_in")
        out_ready = sem2("fin_ready")
        out_stored = sem2("fin_stored")
        dve_own = signals.own("dve_own")
        pool_passed = signals.one("pool_passed")
        block = signals.block()

        @block.sync
        def _(sp):
            def rows(name, n):
                return dram[name][bass.ds(n, 1)].rearrange("a (t p) d -> p (a t) d", p=P)

            with sp.Fori(0, PAIRS) as i:
                for b in range(2):
                    sp.wait_ge(out_stored[b], START + 16 * i)
                    sp.dma_start(x3[b][:], rows("x3", 2 * i + b)).then_inc(x_in[b], 16)
                for b in range(2):
                    sp.wait_ge(out_ready[b], START + i + 1)
                    sp.dma_start(rows("out", 2 * i + b), x3[b][:]).then_inc(out_stored[b], 16)
            for b in range(2):
                sp.wait_ge(out_stored[b], START + 16 * PAIRS)

        @block.gpsimd
        def _(pool):
            def wait(signal, value):
                pool.wait_ge(signal, value)
                pool.sem_inc(pool_passed, 1)

            with pool.Fori(0, PAIRS) as i:
                for b in range(2):
                    wait(index_ready[b], START + i + 1)
                    for t in range(TILES):
                        pool.indirect_dma_start(
                            out=got[b][:, t, :], out_offset=None, in_=dram["rows1"][:, :],
                            in_offset=bass.IndirectOffsetOnAxis(ap=index[b][:, t:t + 1], axis=0),
                            bounds_check=G1 * GS - 1, oob_is_err=False).then_inc(gathered[b], 16)

        @block.vector
        def _(dve):
            own = Chain(dve, dve_own)
            V = nc.vector

            def route(b, n, c):
                own.link(V.tensor_copy(share[b][:], keep["prob"][:, bass.ds(n * TILES, TILES), 0]))
                V.tensor_copy(index[b][:], keep["slot"][:, bass.ds(n * TILES, TILES), 2]).then_inc(index_ready[b], 1)

            def add(b, c):
                dve.wait_ge(x_in[b], START + 16 * (c + 1))
                dve.wait_ge(gathered[b], 16 * TILES * (c + 1))
                for t in range(TILES):
                    own.step(V.scalar_tensor_tensor(out=x3[b][:, t], in0=got[b][:, t], scalar=share[b][:, t:t + 1],
                                                    in1=x3[b][:, t], op0=ALU.mult, op1=ALU.add))
                own.wait()
                dve.sem_inc(out_ready[b], 1)

            for b in range(2):
                route(b, b, 0)
            own.restart()
            with dve.Fori(0, PAIRS - 1) as i:
                for b in range(2):
                    add(b, i)
                    route(b, 2 * i + 2 + b, i + 1)
                own.restart()
            for b in range(2):
                add(b, PAIRS - 1)


PHASES = [phase_project, phase_fir, phase_delta, phase_route0, phase_experts0, phase_linear, phase_route1,
          phase_experts1, phase_finish]

def build(nc, dram, phases=99):
    with ExitStack() as ctx:
        keep = {
            "ident": ctx.enter_context(nc.sbuf_tensor("ident", [P, P], F32)),
            "logits": ctx.enter_context(nc.sbuf_tensor("logits", [P, NT * E], F32)),
            "slot": ctx.enter_context(nc.sbuf_tensor("slot", [P, NT, 4], U32)),
            "prob": ctx.enter_context(nc.sbuf_tensor("prob", [P, NT, 2], F32)),
            "group": ctx.enter_context(nc.sbuf_tensor("group", [P, G0], I32)),
            "slots_zeroed": ctx.enter_context(nc.semaphore("slots_zeroed")),
            "scattered": [[ctx.enter_context(nc.semaphore(f"scattered{k}_{b}")) for b in range(2)] for k in range(2)],
            "gathered": [[ctx.enter_context(nc.semaphore(f"gathered{k}_{b}")) for b in range(2)] for k in range(2)],
        }
        for k, phase in enumerate(PHASES):
            if k < phases:
                phase(nc, dram, keep)


def layout(np, x):
    f = {k: np.asarray(v) for k, v in x.items()}
    out = {"x": f["L0_attn_hidden_states"]}
    out["w_qkv"] = np.stack([f[f"L0_attn_{n}_proj_w"].T for n in "qkv"], axis=1)
    out["w_mix1"] = f["L0_attn_gmix_w1"].T.reshape(P, 2, P)
    gate = np.zeros((P, 2, P), np.float32)
    beta = np.zeros((P, P), np.float32)
    b_gate = np.zeros((P, 1), np.float32)
    for h in range(H):
        for j in range(4):
            gate[:, :, C * h + j] = f["L0_attn_gmix_w2"][j * H + h].reshape(2, P).T
            b_gate[C * h + j, 0] = f["L0_attn_gmix_b2"][j * H + h]
        beta[:, C * h + 4] = f["L0_attn_b_proj_w"][h]
    out["w_gate"], out["w_beta"], out["b_gate"] = gate, beta, b_gate
    out["w_rout0"] = f["L0_ffn_w_g"].T
    out["taps"] = np.stack([f[f"L0_attn_{n}_conv_w"] for n in "qkv"], axis=1)
    out["b_mix1"] = f["L0_attn_gmix_b1"].reshape(2, P).T
    toep = np.zeros((H, C, C, 2, 2 * C), np.float32)
    for p in range(C):
        toep[:, p, :, 0, p:p + KS] = f["L0_attn_fir_short_w"][:, :, ::-1]
        toep[:, p, :, 1, p:p + KL] = f["L0_attn_fir_long_w"][:, :, ::-1]
    out["toep"] = toep.reshape(P, C, 2, 2 * C)
    out["alpha"] = np.repeat(f["L0_attn_alpha"], C, axis=0)
    out["o_norm"] = np.tile(f["L0_attn_o_norm_w"], H).reshape(P, 1)
    out["w_o0"] = f["L0_attn_o_proj_w"].T
    out["w_fc0"], out["w_down0"] = f["L0_ffn_c_fc"], f["L0_ffn_c_proj"]
    out["w_q1"] = f["L1_attn_Wqk"][:, 0:P]
    out["w_k1"] = f["L1_attn_Wqk"][:, P:]
    out["w_v1"] = f["L1_attn_Wv"]
    out["b_qkv1"] = np.stack([f["L1_attn_bqk"][0:P], f["L1_attn_bqk"][P:], f["L1_attn_bv"]], axis=1)
    out["w_n1"] = np.repeat(f["L1_attn_Wn"], P // HEADS1, axis=1)
    out["b_n1"] = np.repeat(f["L1_attn_bn"], P // HEADS1).reshape(P, 1)
    out["w_o1"] = f["L1_attn_Wo"]
    out["b_o1"] = f["L1_attn_bo"].reshape(1, P)
    out["w_rout1"] = f["L1_ffn_gate_w"].T
    out["w_fc1"], out["w_down1"] = f["L1_ffn_w1"], f["L1_ffn_w2"]
    out["b_fc1"] = f["L1_ffn_b1"].reshape(E, FT, P).transpose(0, 2, 1)
    out["b_down1"] = f["L1_ffn_b2"].reshape(E, 1, P)
    p, j = np.arange(P)[:, None], np.arange(C)[None, :]
    t = p % C
    out["ident"] = np.eye(P, dtype=np.float32)
    out["tri"] = (p <= np.arange(P)[None, :]).astype(np.float32)
    out["masks"] = np.stack([-(j > t).astype(np.float32), (j >= t).astype(np.float32),
                             (j == t).astype(np.float32),
                             (j // (C // SUB) == t // (C // SUB)).astype(np.float32)], axis=1)
    out["subs"] = (t // (C // SUB) == np.arange(SUB)[None, :]).astype(np.float32)
    out["expert"] = np.tile(np.arange(E, dtype=np.float32), (P, 1))
    out["group0"] = np.tile((np.arange(G0) * GS // CAP0).astype(np.int32), (P, 1))
    out["starts"] = np.tile(np.arange(G0, dtype=np.float32) * GS, (P, 1))
    return {k: np.ascontiguousarray(v) for k, v in out.items()}


SCRATCH = {"xn": [SEQS, LEN, D], "head": [SEQS, P, 4, LEN], "fir": [SEQS, P, 2, LEN], "x1": [SEQS, LEN, D],
           "xn1": [SEQS, LEN, D], "x2": [SEQS, LEN, D], "x3": [SEQS, LEN, D],
           "slots0": [G0 * GS, D], "rows0": [G0 * GS, D], "slots1": [G1 * GS, D], "rows1": [G1 * GS, D]}


def kernel(**inputs):
    import numpy as np
    import concourse.bacc as bacc
    from concourse.bass_utils import run_bass_kernel_spmd

    nc = bacc.Bacc("TRN2", target_bir_lowering=False, num_devices=1)
    arrays, dram = {}, {}
    for name, a in layout(np, inputs).items():
        arrays[f"in_{name}"] = a
        dram[name] = nc.dram_tensor(f"in_{name}", a.shape, mybir.dt.from_np(a.dtype), kind="ExternalInput").ap()
    for name, shape in SCRATCH.items():
        dram[name] = nc.dram_tensor(f"scratch_{name}", shape, F32, kind="Internal").ap()
    dram["out"] = nc.dram_tensor("out_dram", [SEQS, LEN, D], F32, kind="ExternalOutput").ap()
    build(nc, dram)
    r = run_bass_kernel_spmd(nc, [arrays], core_ids=[0])
    return r.results[0]["out_dram"]
```
